# Optimizing a Trainium2 kernel written in Bass

```python
import numpy as np
import jax
import jax.numpy as jnp

def _softmax(x, axis=-1):
    return jax.nn.softmax(x, axis=axis)

def _gelu(x):
    return jax.nn.gelu(x, approximate=True)

def _silu(x):
    return jax.nn.silu(x)

def _sigmoid(x):
    return jax.nn.sigmoid(x)

def _layernorm(x, axis=-1, eps=1e-05):
    m = jnp.mean(x, axis=axis, keepdims=True)
    v = jnp.var(x, axis=axis, keepdims=True)
    return (x - m) / jnp.sqrt(v + eps)

def _scatter_add(tgt, idx, src, axis=0):
    return tgt.at[idx].add(src)

def _segment_sum(src, seg, n):
    return jax.ops.segment_sum(src, seg, n)
kernel_name = 'mk_prb_d2_jaxref_r8_19e5ac'

def setup_inputs(seed: int=0):
    np.random.seed(seed)
    _w = jnp.asarray

    def _L0_attn_setup():
        import jax, jax.numpy as jnp
        import numpy as np
        B, N, D, H = (8, 512, 128, 16)
        HD = D // H
        EPS = 1e-05
        key = jax.random.key(seed)
        ks = jax.random.split(key, 18)
        s = 1.0 / np.sqrt(D)

        def lin(k):
            return (jax.random.normal(k, (D, D), jnp.float32) * s, jnp.zeros((D,), jnp.float32))
        Wg_w, Wg_b = lin(ks[0])
        Wr_w, Wr_b = lin(ks[1])
        Wk_w, Wk_b = lin(ks[2])
        Wv_w, Wv_b = lin(ks[3])
        Wo_w, Wo_b = lin(ks[4])
        mg = jax.random.uniform(ks[5], (D,), jnp.float32)
        mr = jax.random.uniform(ks[6], (D,), jnp.float32)
        mk = jax.random.uniform(ks[7], (D,), jnp.float32)
        mv = jax.random.uniform(ks[8], (D,), jnp.float32)
        w = jax.random.normal(ks[9], (H, HD), jnp.float32)
        u = jax.random.normal(ks[10], (H, HD), jnp.float32)
        x = jax.random.normal(ks[11], (B, N, D), jnp.float32)
        return {'x': x, 'Wg_w': Wg_w, 'Wg_b': Wg_b, 'Wr_w': Wr_w, 'Wr_b': Wr_b, 'Wk_w': Wk_w, 'Wk_b': Wk_b, 'Wv_w': Wv_w, 'Wv_b': Wv_b, 'Wo_w': Wo_w, 'Wo_b': Wo_b, 'mg': mg, 'mr': mr, 'mk': mk, 'mv': mv, 'w': w, 'u': u}
    _L0_attn_in = _L0_attn_setup()

    def _L0_ffn_setup():
        import jax, jax.numpy as jnp
        import numpy as np
        N_HEAD = 16
        NUM_EXPERTS = 8
        TOP_K = 2
        LN_EPS = 1e-05

        def _layernorm(x, g, b):
            mu = jnp.mean(x, axis=-1, keepdims=True)
            var = jnp.mean(jnp.square(x - mu), axis=-1, keepdims=True)
            return (x - mu) * jax.lax.rsqrt(var + LN_EPS) * g + b

        def _attention(h, Wq, bq, Wk, bk, Wv, bv, Wp, bp):
            B, T, D = h.shape
            hd = D // N_HEAD

            def split(z):
                return z.reshape(B, T, N_HEAD, hd).transpose(0, 2, 1, 3)
            q = split(h @ Wq + bq)
            k = split(h @ Wk + bk)
            v = split(h @ Wv + bv)
            att = jnp.einsum('bhqd,bhkd->bhqk', q, k) / jnp.sqrt(jnp.float32(hd))
            causal = jnp.tril(jnp.ones((T, T), bool))
            att = jnp.where(causal, att, -jnp.inf)
            att = jax.nn.softmax(att, axis=-1)
            y = jnp.einsum('bhqk,bhkd->bhqd', att, v)
            y = y.transpose(0, 2, 1, 3).reshape(B, T, D)
            return y @ Wp + bp

        def _token_moe(h, gate_W, gate_b, exp_W1, exp_b1, exp_W2, exp_b2):
            B, T, D = h.shape
            flat = h.reshape(-1, D)
            N = flat.shape[0]
            logits = flat @ gate_W + gate_b
            top_v, top_i = jax.lax.top_k(logits, TOP_K)
            w = jax.nn.softmax(top_v, axis=-1)
            w_full = jnp.zeros((N, NUM_EXPERTS), flat.dtype)
            w_full = w_full.at[jnp.arange(N)[:, None], top_i].add(w)
            out = jnp.zeros_like(flat)
            for e in range(NUM_EXPERTS):
                mid = jax.nn.gelu(flat @ exp_W1[e] + exp_b1[e], approximate=False)
                y_e = mid @ exp_W2[e] + exp_b2[e]
                out = out + w_full[:, e:e + 1] * y_e
            return out.reshape(B, T, D)
        key = jax.random.key(seed)
        B, T, D = (8, 128, 128)
        H = 4 * D
        E = NUM_EXPERTS
        ks = jax.random.split(key, 24)
        s = 0.02
        inp = {'x': jax.random.normal(ks[0], (B, T, D), jnp.float32), 'ln1_g': jnp.ones((D,), jnp.float32), 'ln1_b': jnp.zeros((D,), jnp.float32), 'ln2_g': jnp.ones((D,), jnp.float32), 'ln2_b': jnp.zeros((D,), jnp.float32), 'Wq': jax.random.normal(ks[1], (D, D), jnp.float32) * s, 'bq': jnp.zeros((D,), jnp.float32), 'Wk': jax.random.normal(ks[2], (D, D), jnp.float32) * s, 'bk': jnp.zeros((D,), jnp.float32), 'Wv': jax.random.normal(ks[3], (D, D), jnp.float32) * s, 'bv': jnp.zeros((D,), jnp.float32), 'Wp': jax.random.normal(ks[4], (D, D), jnp.float32) * s, 'bp': jnp.zeros((D,), jnp.float32), 'gate_W': jax.random.normal(ks[5], (D, E), jnp.float32) * s, 'gate_b': jnp.zeros((E,), jnp.float32), 'exp_W1': jax.random.normal(ks[6], (E, D, H), jnp.float32) * s, 'exp_b1': jnp.zeros((E, H), jnp.float32), 'exp_W2': jax.random.normal(ks[7], (E, H, D), jnp.float32) * s, 'exp_b2': jnp.zeros((E, D), jnp.float32)}
        return inp
    _L0_ffn_in = _L0_ffn_setup()

    def _L1_attn_setup():
        import jax, jax.numpy as jnp
        import numpy as np
        B, S, E = (4, 256, 128)
        H, KVH = (16, 4)
        D = E // H
        QL, KVL = (64, 32)
        ROPE_BASE = 10000.0

        def _rope(x):
            d = x.shape[-1]
            inv_freq = 1.0 / ROPE_BASE ** (jnp.arange(0, d, 2, dtype=jnp.float32) / d)
            t = jnp.arange(x.shape[1], dtype=jnp.float32)
            freqs = jnp.outer(t, inv_freq)
            cos = jnp.cos(freqs)[None, :, None, :].astype(x.dtype)
            sin = jnp.sin(freqs)[None, :, None, :].astype(x.dtype)
            x1, x2 = (x[..., ::2], x[..., 1::2])
            r1 = x1 * cos - x2 * sin
            r2 = x1 * sin + x2 * cos
            return jnp.stack([r1, r2], axis=-1).reshape(x.shape)
        key = jax.random.key(seed)
        ks = jax.random.split(key, 7)
        s = 0.02
        return {'x': jax.random.normal(ks[0], (B, S, E), dtype=jnp.float32), 'Wqa': jax.random.normal(ks[1], (E, QL), dtype=jnp.float32) * s, 'Wqb': jax.random.normal(ks[2], (QL, E), dtype=jnp.float32) * s, 'Wkva': jax.random.normal(ks[3], (E, KVL), dtype=jnp.float32) * s, 'Wkvb': jax.random.normal(ks[4], (KVL, KVH * D * 2), dtype=jnp.float32) * s, 'Wout': jax.random.normal(ks[5], (E, E), dtype=jnp.float32) * s, 'bout': jax.random.normal(ks[6], (E,), dtype=jnp.float32) * s}
    _L1_attn_in = _L1_attn_setup()

    def _L1_ffn_setup():
        import math
        import jax, jax.numpy as jnp
        import numpy as np
        D_MODEL = 128
        D_HIDDEN = 256
        N_EXPERTS = 8
        TOP_K = 2
        CAPACITY_FACTOR = 1.25

        def _moe_forward(x, w_router, w_gate, w_down):
            B, T, D = x.shape
            N = B * T
            xf = x.reshape(N, D)
            logits = xf.astype(jnp.float32) @ w_router.T
            gates = jax.nn.softmax(logits, axis=-1)
            topk_gates, topk_idx = jax.lax.top_k(gates, TOP_K)
            expert_mask = jax.nn.one_hot(topk_idx, N_EXPERTS, dtype=jnp.int32).sum(axis=1)
            capacity = math.ceil(N / N_EXPERTS * CAPACITY_FACTOR)
            position_in_expert = jnp.cumsum(expert_mask, axis=0) - 1
            expert_mask = expert_mask * (position_in_expert < capacity)
            keep = jnp.take_along_axis(expert_mask, topk_idx, axis=1) > 0
            topk_gates = topk_gates * keep
            topk_gates = topk_gates / (topk_gates.sum(axis=-1, keepdims=True) + 1e-06)
            hidden = jax.nn.silu(xf @ w_gate.T)
            combine = (topk_gates[:, :, None] * jax.nn.one_hot(topk_idx, N_EXPERTS, dtype=topk_gates.dtype)).sum(axis=1)
            y = jnp.zeros((N, D), dtype=x.dtype)
            for e in range(N_EXPERTS):
                y = y + combine[:, e:e + 1] * (hidden @ w_down[e].T)
            return y.reshape(B, T, D)
        key = jax.random.key(seed)
        k0, k1, k2, k3 = jax.random.split(key, 4)
        B, T = (2, 256)
        x = jax.random.normal(k0, (B, T, D_MODEL), dtype=jnp.float32)
        w_router = jax.random.normal(k1, (N_EXPERTS, D_MODEL), dtype=jnp.float32) * 0.02
        w_gate = jax.random.normal(k2, (D_HIDDEN, D_MODEL), dtype=jnp.float32) * 0.02
        w_down = jax.random.normal(k3, (N_EXPERTS, D_MODEL, D_HIDDEN), dtype=jnp.float32) * 0.02
        return {'x': x, 'w_router': w_router, 'w_gate': w_gate, 'w_down': w_down}
    _L1_ffn_in = _L1_ffn_setup()
    _d = {'L0_attn_x': _L0_attn_in['x'], 'L0_attn_Wg_w': _L0_attn_in['Wg_w'], 'L0_attn_Wg_b': _L0_attn_in['Wg_b'], 'L0_attn_Wr_w': _L0_attn_in['Wr_w'], 'L0_attn_Wr_b': _L0_attn_in['Wr_b'], 'L0_attn_Wk_w': _L0_attn_in['Wk_w'], 'L0_attn_Wk_b': _L0_attn_in['Wk_b'], 'L0_attn_Wv_w': _L0_attn_in['Wv_w'], 'L0_attn_Wv_b': _L0_attn_in['Wv_b'], 'L0_attn_Wo_w': _L0_attn_in['Wo_w'], 'L0_attn_Wo_b': _L0_attn_in['Wo_b'], 'L0_attn_mg': _L0_attn_in['mg'], 'L0_attn_mr': _L0_attn_in['mr'], 'L0_attn_mk': _L0_attn_in['mk'], 'L0_attn_mv': _L0_attn_in['mv'], 'L0_attn_w': _L0_attn_in['w'], 'L0_attn_u': _L0_attn_in['u'], 'L0_ffn_ln1_g': _L0_ffn_in['ln1_g'], 'L0_ffn_ln1_b': _L0_ffn_in['ln1_b'], 'L0_ffn_ln2_g': _L0_ffn_in['ln2_g'], 'L0_ffn_ln2_b': _L0_ffn_in['ln2_b'], 'L0_ffn_Wq': _L0_ffn_in['Wq'], 'L0_ffn_bq': _L0_ffn_in['bq'], 'L0_ffn_Wk': _L0_ffn_in['Wk'], 'L0_ffn_bk': _L0_ffn_in['bk'], 'L0_ffn_Wv': _L0_ffn_in['Wv'], 'L0_ffn_bv': _L0_ffn_in['bv'], 'L0_ffn_Wp': _L0_ffn_in['Wp'], 'L0_ffn_bp': _L0_ffn_in['bp'], 'L0_ffn_gate_W': _L0_ffn_in['gate_W'], 'L0_ffn_gate_b': _L0_ffn_in['gate_b'], 'L0_ffn_exp_W1': _L0_ffn_in['exp_W1'], 'L0_ffn_exp_b1': _L0_ffn_in['exp_b1'], 'L0_ffn_exp_W2': _L0_ffn_in['exp_W2'], 'L0_ffn_exp_b2': _L0_ffn_in['exp_b2'], 'L1_attn_Wqa': _L1_attn_in['Wqa'], 'L1_attn_Wqb': _L1_attn_in['Wqb'], 'L1_attn_Wkva': _L1_attn_in['Wkva'], 'L1_attn_Wkvb': _L1_attn_in['Wkvb'], 'L1_attn_Wout': _L1_attn_in['Wout'], 'L1_attn_bout': _L1_attn_in['bout'], 'L1_ffn_w_router': _L1_ffn_in['w_router'], 'L1_ffn_w_gate': _L1_ffn_in['w_gate'], 'L1_ffn_w_down': _L1_ffn_in['w_down']}
    _x0 = _d['L0_attn_x']
    _d['L0_attn_x'] = jax.random.normal(jax.random.fold_in(jax.random.key(seed), 1), (2, 1024, 128), dtype=_x0.dtype)
    del _x0
    return _d

def reference(L0_attn_x, L0_attn_Wg_w, L0_attn_Wg_b, L0_attn_Wr_w, L0_attn_Wr_b, L0_attn_Wk_w, L0_attn_Wk_b, L0_attn_Wv_w, L0_attn_Wv_b, L0_attn_Wo_w, L0_attn_Wo_b, L0_attn_mg, L0_attn_mr, L0_attn_mk, L0_attn_mv, L0_attn_w, L0_attn_u, L0_ffn_ln1_g, L0_ffn_ln1_b, L0_ffn_ln2_g, L0_ffn_ln2_b, L0_ffn_Wq, L0_ffn_bq, L0_ffn_Wk, L0_ffn_bk, L0_ffn_Wv, L0_ffn_bv, L0_ffn_Wp, L0_ffn_bp, L0_ffn_gate_W, L0_ffn_gate_b, L0_ffn_exp_W1, L0_ffn_exp_b1, L0_ffn_exp_W2, L0_ffn_exp_b2, L1_attn_Wqa, L1_attn_Wqb, L1_attn_Wkva, L1_attn_Wkvb, L1_attn_Wout, L1_attn_bout, L1_ffn_w_router, L1_ffn_w_gate, L1_ffn_w_down):

    def _L0_attn_ref(x, Wg_w, Wg_b, Wr_w, Wr_b, Wk_w, Wk_b, Wv_w, Wv_b, Wo_w, Wo_b, mg, mr, mk, mv, w, u):
        import jax, jax.numpy as jnp
        import numpy as np
        B, N, D, H = (8, 512, 128, 16)
        HD = D // H
        EPS = 1e-05
        b, n, d = x.shape
        x_shift = jnp.roll(x, shift=1, axis=1)

        def mix(m, W, bias):
            return (m * x + (1.0 - m) * x_shift) @ W.T + bias
        g = mix(mg, Wg_w, Wg_b).reshape(b, n, H, HD)
        r = mix(mr, Wr_w, Wr_b).reshape(b, n, H, HD)
        k = mix(mk, Wk_w, Wk_b).reshape(b, n, H, HD)
        v = mix(mv, Wv_w, Wv_b).reshape(b, n, H, HD)
        kv = k * v
        decay = jnp.exp(-jnp.exp(w))
        kv_t = jnp.swapaxes(kv, 0, 1)

        def step(acc, kvt):
            acc = decay * acc + kvt
            return (acc, acc)
        _, accs = jax.lax.scan(step, jnp.zeros((b, H, HD), x.dtype), kv_t)
        wkv = jnp.swapaxes(accs, 0, 1) + u * kv
        rw = r * wkv
        mean = jnp.mean(rw, axis=-1, keepdims=True)
        var = jnp.var(rw, axis=-1, keepdims=True)
        ln = (rw - mean) * jax.lax.rsqrt(var + EPS)
        out = (jax.nn.sigmoid(g) * ln).reshape(b, n, d)
        return out @ Wo_w.T + Wo_b

    def _L0_ffn_ref(x, ln1_g, ln1_b, ln2_g, ln2_b, Wq, bq, Wk, bk, Wv, bv, Wp, bp, gate_W, gate_b, exp_W1, exp_b1, exp_W2, exp_b2):
        import jax, jax.numpy as jnp
        import numpy as np
        N_HEAD = 16
        NUM_EXPERTS = 8
        TOP_K = 2
        LN_EPS = 1e-05

        def _layernorm(x, g, b):
            mu = jnp.mean(x, axis=-1, keepdims=True)
            var = jnp.mean(jnp.square(x - mu), axis=-1, keepdims=True)
            return (x - mu) * jax.lax.rsqrt(var + LN_EPS) * g + b

        def _attention(h, Wq, bq, Wk, bk, Wv, bv, Wp, bp):
            B, T, D = h.shape
            hd = D // N_HEAD

            def split(z):
                return z.reshape(B, T, N_HEAD, hd).transpose(0, 2, 1, 3)
            q = split(h @ Wq + bq)
            k = split(h @ Wk + bk)
            v = split(h @ Wv + bv)
            att = jnp.einsum('bhqd,bhkd->bhqk', q, k) / jnp.sqrt(jnp.float32(hd))
            causal = jnp.tril(jnp.ones((T, T), bool))
            att = jnp.where(causal, att, -jnp.inf)
            att = jax.nn.softmax(att, axis=-1)
            y = jnp.einsum('bhqk,bhkd->bhqd', att, v)
            y = y.transpose(0, 2, 1, 3).reshape(B, T, D)
            return y @ Wp + bp

        def _token_moe(h, gate_W, gate_b, exp_W1, exp_b1, exp_W2, exp_b2):
            B, T, D = h.shape
            flat = h.reshape(-1, D)
            N = flat.shape[0]
            logits = flat @ gate_W + gate_b
            top_v, top_i = jax.lax.top_k(logits, TOP_K)
            w = jax.nn.softmax(top_v, axis=-1)
            w_full = jnp.zeros((N, NUM_EXPERTS), flat.dtype)
            w_full = w_full.at[jnp.arange(N)[:, None], top_i].add(w)
            out = jnp.zeros_like(flat)
            for e in range(NUM_EXPERTS):
                mid = jax.nn.gelu(flat @ exp_W1[e] + exp_b1[e], approximate=False)
                y_e = mid @ exp_W2[e] + exp_b2[e]
                out = out + w_full[:, e:e + 1] * y_e
            return out.reshape(B, T, D)
        x = x + _attention(_layernorm(x, ln1_g, ln1_b), Wq, bq, Wk, bk, Wv, bv, Wp, bp)
        x = x + _token_moe(_layernorm(x, ln2_g, ln2_b), gate_W, gate_b, exp_W1, exp_b1, exp_W2, exp_b2)
        return x

    def _L1_attn_ref(x, Wqa, Wqb, Wkva, Wkvb, Wout, bout):
        import jax, jax.numpy as jnp
        import numpy as np
        B, S, E = (4, 256, 128)
        H, KVH = (16, 4)
        D = E // H
        QL, KVL = (64, 32)
        ROPE_BASE = 10000.0

        def _rope(x):
            d = x.shape[-1]
            inv_freq = 1.0 / ROPE_BASE ** (jnp.arange(0, d, 2, dtype=jnp.float32) / d)
            t = jnp.arange(x.shape[1], dtype=jnp.float32)
            freqs = jnp.outer(t, inv_freq)
            cos = jnp.cos(freqs)[None, :, None, :].astype(x.dtype)
            sin = jnp.sin(freqs)[None, :, None, :].astype(x.dtype)
            x1, x2 = (x[..., ::2], x[..., 1::2])
            r1 = x1 * cos - x2 * sin
            r2 = x1 * sin + x2 * cos
            return jnp.stack([r1, r2], axis=-1).reshape(x.shape)
        b, s, _ = x.shape
        scale = D ** (-0.5)
        q = (x @ Wqa @ Wqb).reshape(b, s, H, D)
        kv = (x @ Wkva @ Wkvb).reshape(b, s, KVH, D, 2)
        k, v = (kv[..., 0], kv[..., 1])
        q = _rope(q)
        k = _rope(k)
        g = H // KVH
        k = jnp.repeat(k, g, axis=2)
        v = jnp.repeat(v, g, axis=2)
        scores = jnp.einsum('bqhd,bkhd->bhqk', q, k) * scale
        causal = jnp.triu(jnp.ones((s, s), dtype=bool), k=1)
        scores = jnp.where(causal[None, None], -jnp.inf, scores)
        w = jax.nn.softmax(scores, axis=-1)
        out = jnp.einsum('bhqk,bkhd->bqhd', w, v).reshape(b, s, E)
        return out @ Wout + bout

    def _L1_ffn_ref(x, w_router, w_gate, w_down):
        import math
        import jax, jax.numpy as jnp
        import numpy as np
        D_MODEL = 128
        D_HIDDEN = 256
        N_EXPERTS = 8
        TOP_K = 2
        CAPACITY_FACTOR = 1.25

        def _moe_forward(x, w_router, w_gate, w_down):
            B, T, D = x.shape
            N = B * T
            xf = x.reshape(N, D)
            logits = xf.astype(jnp.float32) @ w_router.T
            gates = jax.nn.softmax(logits, axis=-1)
            topk_gates, topk_idx = jax.lax.top_k(gates, TOP_K)
            expert_mask = jax.nn.one_hot(topk_idx, N_EXPERTS, dtype=jnp.int32).sum(axis=1)
            capacity = math.ceil(N / N_EXPERTS * CAPACITY_FACTOR)
            position_in_expert = jnp.cumsum(expert_mask, axis=0) - 1
            expert_mask = expert_mask * (position_in_expert < capacity)
            keep = jnp.take_along_axis(expert_mask, topk_idx, axis=1) > 0
            topk_gates = topk_gates * keep
            topk_gates = topk_gates / (topk_gates.sum(axis=-1, keepdims=True) + 1e-06)
            hidden = jax.nn.silu(xf @ w_gate.T)
            combine = (topk_gates[:, :, None] * jax.nn.one_hot(topk_idx, N_EXPERTS, dtype=topk_gates.dtype)).sum(axis=1)
            y = jnp.zeros((N, D), dtype=x.dtype)
            for e in range(N_EXPERTS):
                y = y + combine[:, e:e + 1] * (hidden @ w_down[e].T)
            return y.reshape(B, T, D)
        return _moe_forward(x, w_router, w_gate, w_down)
    x = L0_attn_x
    xn = _layernorm(x, axis=-1)
    x = x + _L0_attn_ref(xn, L0_attn_Wg_w, L0_attn_Wg_b, L0_attn_Wr_w, L0_attn_Wr_b, L0_attn_Wk_w, L0_attn_Wk_b, L0_attn_Wv_w, L0_attn_Wv_b, L0_attn_Wo_w, L0_attn_Wo_b, L0_attn_mg, L0_attn_mr, L0_attn_mk, L0_attn_mv, L0_attn_w, L0_attn_u) + _L0_ffn_ref(xn, L0_ffn_ln1_g, L0_ffn_ln1_b, L0_ffn_ln2_g, L0_ffn_ln2_b, L0_ffn_Wq, L0_ffn_bq, L0_ffn_Wk, L0_ffn_bk, L0_ffn_Wv, L0_ffn_bv, L0_ffn_Wp, L0_ffn_bp, L0_ffn_gate_W, L0_ffn_gate_b, L0_ffn_exp_W1, L0_ffn_exp_b1, L0_ffn_exp_W2, L0_ffn_exp_b2)
    xn = _layernorm(x, axis=-1)
    x = x + _L1_attn_ref(xn, L1_attn_Wqa, L1_attn_Wqb, L1_attn_Wkva, L1_attn_Wkvb, L1_attn_Wout, L1_attn_bout) + _L1_ffn_ref(xn, L1_ffn_w_router, L1_ffn_w_gate, L1_ffn_w_down)
    return x

_drawn_inputs = setup_inputs


def setup_inputs(seed=0):
    import zlib

    import numpy as np

    out = dict(_drawn_inputs(seed))
    spreads = {'L0_attn_Wg_b': (0.0, 0.738),
     'L0_attn_Wr_b': (0.0, 0.1),
     'L0_attn_Wk_b': (0.0, 0.1),
     'L0_attn_Wv_b': (0.0, 0.1),
     'L0_attn_Wo_b': (0.0, 0.1),
     'L0_ffn_ln1_g': (1.0, 0.6),
     'L0_ffn_ln1_b': (0.0, 0.8),
     'L0_ffn_ln2_g': (1.0, 0.6),
     'L0_ffn_ln2_b': (0.0, 0.8),
     'L0_ffn_bq': (0.0, 0.8),
     'L0_ffn_bk': (0.0, 0.8),
     'L0_ffn_bv': (0.0, 0.613),
     'L0_ffn_bp': (0.0, 0.1),
     'L0_ffn_gate_b': (0.0, 0.295),
     'L0_ffn_exp_b1': (0.0, 0.8),
     'L0_ffn_exp_b2': (0.0, 0.1)}
    factors = {'L0_ffn_Wq': 8.0,
     'L0_ffn_Wk': 8.0,
     'L0_ffn_Wv': 8.0,
     'L0_ffn_Wp': 4.401,
     'L0_ffn_exp_W1': 3.02,
     'L0_ffn_exp_W2': 2.712,
     'L1_attn_Wqa': 8.0,
     'L1_attn_Wqb': 8.0,
     'L1_attn_Wkva': 8.0,
     'L1_attn_Wkvb': 8.0,
     'L1_attn_Wout': 8.0,
     'L1_attn_bout': 5.506,
     'L1_ffn_w_router': 5.875,
     'L1_ffn_w_gate': 5.205,
     'L1_ffn_w_down': 5.156}
    for name, (base, spread) in spreads.items():
        noise = np.random.default_rng([zlib.crc32(name.encode()), seed]).standard_normal(out[name].shape)
        drawn = base * np.exp(spread * noise) if base else spread * noise
        out[name] = jnp.asarray(drawn.astype(out[name].dtype))
    for name, factor in factors.items():
        out[name] = (out[name] * factor).astype(out[name].dtype)
    return out
```

```python
from contextlib import ExitStack

import numpy as np

import concourse.bass as bass
from concourse import mybir

F32 = mybir.dt.float32
BF16 = mybir.dt.bfloat16
ACT = mybir.ActivationFunctionType
ALU = mybir.AluOpType
AX = mybir.AxisListType

D = 128
NB, T = 2, 1024
N = NB * T
CH = 512
NC = N // CH
TB = N // 128
KB = T // 128
H, HD = 16, 8
G = 4
E = 8
HID0, HID1 = 512, 256
CAP = 320.0
KVH = 4
QL, KVL = 64, 32
PARTS = 3
ROWS = PARTS * PARTS * HD
MROWS = ROWS + PARTS
EPS = 1e-5
NEG = -1e30
SCALE = HD ** -0.5

COLS = ["mg", "mr", "mk", "mv", "bg", "br", "bk", "bv", "bo", "w", "u", "ln1g", "ln1b", "ln2g", "ln2b",
        "bq", "bkf", "bp", "bout"]
COL = {n: i for i, n in enumerate(COLS)}


def build_program(nc, t, out, stop=99):
    ctx = ExitStack()
    with ctx:
        def sb(name, shape, dt=F32):
            return ctx.enter_context(nc.sbuf_tensor(name, shape, dt))

        def sem(name):
            return ctx.enter_context(nc.semaphore(name))

        ps = ctx.enter_context(nc.psum_tensor("ps", [128, 8, CH], F32))

        xT = sb("xT", [128, N])
        xnp = sb("xnp", [128, NB, T + 1])
        acc = sb("acc", [128, N])
        cols = sb("cols", [128, len(COLS)])
        wl0 = sb("wl0", [128, 5, 128])
        wf = sb("wf", [128, 4, 128])
        cst = sb("cst", [128, 5, 128])
        idb = sb("idb", [128, 128], BF16)
        mskb = sb("mskb", [128, 2, 128], BF16)
        eps = sb("eps", [128, 1])
        pool_a = sb("pool_a", [128, 8192])
        pool_b = sb("pool_b", [128, 12288])
        vst = sb("vst", [128, 3, KB * G * 32])
        osb = sb("osb", [128, 3, T])
        small = sb("small", [128, 1024])
        wl1 = sb("wl1", [128, 848])
        h = sb("h", [128, N])

        meanM, headM, ident, tri, ones = (cst[:, i, :] for i in range(5))

        def dram(name, shape, dt=F32):
            return nc.dram_tensor(name, shape, dt, kind="Internal").ap()
        qd = [dram(f"qd{l}", [NB, H, PARTS, HD, T], BF16) for l in range(2)]
        kd = [dram("kd0", [NB, H, 5, HD, T], BF16), dram("kd1", [NB, KVH, 5, HD, T], BF16)]
        vd = [dram("vd0", [NB, G, 128, KB * G * 32]), dram("vd1", [NB, KVH, 128, KB * 32])]
        yd = [dram(f"yd{l}", [NB, H, 2, HD, T]) for l in range(2)]
        wd = [dram(f"wd{l}", [E, N]) for l in range(2)]

        def c_of(c):
            return slice(c * CH, (c + 1) * CH)

        def full(buf, k):
            return buf[:, k * N:(k + 1) * N]

        def xn_chunk(c):
            o = (c % 2) * CH
            return xnp[:, c // 2, 1 + o:1 + o + CH]

        def xs_chunk(c):
            o = (c % 2) * CH
            return xnp[:, c // 2, o:o + CH]

        def col(name):
            return cols[:, COL[name]:COL[name] + 1]

        s_mean, s_cent, s_sq, s_var, s_std, s_inv, s_normed, s_scaled = (
            sem(f"norm_{n}") for n in ("mean", "centred", "squared", "variance", "deviation", "inverse", "done",
                                       "scaled"))

        class Norm:
            def __init__(self, k, src, cen, sq, dst, matrix, banks, gain=None, bias=None, extra=None, scaled=0):
                self.base = NC * k
                self.scaled = NC * scaled
                self.src, self.cen, self.sq, self.dst, self.matrix = src, cen, sq, dst, matrix
                self.banks, self.gain, self.bias, self.extra = banks, gain, bias, extra

        def norm_pe(pe, L, ready=None):
            for c in range(NC):
                if ready is not None:
                    pe.wait_ge(ready, c + 1)
                if c >= 2:
                    pe.wait_ge(s_cent, L.base + c - 1)
                nc.tensor.matmul(ps[:, L.banks + c % 2, :], L.matrix, L.src(c), start=True, stop=True)\
                    .then_inc(s_mean, 1)
            for c in range(NC):
                pe.wait_ge(s_sq, L.base + c + 1)
                if c >= 2:
                    pe.wait_ge(s_std, L.base + c - 1)
                nc.tensor.matmul(ps[:, L.banks + 2 + c % 2, :], L.matrix, L.sq(c), start=True, stop=True)\
                    .then_inc(s_var, 1)

        def norm_dve(dve, L):
            for c in range(NC):
                dve.wait_ge(s_mean, L.base + c + 1)
                nc.vector.tensor_tensor(L.cen(c), L.src(c), ps[:, L.banks + c % 2, :], ALU.subtract)\
                    .then_inc(s_cent, 1)
            for c in range(NC):
                dve.wait_ge(s_std, L.base + c + 1)
                nc.vector.reciprocal(L.sq(c), L.sq(c)).then_inc(s_inv, 1)
                dve.wait_ge(s_inv, L.base + c + 1)
                if L.extra is not None:
                    nc.vector.tensor_tensor(L.sq(c), L.sq(c), L.extra(c), ALU.mult).then_inc(s_scaled, 1)
                    dve.wait_ge(s_scaled, L.scaled + c + 1)
                if L.gain is None:
                    nc.vector.tensor_tensor(L.dst(c), L.cen(c), L.sq(c), ALU.mult).then_inc(s_normed, 1)
                else:
                    nc.vector.scalar_tensor_tensor(L.dst(c), L.cen(c), L.gain, L.sq(c), ALU.mult, ALU.mult)\
                        .then_inc(s_scaled, 1)
                    dve.wait_ge(s_scaled, L.scaled + c + 1)
                    nc.vector.tensor_scalar(L.dst(c), L.dst(c), L.bias, None, ALU.add).then_inc(s_normed, 1)

        def norm_act(act, L):
            for c in range(NC):
                act.wait_ge(s_cent, L.base + c + 1)
                nc.scalar.activation(L.sq(c), L.cen(c), ACT.Square).then_inc(s_sq, 1)
            for c in range(NC):
                act.wait_ge(s_var, L.base + c + 1)
                nc.scalar.activation(L.sq(c), ps[:, L.banks + 2 + c % 2, :], ACT.Sqrt, bias=eps[:, 0:1])\
                    .then_inc(s_std, 1)

        class Split:
            def __init__(self, name, f, parts, dst, copies, rows=128, after=None):
                self.copies = copies
                self.f, self.parts, self.dst, self.rows = f, parts, dst, rows
                self.base, self.base_stored = (NC, 16 * after.copies * NC) if after else (0, 0)
                self.full, self.hi, self.r1, self.mid, self.lo, self.stored = (
                    (after.full, after.hi, after.r1, after.mid, after.lo, after.stored) if after else
                    (sem(f"{name}_{s}") for s in ("full", "hi", "r1", "mid", "lo", "stored")))

        def split_dve(dve, S, c):
            R = S.rows
            dve.wait_ge(S.hi, S.base + c + 1)
            nc.vector.tensor_tensor(S.f(c)[0:R], S.f(c)[0:R], S.parts(0, c)[0:R], ALU.subtract).then_inc(S.r1, 1)
            dve.wait_ge(S.mid, S.base + c + 1)
            nc.vector.tensor_tensor(S.parts(2, c)[0:R], S.f(c)[0:R], S.parts(1, c)[0:R], ALU.subtract)\
                .then_inc(S.lo, 1)

        def split_act(act, S, c):
            R = S.rows
            act.wait_ge(S.full, S.base + c + 1)
            nc.scalar.copy(S.parts(0, c)[0:R], S.f(c)[0:R]).then_inc(S.hi, 1)
            act.wait_ge(S.r1, S.base + c + 1)
            nc.scalar.copy(S.parts(1, c)[0:R], S.f(c)[0:R]).then_inc(S.mid, 1)

        def split_store(sp, S, c):
            sp.wait_ge(S.lo, S.base + c + 1)
            half = slice((c % 2) * CH, (c % 2 + 1) * CH)
            for p in range(S.copies):
                sp.dma_start(S.dst[c // 2, :, p, :, half], S.parts(p % PARTS, c)[0:S.rows]).then_inc(S.stored, 16)

        f = [full(pool_b, k) for k in range(6)]
        fa = [full(pool_a, k) for k in range(4)]
        n0 = Norm(0, lambda c: xT[:, c_of(c)], lambda c: f[0][:, c_of(c)], lambda c: f[1][:, c_of(c)],
                  xn_chunk, meanM, 0)
        mixes = [fa[0], fa[1]]
        kv, scn, rw, sig = f[2], f[3], f[4], f[5]
        nr = Norm(1, lambda c: rw[:, c_of(c)], lambda c: f[0][:, c_of(c)], lambda c: f[1][:, c_of(c)],
                  lambda c: kv[:, c_of(c)], headM, 0, extra=lambda c: sig[:, c_of(c)], scaled=0)
        n1 = Norm(2, xn_chunk, lambda c: f[0][:, c_of(c)], lambda c: f[1][:, c_of(c)],
                  lambda c: h[:, c_of(c)], meanM, 0, gain=col("ln1g"), bias=col("ln1b"), scaled=1)
        partb = pool_a[:, 0:PARTS * N].bitcast(BF16).rearrange("p (k a n) -> p k a n", k=2, a=PARTS)
        qs_ = Split("sq", lambda c: f[2][:, c_of(c)], lambda p, c: partb[:, 0, p, c_of(c)], qd[0], 3)
        ks_ = Split("sk", lambda c: f[3][:, c_of(c)], lambda p, c: partb[:, 1, p, c_of(c)], kd[0], 5)
        bvb, gbb, rev = small[:, 0:128], small[:, 128:136], small[:, 136:144]
        dec = small[:, 144:146]
        msk32 = osb[:, 1, 0:256].rearrange("p (k n) -> p k n", k=2)
        decb = osb[:, 0, :]

        ld_x, ld_w, one_eps = sem("ld_x"), sem("ld_w"), sem("eps_set")
        NLD = 9
        wrap, dlt, mixed, proj, vsb, kvd, scd, t2d, rwd, sgd = (
            sem(n) for n in ("wrap", "dlt", "mixed", "proj", "v_there", "kv_done", "scan_done",
                             "bonus_done", "rw_done", "gate_done"))
        dcy, dcyb, wo_mm, wo_ev, qk_mm, v_mm, v_ev, castd = (
            sem(n) for n in ("decay", "decay_wide", "wo_mm", "wo_ev", "qk_mm", "v_mm", "v_ev", "const_cast"))
        v_ones, v_stored = sem("v_ones"), [sem("v_stored0"), sem("v_stored1")]
        vstage = [fa[3], vst[:, 0:2, :].rearrange("p s n -> p (s n)")]
        MIX = ["mk", "mv", "mr", "mg"]
        WIX = [2, 3, 1, 0]

        with nc.Block() as block:
            @block.sync
            def _(sp):
                for c in range(NC):
                    sp.dma_start(xT[:, c_of(c)], t["xT"][:, c_of(c)]).then_inc(ld_x, 16)
                sp.dma_start(wf[:, :, :], t["wf"]).then_inc(ld_w, 16)
                sp.dma_start(bvb, t["bv"].partition_broadcast(128)).then_inc(ld_w, 16)
                sp.dma_start(gbb, t["gate_b"].partition_broadcast(128)).then_inc(ld_w, 16)
                sp.dma_start(rev, t["rev"].partition_broadcast(128)).then_inc(ld_w, 16)
                for c in range(NC):
                    split_store(sp, qs_, c)
                    split_store(sp, ks_, c)
                    sp.wait_ge(v_ev, 4 * (c + 1))
                    k0 = 4 * (c % 2) * G * 32
                    sp.dma_start(vd[0][c // 2].rearrange("g p n -> p g n")[:, :, k0:k0 + 4 * G * 32],
                                 vstage[c % 2].rearrange("p (g n) -> p g n", g=G)).then_inc(v_stored[c % 2], 16)
                for k in range(2):
                    sp.wait_ge(v_stored[k], 16 * NC // 2)
                sp.wait_ge(qs_.stored, 16 * qs_.copies * NC)
                sp.wait_ge(ks_.stored, 16 * ks_.copies * NC)

            @block.gpsimd
            def _(pool):
                nc.gpsimd.memset(vstage[1], 1.0).then_inc(v_ones, 1)
                pool.wait_ge(mixed, 4 * NC)
                nc.gpsimd.memset(vstage[0], 1.0).then_inc(v_ones, 1)

            @block.scalar
            def _(act):
                act.dma_start(cst[:, :, :], t["cst"]).then_inc(ld_w, 16)
                act.dma_start(cols[:, :], t["cols"]).then_inc(ld_w, 16)
                act.dma_start(wl0[:, :, :], t["wl0"]).then_inc(ld_w, 16)
                act.dma_start(wl1[:, :], t["wl1"]).then_inc(ld_w, 16)
                act.dma_start(msk32, t["mask"]).then_inc(ld_w, 16)
                act.wait_ge(ld_w, 16 * NLD)
                nc.scalar.activation(dec[:, 0:1], col("w"), ACT.Exp).then_inc(dcy, 1)
                act.wait_ge(dcy, 1)
                nc.scalar.activation(dec[:, 1:2], dec[:, 0:1], ACT.Exp, scale=-1.0).then_inc(dcy, 1)
                act.wait_ge(one_eps, 1)
                norm_act(act, n0)
                for c in range(NC):
                    act.wait_ge(proj, c + 1)
                    b = 4 * (c % 2)
                    nc.scalar.activation(fa[2][:, c_of(c)], ps[:, b + 1, :], ACT.Identity, bias=col("bv"))\
                        .then_inc(vsb, 1)
                    nc.scalar.activation(sig[:, c_of(c)], ps[:, b + 3, :], ACT.Sigmoid, bias=col("bg"))\
                        .then_inc(sgd, 1)
                norm_act(act, nr)
                norm_act(act, n1)
                for c in range(NC):
                    split_act(act, qs_, c)
                    split_act(act, ks_, c)

            @block.vector
            def _(dve):
                nc.vector.memset(eps[:, :], EPS).then_inc(one_eps, 1)
                dve.wait_ge(ld_w, 16 * NLD)
                nc.vector.tensor_copy(idb[:, :], ident).then_inc(castd, 1)
                nc.vector.tensor_copy(mskb[:, :, :], msk32).then_inc(castd, 1)
                norm_dve(dve, n0)
                dve.wait_ge(dcy, 2)
                dve.wait_ge(s_normed, n0.base + NC)
                nc.vector.tensor_copy(xnp[:, :, 0:1], xnp[:, :, T:T + 1]).then_inc(wrap, 1)
                nc.vector.memset(decb, 0.0).then_inc(dcyb, 1)
                dve.wait_ge(dcyb, 1)
                nc.vector.tensor_scalar(decb, decb, dec[:, 1:2], None, ALU.add).then_inc(dcyb, 1)
                dve.wait_ge(dcyb, 2)
                dve.wait_ge(wrap, 1)

                def mix(c):
                    if c >= 2:
                        dve.wait_ge(proj, c - 1)
                    d = fa[3][:, c_of(c)]
                    nc.vector.tensor_tensor(d, xn_chunk(c), xs_chunk(c), ALU.subtract).then_inc(dlt, 1)
                    dve.wait_ge(dlt, c + 1)
                    for j in range(4):
                        nc.vector.scalar_tensor_tensor(mixes[c % 2][:, j * CH:(j + 1) * CH], d, col(MIX[j]),
                                                       xs_chunk(c), ALU.mult, ALU.add).then_inc(mixed, 1)

                def recur(c):
                    b = 4 * (c % 2)
                    cs = c_of(c)
                    dve.wait_ge(vsb, c + 1)
                    nc.vector.scalar_tensor_tensor(kv[:, cs], ps[:, b + 0, :], col("bk"), fa[2][:, cs],
                                                   ALU.add, ALU.mult).then_inc(kvd, 1)
                    dve.wait_ge(kvd, c + 1)
                    init = 0.0 if c % 2 == 0 else scn[:, c * CH - 1:c * CH]
                    if c % 2:
                        dve.wait_ge(scd, c)
                    nc.vector.tensor_tensor_scan(scn[:, cs], decb[:, 0:CH], kv[:, cs], init, ALU.mult, ALU.add)\
                        .then_inc(scd, 1)
                    dve.wait_ge(scd, c + 1)
                    nc.vector.scalar_tensor_tensor(kv[:, cs], kv[:, cs], col("u"), scn[:, cs],
                                                   ALU.mult, ALU.add).then_inc(t2d, 1)
                    dve.wait_ge(t2d, c + 1)
                    nc.vector.scalar_tensor_tensor(rw[:, cs], ps[:, b + 2, :], col("br"), kv[:, cs],
                                                   ALU.add, ALU.mult).then_inc(rwd, 1)

                mix(0)
                for c in range(NC):
                    if c + 1 < NC:
                        mix(c + 1)
                    recur(c)
                dve.wait_ge(sgd, NC)
                norm_dve(dve, nr)
                norm_dve(dve, n1)
                for c in range(NC):
                    dve.wait_ge(wo_mm, c + 1)
                    nc.vector.scalar_tensor_tensor(acc[:, c_of(c)], ps[:, 4 + c, :], col("bo"), xT[:, c_of(c)],
                                                   ALU.add, ALU.add).then_inc(wo_ev, 1)
                for c in range(NC):
                    b = 2 * (c % 2)
                    dve.wait_ge(qk_mm, c + 1)
                    nc.vector.tensor_scalar(qs_.f(c), ps[:, b, :], col("bq"), SCALE, ALU.add, ALU.mult)\
                        .then_inc(qs_.full, 1)
                    nc.vector.tensor_scalar(ks_.f(c), ps[:, b + 1, :], col("bkf"), None, ALU.add)\
                        .then_inc(ks_.full, 1)
                    split_dve(dve, qs_, c)
                    split_dve(dve, ks_, c)
                    dve.wait_ge(v_mm, c + 1)
                    if c == 0:
                        dve.wait_ge(v_ones, 2)
                    if c >= 2:
                        dve.wait_ge(v_stored[c % 2], 16 * (c // 2))
                    for k in range(4):
                        nc.vector.tensor_tensor(
                            vstage[c % 2].rearrange("p (g k i w) -> p k g i w", g=G, k=4, i=G)[:, k, :, :, 0:HD],
                            ps[:, 4 + c, k * 128:(k + 1) * 128].rearrange("p (g i w) -> p g i w", g=G, i=G),
                            bvb.rearrange("p (g i w) -> p g i w", g=G, i=G), ALU.add).then_inc(v_ev, 1)

            @block.tensor
            def _(pe):
                pe.wait_ge(ld_w, 16 * NLD)
                pe.wait_ge(ld_x, 16 * NC)
                norm_pe(pe, n0)
                for c in range(NC):
                    pe.wait_ge(mixed, 4 * (c + 1))
                    if c == 0:
                        pe.wait_ge(s_std, n0.base + NC)
                    if c >= 2:
                        pe.wait_ge(rwd, c - 1)
                        pe.wait_ge(sgd, c - 1)
                    for j in range(4):
                        ins = nc.tensor.matmul(ps[:, 4 * (c % 2) + j, :], wl0[:, WIX[j], :],
                                               mixes[c % 2][:, j * CH:(j + 1) * CH], start=True, stop=True)
                    ins.then_inc(proj, 1)
                pe.wait_ge(rwd, NC)
                pe.wait_ge(sgd, NC)
                norm_pe(pe, nr)
                pe.wait_ge(s_std, nr.base + NC)
                norm_pe(pe, n1)
                for c in range(NC):
                    pe.wait_ge(s_normed, nr.base + c + 1)
                    nc.tensor.matmul(ps[:, 4 + c, :], wl0[:, 4, :], kv[:, c_of(c)], start=True, stop=True)\
                        .then_inc(wo_mm, 1)
                pe.wait_ge(s_std, n1.base + NC)
                for c in range(NC):
                    b = 2 * (c % 2)
                    pe.wait_ge(s_normed, n1.base + c + 1)
                    if c >= 2:
                        pe.wait_ge(ks_.full, c - 1)
                        pe.wait_ge(qs_.full, c - 1)
                    for j in range(2):
                        ins = nc.tensor.matmul(ps[:, b + j, :], wf[:, j, :], h[:, c_of(c)], start=True, stop=True)
                    ins.then_inc(qk_mm, 1)
                    pe.wait_ge(wo_ev, c + 1)
                    for k in range(4):
                        tb = 4 * c + k
                        ins = nc.tensor.matmul(ps[:, 4 + c, k * 128:(k + 1) * 128], h[:, tb * 128:(tb + 1) * 128],
                                               wf[:, 2, :], start=True, stop=True)
                    ins.then_inc(v_mm, 1)

        if stop == 1:
            return dump(nc, sem, acc, out)


        def attention(l, kh, vw):
            ROLL = 3
            UNITS = NB * G
            qst = pool_b[:, 0:6144].bitcast(BF16).rearrange("p (s i n) -> p s i n", s=ROLL, i=G)
            kst = pool_b[:, 6144:12288].bitcast(BF16).rearrange("p (s i n) -> p s i n", s=ROLL, i=G)
            prob = pool_a[:, :].rearrange("p (s i n) -> p s i n", s=2, i=G)
            vals = vst[:, :, 0:KB * vw * 32].rearrange("p s (k i w) -> p s k i w", k=KB, i=vw)
            lowmax = small[:, 256:288]
            highmax = small[:, 288:304]
            rem = small[:, 304:336]
            mpart = small[:, 336:384].bitcast(BF16).rearrange("p (a c) -> p a c", a=PARTS)
            mT = small[:, 384:576].bitcast(BF16).rearrange("p (s n) -> p s n", s=ROLL)
            turned = ps[:, 6, 0:64].bitcast(BF16)
            s = {n: sem(f"a{l}_{n}") for n in (
                "ones", "a_mm", "a_red", "folded", "hi", "r1", "mid", "parts", "turned", "m_copied",
                "m_set0", "m_set1", "m_set2", "b_mm", "exp", "pv", "evac",
                "st0", "st1", "st2", "ld0", "ld1", "ld2")}
            TILES = [(i, qb, hf) for i in range(G) for qb in range(KB) for hf in range(1 + qb // 4)]
            NT = len(TILES)
            NE = KB * G
            NLOAD = 2 * PARTS + 1
            PEEL = UNITS // ROLL * ROLL

            def all_units(eng, body):
                with eng.Fori(0, UNITS // ROLL) as r:
                    for k in range(ROLL):
                        body(r * ROLL + k, k, r, False)
                for k in range(UNITS - PEEL):
                    body(PEEL + k, k, UNITS // ROLL, k == UNITS - PEEL - 1)

            with nc.Block() as block:
                @block.sync
                def _(sp):
                    qrows = qd[l].rearrange("b h a d n -> (b h a d) n")
                    krows = kd[l].rearrange("b h a d n -> (b h a d) n")
                    vrows = vd[l].rearrange("b g p n -> (b g p) n")
                    yrows = yd[l].rearrange("b h k d n -> (b h k d) n")

                    def load(u, slot):
                        for j in range(PARTS):
                            r = PARTS * HD * j
                            sp.dma_start(qst[r:r + PARTS * HD, slot],
                                         qrows[bass.ds(u * (G * PARTS * HD), G * PARTS * HD), :]
                                         .rearrange("(i x) n -> x i n", i=G)).then_inc(s[f"ld{slot}"], 16)
                            sp.dma_start(kst[r:r + PARTS * HD, slot, 0:kh],
                                         krows[bass.ds(u * (kh * 5 * HD), kh * 5 * HD), :]
                                         .rearrange("(i x) n -> x i n", i=kh)[HD * j:HD * (j + PARTS)])\
                                .then_inc(s[f"ld{slot}"], 16)

                        sp.dma_start(vst[:, slot, 0:KB * vw * 32], vrows[bass.ds(u * 128, 128), :])\
                            .then_inc(s[f"ld{slot}"], 16)

                    def set_max(u, slot):
                        sp.wait_ge(s["m_copied"], u + 1)
                        sp.dma_start(qst[ROWS:MROWS, slot].rearrange("a i n -> a (i n)"), mT[0:96, slot, :])\
                            .then_inc(s[f"m_set{slot}"], 16)

                    for k in range(ROLL):
                        sp.sem_inc(s[f"st{k}"], 16)
                    sp.wait_ge(s["ones"], 1)
                    load(0, 0)
                    load(1, 1)
                    set_max(0, 0)

                    def body(u, slot, r, last):
                        if not isinstance(u, int):
                            sp.wait_ge(s["pv"], u * KB + 1)
                            load(u + 2, (slot + 2) % ROLL)
                        if not last:
                            set_max(u + 1, (slot + 1) % ROLL)
                        sp.wait_ge(s["evac"], u + 2)
                        for i in range(G):
                            sp.dma_start(yrows[bass.ds(u * (G * 2 * HD) + i * 2 * HD, 2 * HD), :],
                                         osb[32 * i:32 * i + 2 * HD, slot, :]).then_inc(s[f"st{slot}"], 16)
                    all_units(sp, body)
                    for k in range(ROLL):
                        sp.wait_ge(s[f"st{k}"], 16 + 16 * G * ((UNITS - k + ROLL - 1) // ROLL))

                @block.gpsimd
                def _(pool):
                    nc.gpsimd.memset(kst[64:MROWS], 1.0).then_inc(s["ones"], 1)

                @block.scalar
                def _(act):
                    act.sem_inc(s["exp"], 1)
                    act.sem_inc(s["evac"], 1)

                    def body(u, slot, r, last):
                        for kb in range(KB):
                            if kb == 0:
                                act.wait_ge(s["pv"], u * KB + 1)
                            if kb >= 2:
                                act.wait_ge(s["pv"], u * KB + kb)
                            for i in range(G):
                                e = kb * G + i
                                w = T - 128 * kb
                                act.wait_ge(s["b_mm"], u * NE + (e + 1))
                                nc.scalar.activation(
                                    prob[:, kb % 2, i, 0:w],
                                    ps[:, 2 * (e % 2):2 * (e % 2) + 2, :].rearrange("p b n -> p (b n)")[:, 0:w],
                                    ACT.Exp).then_inc(s["exp"], 1)
                        act.wait_ge(s[f"st{slot}"], r * (16 * G) + 16)
                        act.wait_ge(s["pv"], u * KB + (KB + 1))
                        nc.scalar.copy(osb[:, slot, :], ps[:, 4:6, :].rearrange("p b n -> p (b n)"))\
                            .then_inc(s["evac"], 1)
                    all_units(act, body)

                @block.vector
                def _(dve):
                    def maxima(u, slot):
                        for n, (i, qb, hf) in enumerate(TILES):
                            w = min(CH, (qb + 1) * 128 - hf * CH)
                            dst = highmax[:, i * 4 + qb - 4:i * 4 + qb - 3] if hf else \
                                lowmax[:, i * KB + qb:i * KB + qb + 1]
                            dve.wait_ge(s["a_mm"], u * NT + (n + 1))
                            nc.vector.tensor_reduce(dst, ps[:, 6 + n % 2, 0:w], AX.X, ALU.max, negate=True)\
                                .then_inc(s["a_red"], 1)
                        dve.wait_ge(s["a_red"], u * NT + NT)
                        late = lowmax.rearrange("p (i k) -> p i k", i=G)[:, :, 4:KB]
                        nc.vector.tensor_tensor(late, late, highmax.rearrange("p (i k) -> p i k", i=G), ALU.min)\
                            .then_inc(s["folded"], 1)
                        dve.wait_ge(s["folded"], u + 1)
                        nc.vector.tensor_copy(mpart[:, 0, :], lowmax).then_inc(s["hi"], 1)
                        dve.wait_ge(s["hi"], u + 1)
                        nc.vector.tensor_tensor(rem, lowmax, mpart[:, 0, :], ALU.subtract).then_inc(s["r1"], 1)
                        dve.wait_ge(s["r1"], u + 1)
                        nc.vector.tensor_copy(mpart[:, 1, :], rem).then_inc(s["mid"], 1)
                        dve.wait_ge(s["mid"], u + 1)
                        nc.vector.tensor_tensor(mpart[:, 2, :], rem, mpart[:, 1, :], ALU.subtract)\
                            .then_inc(s["parts"], 1)
                        dve.wait_ge(s["turned"], u + 1)
                        nc.vector.tensor_copy(mT[0:96, slot, :], turned[0:96, :]).then_inc(s["m_copied"], 1)

                    maxima(0, 0)

                    def body(u, slot, r, last):
                        if not last:
                            maxima(u + 1, (slot + 1) % ROLL)
                    all_units(dve, body)

                @block.tensor
                def _(pe):
                    def tile_a(u, slot, n, first):
                        i, qb, hf = TILES[n]
                        w = min(CH, (qb + 1) * 128 - hf * CH)
                        if n >= 2 or not first:
                            pe.wait_ge(s["a_red"], u * NT + (n - 1))
                        kst_i = kst[0:ROWS, slot, i if kh > 1 else 0, :]
                        diagonal = hf == qb // 4
                        mm = nc.tensor.matmul(ps[:, 6 + n % 2, 0:w], qst[0:ROWS, slot, i, qb * 128:(qb + 1) * 128],
                                              kst_i[:, hf * CH:hf * CH + w], start=True, stop=True)
                        if diagonal:
                            mm = nc.tensor.matmul(ps[:, 6 + n % 2, w - 128:w], idb[:, :], mskb[:, 0, :],
                                                  start=False, stop=True, skip_group_check=True)
                        mm.then_inc(s["a_mm"], 1)

                    def begin_a(u, slot, r_load, first):
                        pe.wait_ge(s[f"ld{slot}"], r_load)
                        if not first:
                            pe.wait_ge(s["m_copied"], u)

                    def turn(u):
                        pe.wait_ge(s["parts"], u + 1)
                        nc.tensor.transpose(turned[0:96, :], mpart.rearrange("p a c -> p (a c)"), idb[:, :])\
                            .then_inc(s["turned"], 1)

                    def multiply(u, slot, kb):
                        if kb == 0:
                            pe.wait_ge(s["evac"], u + 1)
                        pe.wait_ge(s["exp"], u * NE + (G * (kb + 1) + 1))
                        for hf in range(kb // 4, 2):
                            lo = max(0, kb * 128 - hf * CH)
                            for i in range(G):
                                p0 = hf * CH + lo - kb * 128
                                mm = nc.tensor.matmul(ps[32 * i:32 * i + 32, 4 + hf, lo:CH],
                                                      vals[:, slot, kb, i if vw > 1 else 0, :],
                                                      prob[:, kb % 2, i, p0:p0 + CH - lo],
                                                      start=(kb == 0), stop=(kb == 4 * hf + 3),
                                                      tile_position=(0, 32 * i), skip_group_check=True)
                        mm.then_inc(s["pv"], 1)

                    pe.sem_inc(s["pv"], 1)
                    pe.wait_ge(s["ones"], 1)
                    begin_a(0, 0, 16 * NLOAD, True)
                    for n in range(NT):
                        tile_a(0, 0, n, True)
                    turn(0)

                    def body(u, slot, r, last):
                        nxt = (slot + 1) % ROLL
                        if not last:
                            begin_a(u + 1, nxt, (r + (2 if nxt == 0 else 1)) * (16 * NLOAD), False)
                        pe.wait_ge(s[f"m_set{slot}"], r * 16 + 16)
                        for e in range(NE):
                            kb, i = e // G, e % G
                            w = T - 128 * kb
                            pe.wait_ge(s["exp"], u * NE + max(1, e))
                            for c0 in range(0, w, CH):
                                cw = min(CH, w - c0)
                                mm = nc.tensor.matmul(
                                    ps[:, 2 * (e % 2) + c0 // CH, 0:cw],
                                    kst[0:MROWS, slot, i if kh > 1 else 0, kb * 128:(kb + 1) * 128],
                                    qst[0:MROWS, slot, i, kb * 128 + c0:kb * 128 + c0 + cw], start=True, stop=True)
                                if c0 == 0:
                                    mm = nc.tensor.matmul(ps[:, 2 * (e % 2), 0:128], idb[:, :], mskb[:, 1, :],
                                                          start=False, stop=True, skip_group_check=True)
                            mm.then_inc(s["b_mm"], 1)
                            if not last:
                                for n in range(2 * e, min(2 * e + 2, NT)):
                                    tile_a(u + 1, nxt, n, False)
                                if e == NT // 2 + 2:
                                    turn(u + 1)
                            if kb >= 1 and i == 1:
                                multiply(u, slot, kb - 1)
                        multiply(u, slot, KB - 1)
                    all_units(pe, body)

        attention(0, G, G)
        if stop == 2:
            return dump_yd(nc, sem, yd[0], pool_a, out)

        def top_one(dve_step, values, onehot, m, eq, sc, cm):
            v3 = lambda ap: ap.rearrange("p (t e) -> p t e", e=E)
            wide = lambda ap: ap.unsqueeze(2).to_broadcast([128, TB, E])
            dve_step(nc.vector.tensor_reduce(m, v3(values), AX.X, ALU.max))
            dve_step(nc.vector.tensor_tensor(v3(eq), v3(values), wide(m), ALU.is_equal))
            dve_step(nc.vector.tensor_tensor(v3(sc), v3(eq), rev.unsqueeze(1).to_broadcast([128, TB, E]), ALU.mult))
            dve_step(nc.vector.tensor_reduce(cm, v3(sc), AX.X, ALU.max))
            dve_step(nc.vector.tensor_tensor(v3(onehot), v3(sc), wide(cm), ALU.is_equal))

        vflat = vst[:, :, :].rearrange("p s n -> p (s n)")
        rt = lambda k: vflat[:, 1536 + 128 * k:1536 + 128 * (k + 1)]
        rs = lambda k: small[:, 640 + TB * k:640 + TB * (k + 1)]
        v3 = lambda ap: ap.rearrange("p (t e) -> p t e", e=E)
        wide = lambda ap: ap.unsqueeze(2).to_broadcast([128, TB, E])

        def route_pe(pe, weight, done):
            for tb in range(TB):
                mm = nc.tensor.matmul(ps[:, 0, tb * E:(tb + 1) * E], h[:, tb * 128:(tb + 1) * 128], weight,
                                      start=True, stop=True)
            mm.then_inc(done, 1)

        y3, w3 = f[2], f[3]
        n3 = Norm(3, lambda c: f[4][:, c_of(c)], lambda c: f[0][:, c_of(c)], lambda c: f[1][:, c_of(c)],
                  lambda c: h[:, c_of(c)], meanM, 0, gain=col("ln2g"), bias=col("ln2b"), scaled=2)
        ld_y = [sem(f"ld_y{b}") for b in range(NB)]
        rl3, yn3, wp3, xa3, ac3, lg3, ch3, gap3, ex3, w3r, w3t, w3c, w3s = (
            sem(f"s3_{n}") for n in ("recip", "y", "wp", "xa", "acc", "logits", "chain", "gap", "exp",
                                     "weights", "turned", "copied", "stored"))

        with nc.Block() as block:
            @block.sync
            def _(sp):
                for b in range(NB):
                    for k, dst in enumerate((y3, w3)):
                        sp.dma_start(dst[:, b * T:(b + 1) * T], yd[0][b, :, k]).then_inc(ld_y[b], 16)
                sp.wait_ge(w3c, 1)
                sp.dma_start(wd[0].rearrange("e (t n) -> (e t) n", n=128), rt(11)).then_inc(w3s, 16)
                sp.wait_ge(w3s, 16)

            @block.vector
            def _(dve):
                for c in range(NC):
                    dve.wait_ge(ld_y[c // 2], 32)
                    nc.vector.reciprocal(w3[:, c_of(c)], w3[:, c_of(c)]).then_inc(rl3, 1)
                    dve.wait_ge(rl3, c + 1)
                    nc.vector.tensor_tensor(y3[:, c_of(c)], y3[:, c_of(c)], w3[:, c_of(c)], ALU.mult)\
                        .then_inc(yn3, 1)
                for c in range(NC):
                    dve.wait_ge(wp3, c + 1)
                    nc.vector.scalar_tensor_tensor(f[4][:, c_of(c)], ps[:, 4 + c, :], col("bp"), xn_chunk(c),
                                                   ALU.add, ALU.add).then_inc(xa3, 1)
                    dve.wait_ge(xa3, c + 1)
                    nc.vector.tensor_tensor(acc[:, c_of(c)], acc[:, c_of(c)], f[4][:, c_of(c)], ALU.add)\
                        .then_inc(ac3, 1)
                norm_dve(dve, n3)
                steps = [0]

                def step(ins):
                    steps[0] += 1
                    ins.then_inc(ch3, 1)
                    dve.wait_ge(ch3, steps[0])

                dve.wait_ge(lg3, 1)
                logit, one1, one2, eq, sc = rt(0), rt(1), rt(2), rt(3), rt(4)
                m1, m2, cm, ew, w1, w2 = (rs(k) for k in range(6))
                step(nc.vector.tensor_tensor(v3(logit), v3(ps[:, 0, 0:128]),
                                             gbb.unsqueeze(1).to_broadcast([128, TB, E]), ALU.add))
                top_one(step, logit, one1, m1, eq, sc, cm)
                step(nc.vector.scalar_tensor_tensor(logit, one1, -3e38, logit, ALU.mult, ALU.add))
                top_one(step, logit, one2, m2, eq, sc, cm)
                nc.vector.tensor_tensor(m2, m2, m1, ALU.subtract).then_inc(gap3, 1)
                dve.wait_ge(ex3, 1)
                step(nc.vector.tensor_scalar(w1, ew, 1.0, None, ALU.add))
                step(nc.vector.reciprocal(w1, w1))
                step(nc.vector.tensor_tensor(w2, ew, w1, ALU.mult))
                step(nc.vector.tensor_tensor(v3(one1), v3(one1), wide(w1), ALU.mult))
                step(nc.vector.tensor_tensor(v3(one2), v3(one2), wide(w2), ALU.mult))
                nc.vector.tensor_tensor(rt(10).rearrange("p (e t) -> p t e", t=TB), v3(one1), v3(one2), ALU.add)\
                    .then_inc(w3r, 1)
                dve.wait_ge(w3t, 1)
                nc.vector.tensor_copy(rt(11), ps[:, 1, 0:128]).then_inc(w3c, 1)

            @block.scalar
            def _(act):
                norm_act(act, n3)
                act.wait_ge(gap3, 1)
                nc.scalar.activation(rs(3), rs(1), ACT.Exp).then_inc(ex3, 1)

            @block.tensor
            def _(pe):
                for c in range(NC):
                    pe.wait_ge(yn3, c + 1)
                    nc.tensor.matmul(ps[:, 4 + c, :], wf[:, 3, :], y3[:, c_of(c)], start=True, stop=True)\
                        .then_inc(wp3, 1)
                norm_pe(pe, n3, ready=xa3)
                pe.wait_ge(s_normed, n3.base + NC)
                route_pe(pe, wl1[:, 840:848], lg3)
                pe.wait_ge(w3r, 1)
                nc.tensor.transpose(ps[:, 1, 0:128], rt(10), ident).then_inc(w3t, 1)

        if stop == 3:
            return dump(nc, sem, acc, out)

        mid = pool_a[:, 0:4 * CH].rearrange("p (k n) -> p k n", k=4)
        wbc = [f[0], f[1]]
        w1s = [f[2][:, k * HID0:(k + 1) * HID0] for k in range(2)]
        w2s = [f[3][:, k * 512:(k + 1) * 512].rearrange("p (k n) -> p k n", k=4) for k in range(2)]
        tmp = f[4]
        x_ld, x_h, x_gelu, x_y, x_t, x_acc, x_b = ([sem("x_ld0"), sem("x_ld1")], sem("x_h"), sem("x_gelu"),
                                                   sem("x_y"), sem("x_tmp"), sem("x_acc"), sem("x_bias"))
        b1x = [f[5][:, 4 * k:4 * k + 4] for k in range(2)]
        b2x = [f[5][:, 8 + k:9 + k] for k in range(2)]

        with nc.Block() as block:
            @block.sync
            def _(sp):
                def load(e, k):
                    for dst, src in ((w1s[k], t["w1"][bass.ds(e, 1)].rearrange("o p n -> (o p) n")),
                                     (w2s[k], t["w2"][bass.ds(e, 1)].rearrange("o p k n -> (o p) k n")),
                                     (b1x[k], t["b1"][bass.ds(e, 1)].rearrange("o p k -> (o p) k")),
                                     (b2x[k], t["b2"][bass.ds(e, 1)].rearrange("o p k -> (o p) k")),
                                     (wbc[k], wd[0][bass.ds(e, 1)].rearrange("o n -> (o n)")
                                      .partition_broadcast(128))):
                        sp.dma_start(dst, src).then_inc(x_ld[k], 16)
                load(0, 0)
                load(1, 1)
                with sp.Fori(1, E // 2) as r:
                    for k in range(2):
                        sp.wait_ge(x_acc, r * (2 * NC) + (k - 1) * NC)
                        load(r * 2 + k, k)

            @block.tensor
            def _(pe):
                with pe.Fori(0, E // 2) as r:
                    for k in range(2):
                        pe.wait_ge(x_ld[k], r * 80 + 80)
                        for c in range(NC):
                            n = r * (2 * NC) + (k * NC + c)
                            pe.wait_ge(x_gelu, n * 4 + 1)
                            for b in range(4):
                                nc.tensor.matmul(ps[:, b, :], w1s[k][:, b * 128:(b + 1) * 128], h[:, c_of(c)],
                                                 start=True, stop=True).then_inc(x_h, 1)
                            if c % 2 == 0:
                                pe.wait_ge(x_t, n + 1)
                            for b in range(4):
                                pe.wait_ge(x_gelu, n * 4 + (b + 2))
                                mm = nc.tensor.matmul(ps[:, 4 + c, :], w2s[k][:, b, :], mid[:, b, :],
                                                      start=(b == 0), stop=(b == 3))
                            mm.then_inc(x_y, 1)

            @block.scalar
            def _(act):
                act.sem_inc(x_gelu, 1)
                with act.Fori(0, E // 2) as r:
                    for k in range(2):
                        act.wait_ge(x_ld[k], r * 80 + 80)
                        for c in range(NC):
                            n = r * (2 * NC) + (k * NC + c)
                            for b in range(4):
                                act.wait_ge(x_h, n * 4 + (b + 1))
                                nc.scalar.activation(mid[:, b, :], ps[:, b, :], ACT.Gelu, bias=b1x[k][:, b:b + 1])\
                                    .then_inc(x_gelu, 1)

            @block.vector
            def _(dve):
                dve.sem_inc(x_t, 1)
                with dve.Fori(0, E // 2) as r:
                    for k in range(2):
                        dve.wait_ge(x_ld[k], r * 80 + 80)
                        for c in range(NC):
                            n = r * (2 * NC) + (k * NC + c)
                            dve.wait_ge(x_y, n + 1)
                            nc.vector.scalar_tensor_tensor(tmp[:, c_of(c)], ps[:, 4 + c, :], b2x[k],
                                                           wbc[k][:, c_of(c)], ALU.add, ALU.mult).then_inc(x_t, 1)
                            dve.wait_ge(x_t, n + 2)
                            nc.vector.tensor_tensor(acc[:, c_of(c)], acc[:, c_of(c)], tmp[:, c_of(c)], ALU.add)\
                                .then_inc(x_acc, 1)

        if stop == 4:
            return dump(nc, sem, acc, out)

        n5 = Norm(4, lambda c: acc[:, c_of(c)], lambda c: f[0][:, c_of(c)], lambda c: f[1][:, c_of(c)],
                  lambda c: h[:, c_of(c)], meanM, 0)
        low = f[4]
        lowk = f[5]
        cosq, sinq = xT[:, 0:T], xT[:, T:2 * T]
        cosk, sink = osb[0:32, 0, :], osb[0:32, 1, :]
        qs5 = Split("tq", lambda c: f[2][:, c_of(c)], lambda p, c: partb[:, 0, p, c_of(c)], qd[1], 3, after=qs_)
        ks5 = Split("tk", lambda c: f[3][:, c_of(c)], lambda p, c: partb[:, 1, p, c_of(c)], kd[1], 5, rows=32, after=ks_)
        vst5 = fa[3].rearrange("p (g k w) -> p g k w", g=KVH * NB, k=KB)
        tw = vst[:, 0, 0:CH], vst[:, 1, 0:CH]
        ld5, lo5, lc5, hi5, ra5, rb5, rc5, v5, ve5, vs5, vo5 = (
            sem(f"s5_{n}") for n in ("ld", "low", "low_copied", "high", "cos", "sin", "kcos", "v", "v_ev",
                                     "v_stored", "v_ones"))
        lg5, ch5, mx5, ex5, pf5, tot5, w5r, w5t, w5c, w5s, lgc = (
            sem(f"r5_{n}") for n in ("logits", "chain", "less_max", "exp", "counts", "prefix", "weights",
                                     "turned", "copied", "stored", "logits_copied"))

        with nc.Block() as block:
            @block.sync
            def _(sp):
                sp.dma_start(cosq, t["rope"][:, 0, :]).then_inc(ld5, 16)
                sp.dma_start(sinq, t["rope"][:, 1, :]).then_inc(ld5, 16)
                sp.dma_start(cosk, t["ropek"][:, 0, :]).then_inc(ld5, 16)
                sp.dma_start(sink, t["ropek"][:, 1, :]).then_inc(ld5, 16)
                for c in range(NC):
                    split_store(sp, qs5, c)
                    split_store(sp, ks5, c)
                sp.wait_ge(ve5, NC * 4)
                sp.dma_start(vd[1].rearrange("b g p n -> p (b g) n"), vst5.rearrange("p g k w -> p g (k w)"))\
                    .then_inc(vs5, 16)
                sp.wait_ge(w5c, 1)
                sp.dma_start(wd[1].rearrange("e (t n) -> (e t) n", n=128), rt(11)).then_inc(w5s, 16)
                sp.wait_ge(w5s, 16)
                sp.wait_ge(vs5, 16)
                sp.wait_ge(qs5.stored, qs5.base_stored + 16 * qs5.copies * NC)
                sp.wait_ge(ks5.stored, ks5.base_stored + 16 * ks5.copies * NC)

            @block.gpsimd
            def _(pool):
                nc.gpsimd.memset(fa[3], 1.0).then_inc(vo5, 1)

            @block.scalar
            def _(act):
                norm_act(act, n5)
                for c in range(NC + 1):
                    if c < NC:
                        b = 4 * (c % 2)
                        act.wait_ge(lo5, c + 1)
                        nc.scalar.copy(low[0:QL, c_of(c)], ps[0:QL, b, :]).then_inc(lc5, 1)
                        nc.scalar.copy(lowk[0:KVL, c_of(c)], ps[0:KVL, b + 1, :]).then_inc(lc5, 1)
                    if c >= 1:
                        split_act(act, qs5, c - 1)
                        split_act(act, ks5, c - 1)
                act.wait_ge(mx5, 1)
                nc.scalar.activation(rt(5), rt(5), ACT.Exp).then_inc(ex5, 1)

            @block.vector
            def _(dve):
                norm_dve(dve, n5)
                dve.wait_ge(ld5, 64)
                dve.wait_ge(vo5, 1)
                for c in range(NC):
                    b = 4 * (c % 2)
                    cs, half = c_of(c), slice((c % 2) * CH, (c % 2 + 1) * CH)
                    dve.wait_ge(hi5, c + 1)
                    nc.vector.tensor_tensor(qs5.f(c), ps[:, b, :], cosq[:, half], ALU.mult).then_inc(ra5, 1)
                    nc.vector.tensor_tensor(tw[0], ps[:, b + 1, :], sinq[:, half], ALU.mult).then_inc(ra5, 1)
                    nc.vector.tensor_tensor(ks5.f(c)[0:32], ps[0:32, b + 2, :], cosk[:, half], ALU.mult)\
                        .then_inc(ra5, 1)
                    nc.vector.tensor_tensor(tw[1][0:32], ps[0:32, b + 3, :], sink[:, half], ALU.mult).then_inc(ra5, 1)
                    dve.wait_ge(ra5, 4 * (c + 1))
                    nc.vector.tensor_tensor(qs5.f(c), qs5.f(c), tw[0], ALU.add).then_inc(qs5.full, 1)
                    nc.vector.tensor_tensor(ks5.f(c)[0:32], ks5.f(c)[0:32], tw[1][0:32], ALU.add)\
                        .then_inc(ks5.full, 1)
                    split_dve(dve, qs5, c)
                    split_dve(dve, ks5, c)
                dve.wait_ge(v5, 1)
                for b in range(NB):
                    for k in range(KB):
                        nc.vector.tensor_copy(vst5[:, b * KVH:(b + 1) * KVH, k, 0:HD],
                                              ps[:, 6, (b * KB + k) * 32:(b * KB + k + 1) * 32]
                                              .rearrange("p (g d) -> p g d", g=KVH)).then_inc(ve5, 1)
                steps = [0]

                def step(ins):
                    steps[0] += 1
                    ins.then_inc(ch5, 1)
                    dve.wait_ge(ch5, steps[0])

                dve.wait_ge(lg5, 1)
                gate, one1, one2, eq, sc, ex = rt(0), rt(1), rt(2), rt(3), rt(4), rt(5)
                m1, m2, cm, sm = (rs(k) for k in range(4))
                step(nc.vector.tensor_copy(gate, ps[:, 7, 0:128]))
                step(nc.vector.tensor_reduce(m1, v3(gate), AX.X, ALU.max))
                nc.vector.tensor_tensor(v3(ex), v3(gate), wide(m1), ALU.subtract).then_inc(mx5, 1)
                dve.wait_ge(ex5, 1)
                step(nc.vector.tensor_reduce(sm, v3(ex), AX.X, ALU.add))
                step(nc.vector.reciprocal(sm, sm))
                step(nc.vector.tensor_tensor(v3(gate), v3(ex), wide(sm), ALU.mult))
                top_one(step, gate, one1, m1, eq, sc, cm)
                step(nc.vector.scalar_tensor_tensor(ex, one1, -2.0, gate, ALU.mult, ALU.add))
                top_one(step, ex, one2, m2, eq, sc, cm)
                picked, run, run2 = rt(6), rt(7), rt(8)
                step(nc.vector.tensor_tensor(picked, one1, one2, ALU.add))
                step(nc.vector.memset(run, 0.0))
                step(nc.vector.tensor_copy(run[:, E:128], picked[:, 0:128 - E]))
                src, dst = run, run2
                for k in (1, 2, 4, 8):
                    step(nc.vector.tensor_copy(dst[:, 0:k * E], src[:, 0:k * E]))
                    step(nc.vector.tensor_tensor(dst[:, k * E:128], src[:, k * E:128], src[:, 0:128 - k * E], ALU.add))
                    src, dst = dst, src
                nc.vector.tensor_scalar(src, src, 1.0, None, ALU.mult).then_inc(pf5, 1)
                dve.wait_ge(tot5, 1)
                step(nc.vector.tensor_scalar(eq, ps[:, 7, 128:256], CAP, None, ALU.is_le))
                step(nc.vector.tensor_tensor(picked, picked, eq, ALU.mult))
                step(nc.vector.tensor_tensor(gate, gate, picked, ALU.mult))
                step(nc.vector.tensor_reduce(sm, v3(gate), AX.X, ALU.add))
                step(nc.vector.tensor_scalar(sm, sm, 1e-6, None, ALU.add))
                step(nc.vector.reciprocal(sm, sm))
                nc.vector.tensor_tensor(rt(10).rearrange("p (e t) -> p t e", t=TB), v3(gate), wide(sm), ALU.mult)\
                    .then_inc(w5r, 1)
                dve.wait_ge(w5t, 1)
                nc.vector.tensor_copy(rt(11), ps[:, 7, 256:384]).then_inc(w5c, 1)

            @block.tensor
            def _(pe):
                norm_pe(pe, n5)
                pe.wait_ge(s_std, n5.base + NC)
                for c in range(NC):
                    b = 4 * (c % 2)
                    pe.wait_ge(s_normed, n5.base + c + 1)
                    if c >= 2:
                        pe.wait_ge(ra5, 4 * (c - 1))
                    nc.tensor.matmul(ps[0:QL, b, :], wl1[:, 0:64], h[:, c_of(c)], start=True, stop=True)
                    nc.tensor.matmul(ps[0:KVL, b + 1, :], wl1[:, 320:352], h[:, c_of(c)], start=True, stop=True)\
                        .then_inc(lo5, 1)
                    pe.wait_ge(lc5, 2 * (c + 1))
                    ql, kl = low[0:QL, c_of(c)], lowk[0:KVL, c_of(c)]
                    nc.tensor.matmul(ps[:, b, :], wl1[0:QL, 64:192], ql, start=True, stop=True)
                    nc.tensor.matmul(ps[:, b + 1, :], wl1[0:QL, 192:320], ql, start=True, stop=True)
                    nc.tensor.matmul(ps[0:32, b + 2, :], wl1[0:KVL, 352:384], kl, start=True, stop=True)
                    nc.tensor.matmul(ps[0:32, b + 3, :], wl1[0:KVL, 384:416], kl, start=True, stop=True)\
                        .then_inc(hi5, 1)
                pe.wait_ge(ra5, 4 * NC)
                for tb in range(TB):
                    mm = nc.tensor.matmul(ps[:, 6, tb * 32:(tb + 1) * 32], lowk[0:KVL, tb * 128:(tb + 1) * 128],
                                          wl1[0:KVL, 416:448], start=True, stop=True)
                mm.then_inc(v5, 1)
                for tb in range(TB):
                    mm = nc.tensor.matmul(ps[:, 7, tb * E:(tb + 1) * E], h[:, tb * 128:(tb + 1) * 128],
                                          wl1[:, 576:584], start=True, stop=True)
                mm.then_inc(lg5, 1)
                pe.wait_ge(pf5, 1)
                nc.tensor.matmul(ps[:, 7, 128:256], tri, rt(6), start=True, stop=False, skip_group_check=True)
                nc.tensor.matmul(ps[:, 7, 128:256], ones, rt(7), start=False, stop=True, skip_group_check=True)\
                    .then_inc(tot5, 1)
                pe.wait_ge(w5r, 1)
                nc.tensor.transpose(ps[:, 7, 256:384], rt(10), ident).then_inc(w5t, 1)

        if stop == 5:
            return dump(nc, sem, h, out)

        attention(1, 1, 1)
        if stop == 6:
            return dump_yd(nc, sem, yd[1], pool_a, out)

        hidden = [fa[0], fa[1]]
        y7, w7 = f[2], f[3]
        wds = [f[5][:, k * 256:(k + 1) * 256].rearrange("p (k n) -> p k n", k=2) for k in range(2)]
        ld_y7 = [sem(f"ld7_y{b}") for b in range(NB)]
        z_ld, z_h, z_silu, z_rl, z_yn, z_wo, z_a, z_y, z_t, z_acc, z_out = (
            [sem("z_ld0"), sem("z_ld1")], sem("z_h"), sem("z_silu"), sem("z_recip"), sem("z_yn"), sem("z_wo"),
            sem("z_att"), sem("z_y"), sem("z_tmp"), sem("z_acc"), sem("z_out"))

        with nc.Block() as block:
            @block.sync
            def _(sp):
                def load(e, k):
                    sp.dma_start(wds[k], t["wdn"][bass.ds(e, 1)].rearrange("o p k n -> (o p) k n"))\
                        .then_inc(z_ld[k], 16)
                    sp.dma_start(wbc[k], wd[1][bass.ds(e, 1)].rearrange("o n -> (o n)").partition_broadcast(128))\
                        .then_inc(z_ld[k], 16)
                for b in range(NB):
                    for k, dst in enumerate((y7, w7)):
                        sp.dma_start(dst[:, b * T:(b + 1) * T], yd[1][b, :, k]).then_inc(ld_y7[b], 16)
                load(0, 0)
                load(1, 1)
                with sp.Fori(1, E // 2) as r:
                    for k in range(2):
                        sp.wait_ge(z_acc, r * (2 * NC) + (k - 1) * NC)
                        load(r * 2 + k, k)
                for c in range(NC):
                    sp.wait_ge(z_acc, NC * (E - 1) + c + 1)
                    sp.dma_start(out[:, c_of(c)], acc[:, c_of(c)]).then_inc(z_out, 16)
                sp.wait_ge(z_out, 16 * NC)

            @block.scalar
            def _(act):
                for c in range(NC):
                    for b in range(2):
                        act.wait_ge(z_h, 2 * c + b + 1)
                        nc.scalar.activation(hidden[b][:, c_of(c)], ps[:, 2 * (c % 2) + b, :], ACT.Silu)\
                            .then_inc(z_silu, 1)

            @block.vector
            def _(dve):
                dve.sem_inc(z_t, 1)
                for c in range(NC):
                    dve.wait_ge(ld_y7[c // 2], 32)
                    nc.vector.reciprocal(w7[:, c_of(c)], w7[:, c_of(c)]).then_inc(z_rl, 1)
                    dve.wait_ge(z_rl, c + 1)
                    nc.vector.tensor_tensor(y7[:, c_of(c)], y7[:, c_of(c)], w7[:, c_of(c)], ALU.mult)\
                        .then_inc(z_yn, 1)
                for c in range(NC):
                    dve.wait_ge(z_wo, c + 1)
                    nc.vector.scalar_tensor_tensor(acc[:, c_of(c)], ps[:, 4 + c, :], col("bout"), acc[:, c_of(c)],
                                                   ALU.add, ALU.add).then_inc(z_a, 1)
                dve.wait_ge(z_a, NC)
                with dve.Fori(0, E // 2) as r:
                    for k in range(2):
                        dve.wait_ge(z_ld[k], r * 32 + 32)
                        for c in range(NC):
                            n = r * (2 * NC) + (k * NC + c)
                            dve.wait_ge(z_y, n + 1)
                            nc.vector.tensor_tensor(tmp[:, c_of(c)], ps[:, 4 + c, :], wbc[k][:, c_of(c)], ALU.mult)\
                                .then_inc(z_t, 1)
                            dve.wait_ge(z_t, n + 2)
                            nc.vector.tensor_tensor(acc[:, c_of(c)], acc[:, c_of(c)], tmp[:, c_of(c)], ALU.add)\
                                .then_inc(z_acc, 1)

            @block.tensor
            def _(pe):
                for c in range(NC):
                    if c >= 2:
                        pe.wait_ge(z_silu, 2 * (c - 1))
                    for b in range(2):
                        nc.tensor.matmul(ps[:, 2 * (c % 2) + b, :], wl1[:, 584 + b * 128:584 + (b + 1) * 128],
                                         h[:, c_of(c)], start=True, stop=True).then_inc(z_h, 1)
                for c in range(NC):
                    pe.wait_ge(z_yn, c + 1)
                    nc.tensor.matmul(ps[:, 4 + c, :], wl1[:, 448:576], y7[:, c_of(c)], start=True, stop=True)\
                        .then_inc(z_wo, 1)
                pe.wait_ge(z_a, NC)
                pe.wait_ge(z_silu, 2 * NC)
                with pe.Fori(0, E // 2) as r:
                    for k in range(2):
                        pe.wait_ge(z_ld[k], r * 32 + 32)
                        for c in range(NC):
                            n = r * (2 * NC) + (k * NC + c)
                            if c % 2 == 0:
                                pe.wait_ge(z_t, n + 1)
                            for b in range(2):
                                mm = nc.tensor.matmul(ps[:, 4 + c, :], wds[k][:, b, :], hidden[b][:, c_of(c)],
                                                      start=(b == 0), stop=(b == 1))
                            mm.then_inc(z_y, 1)


def dump(nc, sem, tensor, out):
    done = sem("dumped")
    with nc.Block() as block:
        @block.sync
        def _(sp):
            sp.dma_start(out, tensor[:, :]).then_inc(done, 16)
            sp.wait_ge(done, 16)


def dump_yd(nc, sem, yd, buf, out):
    ld, done, rc, ml = sem("dump_ld"), sem("dumped"), sem("dump_r"), sem("dump_m")
    with nc.Block() as block:
        @block.sync
        def _(sp):
            for b in range(NB):
                for k in range(2):
                    o = (2 * b + k) * T
                    sp.dma_start(buf[:, o:o + T], yd[b, :, k]).then_inc(ld, 16)
            sp.wait_ge(ml, 2)
            for b in range(NB):
                sp.dma_start(out[:, b * T:(b + 1) * T], buf[:, 2 * b * T:(2 * b + 1) * T]).then_inc(done, 16)
            sp.wait_ge(done, 32)

        @block.vector
        def _(dve):
            dve.wait_ge(ld, 64)
            for b in range(NB):
                y, w = buf[:, 2 * b * T:(2 * b + 1) * T], buf[:, (2 * b + 1) * T:(2 * b + 2) * T]
                nc.vector.reciprocal(w, w).then_inc(rc, 1)
                dve.wait_ge(rc, b + 1)
                nc.vector.tensor_tensor(y, y, w, ALU.mult).then_inc(ml, 1)


def kernel(**inputs):
    import numpy as _np
    import concourse.bacc as _bacc
    from concourse import mybir as _mybir
    from concourse.bass_utils import run_bass_kernel_spmd as _run

    a = {k: _np.asarray(v) for k, v in inputs.items()}
    f = _np.float32

    def stack(mats):
        return _np.ascontiguousarray(_np.stack(mats, axis=1))

    swap = _np.arange(128) ^ 1
    kv = a["L1_attn_Wkvb"].reshape(KVL, KVH * HD, 2)
    wl1 = _np.zeros((128, 848), f)
    wl1[:, 0:64] = a["L1_attn_Wqa"]
    wl1[0:QL, 64:192] = a["L1_attn_Wqb"]
    wl1[0:QL, 192:320] = a["L1_attn_Wqb"][:, swap]
    wl1[:, 320:352] = a["L1_attn_Wkva"]
    wl1[0:KVL, 352:384] = kv[:, :, 0]
    wl1[0:KVL, 384:416] = kv[:, swap[0:32], 0]
    wl1[0:KVL, 416:448] = kv[:, :, 1]
    wl1[:, 448:576] = a["L1_attn_Wout"]
    wl1[:, 576:584] = a["L1_ffn_w_router"].T
    wl1[:, 584:840] = a["L1_ffn_w_gate"].T
    wl1[:, 840:848] = a["L0_ffn_gate_W"]
    i = _np.arange(128)
    head = (i[:, None] // HD == i[None, :] // HD).astype(f) / f(HD)
    cst = stack([_np.full((128, 128), 1.0 / 128, f), head, _np.eye(128, dtype=f),
                 (i[:, None] <= i[None, :]).astype(f), _np.ones((128, 128), f)])
    mask = _np.where(i[None, :] > i[:, None], f(NEG), f(0.0)).astype(f)
    inv = (f(1.0) / f(10000.0) ** (_np.arange(0, HD, 2, dtype=f) / f(HD))).astype(f)
    ang = (_np.arange(T, dtype=f)[None, :] * inv[(i % HD) // 2][:, None]).astype(f).astype(_np.float64)
    cos, sin = _np.cos(ang), _np.sin(ang) * _np.where(i % 2 == 0, -1.0, 1.0)[:, None]
    rope = stack([(cos * SCALE).astype(f), (sin * SCALE).astype(f)])
    ropek = stack([cos.astype(f)[0:32], sin.astype(f)[0:32]])
    column = {"mg": "L0_attn_mg", "mr": "L0_attn_mr", "mk": "L0_attn_mk", "mv": "L0_attn_mv",
              "bg": "L0_attn_Wg_b", "br": "L0_attn_Wr_b", "bk": "L0_attn_Wk_b", "bv": "L0_attn_Wv_b",
              "bo": "L0_attn_Wo_b", "w": "L0_attn_w", "u": "L0_attn_u", "ln1g": "L0_ffn_ln1_g",
              "ln1b": "L0_ffn_ln1_b", "ln2g": "L0_ffn_ln2_g", "ln2b": "L0_ffn_ln2_b", "bq": "L0_ffn_bq",
              "bkf": "L0_ffn_bk", "bp": "L0_ffn_bp", "bout": "L1_attn_bout"}
    arrays = {
        "xT": _np.ascontiguousarray(a["L0_attn_x"].reshape(N, D).T),
        "cols": _np.ascontiguousarray(_np.stack([a[column[n]].reshape(128) for n in COLS], axis=1)),
        "wl0": stack([a[f"L0_attn_W{n}_w"].T for n in "grkvo"]),
        "wf": stack([a[f"L0_ffn_W{n}"] for n in "qkvp"]),
        "wl1": wl1, "cst": cst, "mask": stack([mask, mask.T]), "rope": rope, "ropek": ropek,
        "bv": a["L0_ffn_bv"], "gate_b": a["L0_ffn_gate_b"], "rev": (E - _np.arange(E)).astype(f),
        "w1": a["L0_ffn_exp_W1"],
        "w2": _np.ascontiguousarray(a["L0_ffn_exp_W2"].reshape(E, 4, 128, 128).transpose(0, 2, 1, 3)),
        "b1": _np.ascontiguousarray(a["L0_ffn_exp_b1"].reshape(E, 4, 128).transpose(0, 2, 1)),
        "b2": _np.ascontiguousarray(a["L0_ffn_exp_b2"].reshape(E, 128, 1)),
        "wdn": _np.ascontiguousarray(a["L1_ffn_w_down"].transpose(0, 2, 1).reshape(E, 2, 128, 128)
                                     .transpose(0, 2, 1, 3)),
    }
    nc = _bacc.Bacc("TRN2", target_bir_lowering=False, num_devices=1)
    t = {n: nc.dram_tensor(f"in_{n}", v.shape, _mybir.dt.from_np(v.dtype), kind="ExternalInput").ap()
         for n, v in arrays.items()}
    out = nc.dram_tensor("out_T", (128, N), F32, kind="ExternalOutput").ap()
    build_program(nc, t, out)
    r = _run(nc, [{f"in_{n}": v for n, v in arrays.items()}], core_ids=[0])
    return _np.ascontiguousarray(r.results[0]["out_T"].T).reshape(NB, T, D)
```

```python
from contextlib import ExitStack

import numpy as np

import concourse.bass as bass
from concourse import mybir

F32 = mybir.dt.float32
BF16 = mybir.dt.bfloat16
ACT = mybir.ActivationFunctionType
ALU = mybir.AluOpType
AX = mybir.AxisListType

D = 128
NB, T = 2, 1024
N = NB * T
CH = 512
NC = N // CH
TB = N // 128
KB = T // 128
H, HD = 16, 8
G = 4
E = 8
HID0, HID1 = 512, 256
CAP = 320.0
KVH = 4
QL, KVL = 64, 32
PARTS = 3
ROWS = PARTS * PARTS * HD
MROWS = ROWS + PARTS
EPS = 1e-5
NEG = -1e30
SCALE = HD ** -0.5

LOG_EXP = "natural_log_exp_and_others"

COLS = ["mg", "mr", "mk", "mv", "bg", "br", "bk", "bv", "bo", "w", "u", "ln1g", "ln1b", "ln2g", "ln2b",
        "bq", "bkf", "bp", "bout"]
COL = {n: i for i, n in enumerate(COLS)}


def build_program(nc, t, out, stop=99):
    ctx = ExitStack()
    with ctx:
        def sb(name, shape, dt=F32):
            return ctx.enter_context(nc.sbuf_tensor(name, shape, dt))

        def sem(name):
            return ctx.enter_context(nc.semaphore(name))

        ps = ctx.enter_context(nc.psum_tensor("ps", [128, 8, CH], F32))

        xT = sb("xT", [128, N])
        xn = sb("xn", [128, N])
        xs = sb("xs", [128, N])
        spare = sb("spare", [128, N])
        acc = sb("acc", [128, N])
        cols = sb("cols", [128, len(COLS)])
        wl0 = sb("wl0", [128, 5, 128])
        wf = sb("wf", [128, 4, 128])
        cst = sb("cst", [128, 5, 128])
        idb = sb("idb", [128, 128], BF16)
        mskb = sb("mskb", [128, 2, 128], BF16)
        eps = sb("eps", [128, 1])
        pool_a = sb("pool_a", [128, 8192])
        shortp = sb("shortp", [128, 4096])
        pool_b = sb("pool_b", [128, 12288])
        vst = sb("vst", [128, 3, KB * G * 32])
        osb = sb("osb", [128, 3, T])
        small = sb("small", [128, 1024])
        wl1 = sb("wl1", [128, 848])
        h = sb("h", [128, N])

        meanM, headM, ident, tri, ones = (cst[:, i, :] for i in range(5))

        def dram(name, shape, dt=F32):
            return nc.dram_tensor(name, shape, dt, kind="Internal").ap()
        qd = [dram(f"qd{l}", [NB, H, PARTS, HD, T], BF16) for l in range(2)]
        kd = [dram("kd0", [NB, H, PARTS, HD, T], BF16), dram("kd1", [NB, KVH, PARTS, HD, T], BF16)]
        yd = [dram(f"yd{l}", [NB, H, 2, HD, T]) for l in range(2)]
        wd = [dram(f"wd{l}", [E, N]) for l in range(2)]

        def c_of(c):
            return slice(c * CH, (c + 1) * CH)

        def full(buf, k):
            return buf[:, k * N:(k + 1) * N]

        def xn_chunk(c):
            return xn[:, c_of(c)]

        def col(name):
            return cols[:, COL[name]:COL[name] + 1]

        s_mean, s_cent, s_sq, s_var, s_log, s_inv, s_normed, s_scaled = (
            sem(f"norm_{n}") for n in ("mean", "centred", "squared", "variance", "log_variance", "inverse", "done",
                                       "scaled"))

        class Norm:
            def __init__(self, k, src, cen, sq, dst, matrix, banks, gain=None, bias=None, scaled=0):
                self.base = NC * k
                self.scaled = NC * scaled
                self.src, self.cen, self.sq, self.dst, self.matrix = src, cen, sq, dst, matrix
                self.banks, self.gain, self.bias = banks, gain, bias

        def norm_pe(pe, L, ready=None):
            for c in range(NC):
                if ready is not None:
                    pe.wait_ge(ready, c + 1)
                if c >= 2:
                    pe.wait_ge(s_cent, L.base + c - 1)
                nc.tensor.matmul(ps[:, L.banks + c % 2, :], L.matrix, L.src(c), start=True, stop=True)\
                    .then_inc(s_mean, 1)
            for c in range(NC):
                pe.wait_ge(s_sq, L.base + c + 1)
                if c >= 2:
                    pe.wait_ge(s_log, L.base + c - 1)
                nc.tensor.matmul(ps[:, L.banks + 2 + c % 2, :], L.matrix, L.sq(c), start=True, stop=True)\
                    .then_inc(s_var, 1)

        def norm_dve(dve, L):
            for c in range(NC):
                dve.wait_ge(s_mean, L.base + c + 1)
                nc.vector.tensor_tensor(L.cen(c), L.src(c), ps[:, L.banks + c % 2, :], ALU.subtract)\
                    .then_inc(s_cent, 1)
            for c in range(NC):
                dve.wait_ge(s_inv, L.base + c + 1)
                if L.gain is None:
                    nc.vector.tensor_tensor(L.dst(c), L.cen(c), L.sq(c), ALU.mult).then_inc(s_normed, 1)
                else:
                    nc.vector.scalar_tensor_tensor(L.dst(c), L.cen(c), L.gain, L.sq(c), ALU.mult, ALU.mult)\
                        .then_inc(s_scaled, 1)
                    dve.wait_ge(s_scaled, L.scaled + c + 1)
                    nc.vector.tensor_scalar(L.dst(c), L.dst(c), L.bias, None, ALU.add).then_inc(s_normed, 1)

        def norm_act(act, L):
            for c in range(NC):
                act.wait_ge(s_cent, L.base + c + 1)
                nc.scalar.activation(L.sq(c), L.cen(c), ACT.Square).then_inc(s_sq, 1)
            for c in range(NC + 1):
                if c < NC:
                    act.wait_ge(s_var, L.base + c + 1)
                    nc.scalar.activation(L.sq(c), ps[:, L.banks + 2 + c % 2, :], ACT.Ln, bias=eps[:, 0:1])\
                        .then_inc(s_log, 1)
                if c >= 1:
                    act.wait_ge(s_log, L.base + c)
                    nc.scalar.activation(L.sq(c - 1), L.sq(c - 1), ACT.Exp, scale=-0.5).then_inc(s_inv, 1)

        class Split:
            def __init__(self, name, f, parts, dst, after=None):
                self.f, self.parts, self.dst = f, parts, dst
                self.base, self.base_stored = (NC, 16 * PARTS * NC) if after else (0, 0)
                self.full, self.hi, self.r1, self.mid, self.lo, self.stored = (
                    (after.full, after.hi, after.r1, after.mid, after.lo, after.stored) if after else
                    (sem(f"{name}_{s}") for s in ("full", "hi", "r1", "mid", "lo", "stored")))

        def remainder(dve, S, c):
            dve.wait_ge(S.hi, S.base + c + 1)
            nc.vector.tensor_tensor(S.f(c), S.f(c), S.parts(0, c), ALU.subtract).then_inc(S.r1, 1)

        def last_part(dve, S, c):
            dve.wait_ge(S.mid, S.base + c + 1)
            nc.vector.tensor_tensor(S.parts(2, c), S.f(c), S.parts(1, c), ALU.subtract).then_inc(S.lo, 1)

        def first_part(act, S, c):
            act.wait_ge(S.full, S.base + c + 1)
            nc.scalar.copy(S.parts(0, c), S.f(c)).then_inc(S.hi, 1)

        def second_part(act, S, c):
            act.wait_ge(S.r1, S.base + c + 1)
            nc.scalar.copy(S.parts(1, c), S.f(c)).then_inc(S.mid, 1)

        def split_store(sp, S, c):
            sp.wait_ge(S.lo, S.base + c + 1)
            half = slice((c % 2) * CH, (c % 2 + 1) * CH)
            for p in range(PARTS):
                sp.dma_start(S.dst[c // 2, :, p, :, half], S.parts(p, c)).then_inc(S.stored, 16)

        f = [full(pool_b, k) for k in range(6)]
        fa = [full(pool_a, k) for k in range(4)]
        k_ones = sem("k_ones")
        shifted = sem("shifted")
        n0 = Norm(0, lambda c: xT[:, c_of(c)], lambda c: f[0][:, c_of(c)], lambda c: f[1][:, c_of(c)],
                  xn_chunk, meanM, 0)
        n1 = Norm(1, xn_chunk, lambda c: f[0][:, c_of(c)], lambda c: f[1][:, c_of(c)],
                  lambda c: h[:, c_of(c)], meanM, 0, gain=col("ln1g"), bias=col("ln1b"), scaled=0)
        partb = pool_a[:, 0:PARTS * N].bitcast(BF16).rearrange("p (k a n) -> p k a n", k=2, a=PARTS)
        qs_ = Split("sq", lambda c: f[2][:, c_of(c)], lambda p, c: partb[:, 0, p, c_of(c)], qd[0])
        ks_ = Split("sk", lambda c: fa[3][:, c_of(c)], lambda p, c: partb[:, 1, p, c_of(c)], kd[0])
        bvb, gbb, rev = small[:, 0:128], small[:, 128:136], small[:, 136:144]
        dec, hbg = small[:, 144:146], small[:, 146:147]
        msk32 = osb[:, 1, 0:256].rearrange("p (k n) -> p k n", k=2)

        ld_x, ld_w, one_eps = sem("ld_x"), sem("ld_w"), sem("eps_set")
        NLD = 9
        qk_mm, v_mm, v_ev, castd = (sem(n) for n in ("qk_mm", "v_mm", "v_ev", "const_cast"))
        v_ones = sem("v_ones")
        home0 = acc[:, :].rearrange("p (b g k x) -> p b g k x", b=NB, g=G, k=KB)

        with nc.Block() as block:
            @block.sync
            def _(sp):
                for c in range(NC):
                    sp.dma_start(xT[:, c_of(c)], t["xT"][:, c_of(c)]).then_inc(ld_x, 16)
                sp.dma_start(wf[:, :, :], t["wf"]).then_inc(ld_w, 16)
                sp.dma_start(bvb, t["bv"].partition_broadcast(128)).then_inc(ld_w, 16)
                sp.dma_start(gbb, t["gate_b"].partition_broadcast(128)).then_inc(ld_w, 16)
                sp.dma_start(rev, t["rev"].partition_broadcast(128)).then_inc(ld_w, 16)
                for c in range(NC):
                    split_store(sp, qs_, c)
                    split_store(sp, ks_, c)
                sp.wait_ge(qs_.stored, 16 * PARTS * NC)
                sp.wait_ge(ks_.stored, 16 * PARTS * NC)

            @block.gpsimd
            def _(pool):
                nc.gpsimd.memset(vst[:, :, :], 1.0).then_inc(v_ones, 1)
                pool.wait_ge(v_ones, 1)
                nc.gpsimd.memset(pool_b[64:MROWS, 6144:12288].bitcast(BF16), 1.0).then_inc(v_ones, 1)

            @block.scalar
            def _(act):
                act.dma_start(cst[:, :, :], t["cst"]).then_inc(ld_w, 16)
                act.dma_start(cols[:, :], t["cols"]).then_inc(ld_w, 16)
                act.dma_start(wl0[:, :, :], t["wl0"]).then_inc(ld_w, 16)
                act.dma_start(wl1[:, :], t["wl1"]).then_inc(ld_w, 16)
                act.dma_start(msk32, t["mask"]).then_inc(ld_w, 16)
                nc.scalar.preload_act_table_set(LOG_EXP)
                act.wait_ge(ld_w, 16 * NLD)
                act.wait_ge(one_eps, 1)
                norm_act(act, n0)
                norm_act(act, n1)
                for c in range(NC):
                    act.wait_ge(qk_mm, c + 1)
                    nc.scalar.activation(ks_.f(c), ps[:, 2 * (c % 2) + 1, :], ACT.Identity, bias=col("bkf"))\
                        .then_inc(ks_.full, 1)
                    for part in (first_part, second_part):
                        for S in (qs_, ks_):
                            part(act, S, c)

            @block.vector
            def _(dve):
                nc.vector.memset(eps[:, :], EPS).then_inc(one_eps, 1)
                dve.wait_ge(ld_w, 16 * NLD)
                nc.vector.tensor_copy(idb[:, :], ident).then_inc(castd, 1)
                nc.vector.tensor_copy(mskb[:, :, :], msk32).then_inc(castd, 1)
                norm_dve(dve, n0)
                norm_dve(dve, n1)
                for c in range(NC):
                    b = 2 * (c % 2)
                    dve.wait_ge(qk_mm, c + 1)
                    nc.vector.tensor_scalar(qs_.f(c), ps[:, b, :], col("bq"), SCALE, ALU.add, ALU.mult)\
                        .then_inc(qs_.full, 1)
                    remainder(dve, qs_, c)
                    remainder(dve, ks_, c)
                    dve.wait_ge(v_mm, c + 1)
                    nc.vector.tensor_tensor(home0[:, c // 2, :, 4 * (c % 2):4 * (c % 2 + 1), :],
                                            ps[:, 4 + c, :].rearrange("p (k g x) -> p g k x", k=4, g=G),
                                            bvb.rearrange("p (g x) -> p g x", g=G).unsqueeze(2)
                                            .to_broadcast([128, G, 4, 32]), ALU.add).then_inc(v_ev, 1)
                    last_part(dve, qs_, c)
                    last_part(dve, ks_, c)

            @block.tensor
            def _(pe):
                pe.wait_ge(ld_w, 16 * NLD)
                pe.wait_ge(ld_x, 16 * NC)
                norm_pe(pe, n0)
                pe.wait_ge(s_log, n0.base + NC)
                norm_pe(pe, n1, ready=s_normed)
                pe.wait_ge(s_log, n1.base + NC)
                for c in range(NC):
                    b = 2 * (c % 2)
                    pe.wait_ge(s_normed, n1.base + c + 1)
                    if c >= 2:
                        pe.wait_ge(ks_.full, c - 1)
                        pe.wait_ge(qs_.full, c - 1)
                    for j in range(2):
                        ins = nc.tensor.matmul(ps[:, b + j, :], wf[:, j, :], h[:, c_of(c)], start=True, stop=True)
                    ins.then_inc(qk_mm, 1)
                    for k in range(4):
                        tb = 4 * c + k
                        ins = nc.tensor.matmul(ps[:, 4 + c, k * 128:(k + 1) * 128], h[:, tb * 128:(tb + 1) * 128],
                                               wf[:, 2, :], start=True, stop=True)
                    ins.then_inc(v_mm, 1)

        if stop == 1:
            return dump(nc, sem, acc, out)


        def sums(b):
            buf = (h[:, :], fa[0])[b]
            return buf[:, 0:T], buf[:, T:2 * T]

        ld_y = [[sem(f"ld_y{l}{b}") for b in range(NB)] for l in range(2)]

        def load_sums(sp, l, b):
            for k, dst in enumerate(sums(b)):
                sp.dma_start(dst, yd[l][b, :, k]).then_inc(ld_y[l][b], 16)

        def sums_chunk(c, k):
            return sums(c // 2)[k][:, (c % 2) * CH:(c % 2 + 1) * CH]

        def attention(l, kh, vw, home, beside=None):
            ROLL = 3
            UNITS = NB * G
            qst = pool_b[:, 0:6144].bitcast(BF16).rearrange("p (s i n) -> p s i n", s=ROLL, i=G)
            kst = pool_b[:, 6144:12288].bitcast(BF16).rearrange("p (s i n) -> p s i n", s=ROLL, i=G)
            prob = (pool_a[:, :].rearrange("p (s i n) -> p s i n", s=2, i=G),
                    shortp[:, :].rearrange("p (s i n) -> p s i n", s=2, i=G))
            vals = vst[:, :, 0:KB * vw * 32].rearrange("p s (k i w) -> p s k i w", k=KB, i=vw)
            lowmax = small[:, 256:288]
            highmax = small[:, 288:304]
            rem = small[:, 304:336]
            mpart = small[:, 336:384].bitcast(BF16).rearrange("p (a c) -> p a c", a=PARTS)
            mT = small[:, 384:576].bitcast(BF16).rearrange("p (s n) -> p s n", s=ROLL)
            turned = ps[:, 6, 0:64].bitcast(BF16)
            s = {n: sem(f"a{l}_{n}") for n in (
                "a_mm", "a_red", "folded", "hi", "r1", "mid", "parts", "turned", "m_copied",
                "m_set0", "m_set1", "m_set2", "v_set", "b_mm", "exp", "pv", "evac",
                "st0", "st1", "st2", "ld0", "ld1", "ld2")}
            TILES = [(i, qb, hf) for i in range(G) for qb in range(KB) for hf in range(1 + qb // 4)]
            NT = len(TILES)
            A_BANKS = (3, 6, 7)
            RING = len(A_BANKS)
            NP = KB // 2
            NE = KB * G
            A_STEPS = 14
            PV0, EXP0, EVAC0, RED0 = 4, 2, 1, 3
            NH = NT // G
            BLOCKS = [(PARTS * HD * j, j, PARTS - j) for j in range(PARTS)] + \
                     [(PARTS * HD * j + HD * (PARTS - j), 0, j) for j in range(1, PARTS)]
            NLOAD = PARTS + len(BLOCKS)
            PEEL = UNITS // ROLL * ROLL

            def all_units(eng, body):
                with eng.Fori(0, UNITS // ROLL) as r:
                    for k in range(ROLL):
                        body(r * ROLL + k, k, r, False)
                for k in range(UNITS - PEEL):
                    body(PEEL + k, k, UNITS // ROLL, k == UNITS - PEEL - 1)

            with nc.Block() as block:
                @block.sync
                def _(sp):
                    qrows = qd[l].rearrange("b h a d n -> (b h a d) n")
                    krows = kd[l].rearrange("b h a d n -> (b h a d) n")
                    yrows = yd[l].rearrange("b h k d n -> (b h k d) n")

                    def load(u, slot):
                        for j in range(PARTS):
                            r = PARTS * HD * j
                            sp.dma_start(qst[r:r + PARTS * HD, slot],
                                         qrows[bass.ds(u * (G * PARTS * HD), G * PARTS * HD), :]
                                         .rearrange("(i x) n -> x i n", i=G)).then_inc(s[f"ld{slot}"], 16)
                        for r, part, parts in BLOCKS:
                            sp.dma_start(kst[r:r + parts * HD, slot, 0:kh],
                                         krows[bass.ds(u * (kh * PARTS * HD), kh * PARTS * HD), :]
                                         .rearrange("(i x) n -> x i n", i=kh)[HD * part:HD * (part + parts)])\
                                .then_inc(s[f"ld{slot}"], 16)

                    def set_max(u, slot):
                        sp.wait_ge(s["m_copied"], u + 1)
                        sp.dma_start(qst[ROWS:MROWS, slot].rearrange("a i n -> a (i n)"), mT[0:96, slot, :])\
                            .then_inc(s[f"m_set{slot}"], 16)

                    for k in range(ROLL):
                        sp.sem_inc(s[f"st{k}"], 16)
                    if l == 1:
                        sp.wait_ge(k_ones, 1)
                    load(0, 0)
                    load(1, 1)
                    if beside:
                        beside.sync(sp)
                    set_max(0, 0)

                    def body(u, slot, r, last):
                        if not isinstance(u, int):
                            sp.wait_ge(s["pv"], u * KB + PV0)
                            load(u + 2, (slot + 2) % ROLL)
                        if not last:
                            set_max(u + 1, (slot + 1) % ROLL)
                        if last:
                            for k in range(ROLL):
                                sp.wait_ge(s[f"st{k}"], 16 + 16 * G * ((G - k + ROLL - 1) // ROLL))
                            load_sums(sp, l, 0)
                        sp.wait_ge(s["evac"], u + (EVAC0 + 1))
                        for i in range(G):
                            sp.dma_start(yrows[bass.ds(u * (G * 2 * HD) + i * 2 * HD, 2 * HD), :],
                                         osb[32 * i:32 * i + 2 * HD, slot, :]).then_inc(s[f"st{slot}"], 16)
                    all_units(sp, body)
                    for k in range(ROLL):
                        sp.wait_ge(s[f"st{k}"], 16 + 16 * G * ((UNITS - k + ROLL - 1) // ROLL))

                @block.gpsimd
                def _(pool):
                    if l == 0:
                        for b in range(NB):
                            o = b * T
                            nc.gpsimd.tensor_copy(xs[:, o + 1:o + T], xn[:, o:o + T - 1]).then_inc(shifted, 1)
                            pool.wait_ge(shifted, 2 * b + 1)
                            nc.gpsimd.tensor_copy(xs[:, o:o + 1], xn[:, o + T - 1:o + T]).then_inc(shifted, 1)
                            pool.wait_ge(shifted, 2 * b + 2)

                    if beside:
                        beside.pool(pool)

                @block.scalar
                def _(act):
                    if beside:
                        beside.act(act)
                    nc.scalar.preload_act_table_set(LOG_EXP)
                    act.sem_inc(s["exp"], EXP0)

                    def set_values(u, slot):
                        n = KB * vw
                        nc.scalar.copy(vst[:, slot, 0:n * 32].rearrange("p (k w) -> p k w", k=n)[:, :, 0:HD],
                                       home[:, bass.ds(u * (n * HD), n * HD)].rearrange("p (k w) -> p k w", k=n))\
                            .then_inc(s["v_set"], 1)
                    set_values(0, 0)
                    set_values(1, 1)

                    def body(u, slot, r, last):
                        if not isinstance(u, int):
                            act.wait_ge(s["pv"], u * KB + PV0)
                            set_values(u + 2, (slot + 2) % ROLL)
                        for e in range(NE):
                            p, i, kind = e // (2 * G), e // 2 % G, e % 2
                            if i == 0:
                                act.wait_ge(s["pv"], u * KB + (2 * p + 1 + kind))
                            w = T - 128 * (KB - 1 - p if kind else p)
                            act.wait_ge(s["b_mm"], u * NE + (e + 1))
                            nc.scalar.activation(
                                prob[kind][:, p % 2, i, 0:w],
                                ps[:, 2 * kind:2 * kind + 2, :].rearrange("p b n -> p (b n)")[:, 0:w],
                                ACT.Exp).then_inc(s["exp"], 1)
                    all_units(act, body)

                @block.vector
                def _(dve):
                    def tile_max(count, n, low, high):
                        i, qb, hf = TILES[n]
                        w = min(CH, (qb + 1) * 128 - hf * CH)
                        dve.wait_ge(s["a_mm"], count + (n + 1))
                        nc.vector.tensor_reduce(high(i, qb - 4) if hf else low(i, qb), ps[:, A_BANKS[n % RING], 0:w],
                                                AX.X, ALU.max, negate=True).then_inc(s["a_red"], 1)

                    def split_max(u, slot):
                        dve.wait_ge(s["a_red"], u * NT + (NT + RED0))
                        late = lowmax.rearrange("p (i k) -> p i k", i=G)[:, :, 4:KB]
                        nc.vector.tensor_tensor(late, late, highmax.rearrange("p (i k) -> p i k", i=G), ALU.min)\
                            .then_inc(s["folded"], 1)
                        dve.wait_ge(s["folded"], u + 1)
                        nc.vector.tensor_copy(mpart[:, 0, :], lowmax).then_inc(s["hi"], 1)
                        dve.wait_ge(s["hi"], u + 1)
                        nc.vector.tensor_tensor(rem, lowmax, mpart[:, 0, :], ALU.subtract).then_inc(s["r1"], 1)
                        dve.wait_ge(s["r1"], u + 1)
                        nc.vector.tensor_copy(mpart[:, 1, :], rem).then_inc(s["mid"], 1)
                        dve.wait_ge(s["mid"], u + 1)
                        nc.vector.tensor_tensor(mpart[:, 2, :], rem, mpart[:, 1, :], ALU.subtract)\
                            .then_inc(s["parts"], 1)
                        dve.wait_ge(s["turned"], u + 1)
                        nc.vector.tensor_copy(mT[0:96, slot, :], turned[0:96, :]).then_inc(s["m_copied"], 1)

                    if l == 1:
                        nc.vector.memset(kst[64:MROWS, :, 0:kh], 1.0).then_inc(k_ones, 1)
                    dve.sem_inc(s["evac"], EVAC0)
                    dve.sem_inc(s["a_red"], RED0)
                    if beside:
                        beside.begin_dve(dve)
                    with dve.Fori(0, G) as i:
                        for n in range(NH):
                            tile_max(i * NH, n, lambda _, qb: lowmax[:, bass.ds(i * KB + qb, 1)],
                                     lambda _, qb: highmax[:, bass.ds(i * 4 + qb, 1)])
                            if beside:
                                beside.dve(dve, i, n)
                    split_max(0, 0)
                    if beside:
                        beside.end_dve(dve)

                    def body(u, slot, r, last):
                        if not last:
                            for n in range(NT):
                                tile_max((u + 1) * NT, n, lambda i, qb: lowmax[:, i * KB + qb:i * KB + qb + 1],
                                         lambda i, qb: highmax[:, i * 4 + qb:i * 4 + qb + 1])
                            split_max(u + 1, (slot + 1) % ROLL)
                        dve.wait_ge(s[f"st{slot}"], r * (16 * G) + 16)
                        dve.wait_ge(s["pv"], u * KB + (KB + PV0))
                        nc.vector.tensor_copy(osb[:, slot, :], ps[:, 4:6, :].rearrange("p b n -> p (b n)"))\
                            .then_inc(s["evac"], 1)
                    all_units(dve, body)

                @block.tensor
                def _(pe):
                    def tile_a(count, slot, head, n):
                        _, qb, hf = TILES[n]
                        w = min(CH, (qb + 1) * 128 - hf * CH)
                        pe.wait_ge(s["a_red"], count + (n - RING + 1 + RED0))
                        diagonal = hf == qb // 4
                        bank = A_BANKS[n % RING]
                        if isinstance(head, int):
                            queries = qst[0:ROWS, slot, head, qb * 128:(qb + 1) * 128]
                            keys = kst[0:ROWS, slot, head if kh > 1 else 0, hf * CH:hf * CH + w]
                        else:
                            flat = lambda st: st[0:ROWS, slot].rearrange("p i n -> p (i n)")
                            queries = flat(qst)[:, bass.ds(head * T + qb * 128, 128)]
                            keys = flat(kst)[:, bass.ds(head * T + hf * CH, w)] if kh > 1 else \
                                kst[0:ROWS, slot, 0, hf * CH:hf * CH + w]
                        mm = nc.tensor.matmul(ps[:, bank, 0:w], queries, keys, start=True, stop=True)
                        if diagonal:
                            mm = nc.tensor.matmul(ps[:, bank, w - 128:w], idb[:, :], mskb[:, 0, :],
                                                  start=False, stop=True, skip_group_check=True)
                        mm.then_inc(s["a_mm"], 1)

                    def turn(u):
                        pe.wait_ge(s["parts"], u + 1)
                        nc.tensor.transpose(turned[0:96, :], mpart.rearrange("p a c -> p (a c)"), idb[:, :])\
                            .then_inc(s["turned"], 1)

                    def multiply(u, slot, p, kind, halves=(0, 1)):
                        kb = KB - 1 - p if kind else p
                        if p == 0 and kind == 0 and halves[0] == 0:
                            pe.wait_ge(s["evac"], u + EVAC0)
                        if halves[0] == 0:
                            pe.wait_ge(s["exp"], u * NE + (2 * G * p + 2 * G - 1 + kind + EXP0))
                        for hf in halves if kind == 0 else (1,):
                            lo = max(0, kb * 128 - hf * CH)
                            for i in range(G):
                                p0 = hf * CH + lo - kb * 128
                                mm = nc.tensor.matmul(ps[32 * i:32 * i + 32, 4 + hf, lo:CH],
                                                      vals[:, slot, kb, i if vw > 1 else 0, :],
                                                      prob[kind][:, p % 2, i, p0:p0 + CH - lo],
                                                      start=(kb == 0), stop=(kb == (4 if hf else 3)),
                                                      tile_position=(0, 32 * i), skip_group_check=True)
                        if kind or halves[-1] == 1:
                            mm.then_inc(s["pv"], 1)

                    pe.sem_inc(s["pv"], PV0)
                    if beside:
                        beside.begin_pe(pe)
                    pe.wait_ge(s["ld0"], 16 * NLOAD)
                    with pe.Fori(0, G) as i:
                        for n in range(NH):
                            tile_a(i * NH, 0, i, n)
                            if beside:
                                beside.pe(pe, i, n)
                    turn(0)
                    if beside:
                        beside.end_pe(pe)

                    def body(u, slot, r, last):
                        nxt = (slot + 1) % ROLL
                        if not last:
                            pe.wait_ge(s[f"ld{nxt}"], (r + (2 if nxt == 0 else 1)) * (16 * NLOAD))
                            pe.wait_ge(s["m_copied"], u + 1)
                        pe.wait_ge(s[f"m_set{slot}"], r * 16 + 16)
                        pe.wait_ge(s["v_set"], u + 1)
                        for e in range(NE):
                            p, i, kind = e // (2 * G), e // 2 % G, e % 2
                            kb = KB - 1 - p if kind else p
                            w = T - 128 * kb
                            pe.wait_ge(s["exp"], u * NE + (e - 1 + EXP0))
                            for c0 in range(0, w, CH):
                                cw = min(CH, w - c0)
                                mm = nc.tensor.matmul(
                                    ps[:, 2 * kind + c0 // CH, 0:cw],
                                    kst[0:MROWS, slot, i if kh > 1 else 0, kb * 128:(kb + 1) * 128],
                                    qst[0:MROWS, slot, i, kb * 128 + c0:kb * 128 + c0 + cw], start=True, stop=True)
                                if c0 == 0:
                                    mm = nc.tensor.matmul(ps[:, 2 * kind, 0:128], idb[:, :], mskb[:, 1, :],
                                                          start=False, stop=True, skip_group_check=True)
                            mm.then_inc(s["b_mm"], 1)
                            if not last:
                                for n in range(e * NT // (2 * A_STEPS), min((e + 1) * NT // (2 * A_STEPS), NT)):
                                    tile_a((u + 1) * NT, nxt, TILES[n][0], n)
                                if e == 2 * A_STEPS + 1:
                                    turn(u + 1)
                            if p >= 1 and kind and i in (1, 2):
                                multiply(u, slot, p - 1, 0, (i - 1,))
                            if 1 <= p < NP - 1 and kind and i == 3:
                                multiply(u, slot, p - 1, 1)
                        multiply(u, slot, NP - 2, 1)
                        multiply(u, slot, NP - 1, 0)
                        multiply(u, slot, NP - 1, 1)
                    all_units(pe, body)

        attention(0, G, G, acc)
        if stop == 2:
            return dump_yd(nc, sem, yd[0], pool_a, out)

        def top_one(dve_step, values, onehot, m, eq, sc, cm):
            v3 = lambda ap: ap.rearrange("p (t e) -> p t e", e=E)
            wide = lambda ap: ap.unsqueeze(2).to_broadcast([128, TB, E])
            dve_step(nc.vector.tensor_reduce(m, v3(values), AX.X, ALU.max))
            dve_step(nc.vector.tensor_tensor(v3(eq), v3(values), wide(m), ALU.is_equal))
            dve_step(nc.vector.tensor_tensor(v3(sc), v3(eq), rev.unsqueeze(1).to_broadcast([128, TB, E]), ALU.mult))
            dve_step(nc.vector.tensor_reduce(cm, v3(sc), AX.X, ALU.max))
            dve_step(nc.vector.tensor_tensor(v3(onehot), v3(sc), wide(cm), ALU.is_equal))

        rt = lambda k: shortp[:, 128 * k:128 * (k + 1)]
        rs = lambda k: small[:, 640 + TB * k:640 + TB * (k + 1)]
        v3 = lambda ap: ap.rearrange("p (t e) -> p t e", e=E)
        wide = lambda ap: ap.unsqueeze(2).to_broadcast([128, TB, E])

        def route_pe(pe, weight, done):
            for tb in range(TB):
                mm = nc.tensor.matmul(ps[:, 0, tb * E:(tb + 1) * E], h[:, tb * 128:(tb + 1) * 128], weight,
                                      start=True, stop=True)
            mm.then_inc(done, 1)

        def invert_act(act, l):
            for c in range(NC + 1):
                if c < NC:
                    w = sums_chunk(c, 1)
                    act.wait_ge(ld_y[l][c // 2], 32)
                    nc.scalar.activation(w, w, ACT.Ln).then_inc(s_log_sum, 1)
                if c >= 1:
                    w = sums_chunk(c - 1, 1)
                    act.wait_ge(s_log_sum, l * NC + c)
                    nc.scalar.activation(w, w, ACT.Exp, scale=-1.0).then_inc(s_inv_sum, 1)

        w1s = [f[2][:, k * HID0:(k + 1) * HID0] for k in range(2)]
        w2s = [f[3][:, k * 512:(k + 1) * 512].rearrange("p (k n) -> p k n", k=4) for k in range(2)]
        b1x = [f[5][:, 4 * k:4 * k + 4] for k in range(2)]
        b2x = [f[5][:, 8 + k:9 + k] for k in range(2)]
        x_ld = [sem("x_ld0"), sem("x_ld1")]
        XLD = 4 * 16

        def load_weights(sp, e, k):
            for dst, src in ((w1s[k], t["w1"][bass.ds(e, 1)].rearrange("o p n -> (o p) n")),
                             (w2s[k], t["w2"][bass.ds(e, 1)].rearrange("o p k n -> (o p) k n")),
                             (b1x[k], t["b1"][bass.ds(e, 1)].rearrange("o p k -> (o p) k")),
                             (b2x[k], t["b2"][bass.ds(e, 1)].rearrange("o p k -> (o p) k"))):
                sp.dma_start(dst, src).then_inc(x_ld[k], 16)

        n3 = Norm(2, lambda c: f[4][:, c_of(c)], lambda c: f[0][:, c_of(c)], lambda c: f[1][:, c_of(c)],
                  lambda c: h[:, c_of(c)], meanM, 0, gain=col("ln2g"), bias=col("ln2b"), scaled=1)
        s_log_sum, s_inv_sum, yn3, wp3, xa3, ac3, lg3, ch3, gap3, ex3, w3r, w3t, w3c, w3s = (
            sem(f"s3_{n}") for n in ("log_sum", "inverse_sum", "y", "wp", "xa", "acc", "logits", "chain", "gap", "exp",
                                     "weights", "turned", "copied", "stored"))

        with nc.Block() as block:
            @block.sync
            def _(sp):
                load_sums(sp, 0, 1)
                load_weights(sp, 0, 0)
                load_weights(sp, 1, 1)
                sp.wait_ge(w3c, 1)
                sp.dma_start(wd[0].rearrange("e (t n) -> (e t) n", n=128), rt(11)).then_inc(w3s, 16)
                sp.wait_ge(w3s, 16)

            @block.vector
            def _(dve):
                for c in range(NC):
                    dve.wait_ge(ld_y[0][c // 2], 32)
                    dve.wait_ge(s_inv_sum, c + 1)
                    nc.vector.tensor_tensor(sums_chunk(c, 0), sums_chunk(c, 0), sums_chunk(c, 1), ALU.mult)\
                        .then_inc(yn3, 1)
                for c in range(NC):
                    dve.wait_ge(wp3, c + 1)
                    nc.vector.scalar_tensor_tensor(f[4][:, c_of(c)], ps[:, 4 + c, :], col("bp"), xn_chunk(c),
                                                   ALU.add, ALU.add).then_inc(xa3, 1)
                    dve.wait_ge(xa3, c + 1)
                    nc.vector.tensor_tensor(acc[:, c_of(c)], xT[:, c_of(c)], f[4][:, c_of(c)], ALU.add)\
                        .then_inc(ac3, 1)
                norm_dve(dve, n3)
                steps = [0]

                def step(ins):
                    steps[0] += 1
                    ins.then_inc(ch3, 1)
                    dve.wait_ge(ch3, steps[0])

                dve.wait_ge(lg3, 1)
                logit, one1, one2, eq, sc = rt(0), rt(1), rt(2), rt(3), rt(4)
                m1, m2, cm, ew, w1, w2 = (rs(k) for k in range(6))
                step(nc.vector.tensor_tensor(v3(logit), v3(ps[:, 0, 0:128]),
                                             gbb.unsqueeze(1).to_broadcast([128, TB, E]), ALU.add))
                top_one(step, logit, one1, m1, eq, sc, cm)
                step(nc.vector.scalar_tensor_tensor(logit, one1, -3e38, logit, ALU.mult, ALU.add))
                top_one(step, logit, one2, m2, eq, sc, cm)
                nc.vector.tensor_tensor(m2, m2, m1, ALU.subtract).then_inc(gap3, 1)
                dve.wait_ge(ex3, 1)
                step(nc.vector.tensor_scalar(w1, ew, 1.0, None, ALU.add))
                step(nc.vector.reciprocal(w1, w1))
                step(nc.vector.tensor_tensor(w2, ew, w1, ALU.mult))
                step(nc.vector.tensor_tensor(v3(one1), v3(one1), wide(w1), ALU.mult))
                step(nc.vector.tensor_tensor(v3(one2), v3(one2), wide(w2), ALU.mult))
                nc.vector.tensor_tensor(rt(10).rearrange("p (e t) -> p t e", t=TB), v3(one1), v3(one2), ALU.add)\
                    .then_inc(w3r, 1)
                dve.wait_ge(w3t, 1)
                nc.vector.tensor_copy(rt(11), ps[:, 1, 0:128]).then_inc(w3c, 1)

            @block.scalar
            def _(act):
                invert_act(act, 0)
                norm_act(act, n3)
                act.wait_ge(gap3, 1)
                nc.scalar.activation(rs(3), rs(1), ACT.Exp).then_inc(ex3, 1)

            @block.tensor
            def _(pe):
                for c in range(NC):
                    pe.wait_ge(yn3, c + 1)
                    nc.tensor.matmul(ps[:, 4 + c, :], wf[:, 3, :], sums_chunk(c, 0), start=True, stop=True)\
                        .then_inc(wp3, 1)
                norm_pe(pe, n3, ready=xa3)
                pe.wait_ge(s_normed, n3.base + NC)
                route_pe(pe, wl1[:, 840:848], lg3)
                pe.wait_ge(w3r, 1)
                nc.tensor.transpose(ps[:, 1, 0:128], rt(10), ident).then_inc(w3t, 1)

        if stop == 3:
            return dump(nc, sem, acc, out)

        mid = pool_a[:, 0:4 * CH].rearrange("p (k n) -> p k n", k=4)
        wbc = [f[0], f[1]]
        tmp = f[4]
        x_row, x_h, x_gelu, x_y, x_t, x_acc = ([sem("x_row0"), sem("x_row1")], sem("x_h"), sem("x_gelu"),
                                              sem("x_y"), sem("x_tmp"), sem("x_acc"))
        EB = E // NB
        STEPS = EB * NC
        T0 = 2
        rb = [pool_a[:, N + CH * k:N + CH * (k + 1)] for k in range(12)]
        dlt_, mix_, v_, kv_, rw_, gate_, cen_, sq_ = rb[0], rb[1:5], rb[5], rb[6], rb[8], rb[9], rb[10], rb[11]
        scan_ = [rb[7], osb[:, 0, CH:2 * CH]]
        decb = osb[:, 0, 0:CH]
        dcy, dcyb, dlt, mixed, kv_mm, vsb, kvd, scd, t2d, rg_mm, sgd, rwd = (
            sem(n) for n in ("decay", "decay_wide", "difference", "mixed", "kv_mm", "v_there", "kv_done",
                             "scan_done", "bonus_done", "rg_mm", "gate_done", "rw_done"))
        rmean, rcen, rsq, rvar, rlog, rinv, rgated, rnorm, wo_mm, wo_ev = (
            sem(f"branch_{n}") for n in ("mean", "centred", "squared", "variance", "log_variance", "inverse",
                                         "gated", "normed", "wo_mm", "added"))

        def branch_tokens(r, q):
            return bass.ds(r * T + q * CH, CH)

        def branch_dve(dve, r, q, t, n):
            m = r * 2 + q
            tok = branch_tokens(r, q)
            if t == 0:
                nc.vector.tensor_tensor(dlt_, xn[:, tok], xs[:, tok], ALU.subtract).then_inc(dlt, 1)
                dve.wait_ge(dlt, m + 1)
                for j, name in enumerate(("mk", "mv", "mr", "mg")):
                    nc.vector.scalar_tensor_tensor(mix_[j], dlt_, col(name), xs[:, tok], ALU.mult, ALU.add)\
                        .then_inc(mixed, 1)
            if t == 1:
                dve.wait_ge(vsb, m + 1)
                nc.vector.scalar_tensor_tensor(kv_, ps[:, 6, :], col("bk"), v_, ALU.add, ALU.mult)\
                    .then_inc(kvd, 1)
                dve.wait_ge(kvd, m + 1)
                init = scan_[0][:, CH - 1:CH] if q else 0.0
                nc.vector.tensor_tensor_scan(scan_[q], decb, kv_, init, ALU.mult, ALU.add).then_inc(scd, 1)
                dve.wait_ge(scd, m + 1)
                nc.vector.scalar_tensor_tensor(kv_, kv_, col("u"), scan_[q], ALU.mult, ALU.add)\
                    .then_inc(t2d, 1)
            if t == 2:
                dve.wait_ge(rg_mm, m + 1)
                dve.wait_ge(t2d, m + 1)
                nc.vector.scalar_tensor_tensor(rw_, ps[:, 6, :], col("br"), kv_, ALU.add, ALU.mult)\
                    .then_inc(rwd, 1)
            if t == 3:
                dve.wait_ge(rmean, m + 1)
                nc.vector.tensor_tensor(cen_, rw_, ps[:, 6, :], ALU.subtract).then_inc(rcen, 1)
            if t == 5:
                dve.wait_ge(rinv, m + 1)
                nc.vector.scalar_tensor_tensor(sq_, gate_, 1.0, sq_, ALU.add, ALU.mult).then_inc(rgated, 1)
                dve.wait_ge(rgated, m + 1)
                nc.vector.tensor_tensor(rw_, cen_, sq_, ALU.mult).then_inc(rnorm, 1)
            if t == 6:
                dve.wait_ge(wo_mm, m + 1)
                dve.wait_ge(x_acc, n)
                nc.vector.scalar_tensor_tensor(acc[:, tok], ps[:, 6, :], col("bo"), acc[:, tok], ALU.add, ALU.add)\
                    .then_inc(wo_ev, 1)
                dve.wait_ge(wo_ev, m + 1)

        def branch_act(act, r, q, t):
            m = r * 2 + q
            if t == 1:
                act.wait_ge(kv_mm, m + 1)
                nc.scalar.activation(v_, ps[:, 7, :], ACT.Identity, bias=col("bv")).then_inc(vsb, 1)
            if t == 2:
                act.wait_ge(dcyb, 3)
                act.wait_ge(rg_mm, m + 1)
                nc.scalar.activation(gate_, ps[:, 7, :], ACT.Tanh, bias=hbg, scale=0.5).then_inc(sgd, 1)
            if t == 3:
                act.wait_ge(rcen, m + 1)
                nc.scalar.activation(sq_, cen_, ACT.Square).then_inc(rsq, 1)
            if t == 4:
                nc.scalar.preload_act_table_set(LOG_EXP)
                act.wait_ge(rvar, m + 1)
                nc.scalar.activation(sq_, ps[:, 7, :], ACT.Ln, bias=eps[:, 0:1]).then_inc(rlog, 1)
                act.wait_ge(rlog, m + 1)
                nc.scalar.activation(sq_, sq_, ACT.Exp, scale=-0.5).then_inc(rinv, 1)

        def branch_pe(pe, r, q, t):
            m = r * 2 + q

            def product(bank, weight, operand, done):
                mm = nc.tensor.matmul(ps[:, bank, :], weight, operand, start=True, stop=True)
                if done is not None:
                    mm.then_inc(done, 1)
            if t == 1:
                pe.wait_ge(mixed, m * 4 + 4)
                product(6, wl0[:, 2, :], mix_[0], None)
                product(7, wl0[:, 3, :], mix_[1], kv_mm)
            if t == 2:
                pe.wait_ge(kvd, m + 1)
                product(6, wl0[:, 1, :], mix_[2], None)
                product(7, wl0[:, 0, :], mix_[3], rg_mm)
            if t == 3:
                pe.wait_ge(rwd, m + 1)
                product(6, headM, rw_, rmean)
            if t == 4:
                pe.wait_ge(rsq, m + 1)
                pe.wait_ge(sgd, m + 1)
                product(7, headM, sq_, rvar)
            if t == 6:
                pe.wait_ge(dcyb, 3)
                pe.wait_ge(rnorm, m + 1)
                product(6, wl0[:, 4, :], rw_, wo_mm)

        with nc.Block() as block:
            @block.sync
            def _(sp):
                def load_row(e, k):
                    sp.dma_start(wbc[k], wd[0][bass.ds(e, 1)].rearrange("o n -> (o n)").partition_broadcast(128))\
                        .then_inc(x_row[k], 16)
                load_row(0, 0)
                load_row(1, 1)
                with sp.Fori(1, E // 2) as r:
                    for k in range(2):
                        sp.wait_ge(x_acc, r * (2 * NC) + (k - 1) * NC)
                        load_weights(sp, r * 2 + k, k)
                        load_row(r * 2 + k, k)

            @block.tensor
            def _(pe):
                with pe.Fori(0, NB) as r:
                    for k in range(EB):
                        pe.wait_ge(x_ld[k % 2], r * (XLD * EB // 2) + XLD * (k // 2 + 1))
                        for c in range(NC):
                            branch_pe(pe, r, (k * NC + c) // 8, (k * NC + c) % 8)
                            n = r * STEPS + (k * NC + c)
                            pe.wait_ge(x_gelu, n * 4 + 1)
                            for b in range(4):
                                nc.tensor.matmul(ps[:, b, :], w1s[k % 2][:, b * 128:(b + 1) * 128], h[:, c_of(c)],
                                                 start=True, stop=True).then_inc(x_h, 1)
                            pe.wait_ge(x_t, n + (T0 - 1))
                            for b in range(4):
                                pe.wait_ge(x_gelu, n * 4 + (b + 2))
                                mm = nc.tensor.matmul(ps[:, 4 + c % 2, :], w2s[k % 2][:, b, :], mid[:, b, :],
                                                      start=(b == 0), stop=(b == 3))
                            mm.then_inc(x_y, 1)

            @block.scalar
            def _(act):
                act.sem_inc(x_gelu, 1)
                nc.scalar.activation(dec[:, 0:1], col("w"), ACT.Exp).then_inc(dcy, 1)
                act.wait_ge(dcy, 1)
                nc.scalar.activation(dec[:, 1:2], dec[:, 0:1], ACT.Exp, scale=-1.0).then_inc(dcy, 1)
                with act.Fori(0, NB) as r:
                    for k in range(EB):
                        act.wait_ge(x_ld[k % 2], r * (XLD * EB // 2) + XLD * (k // 2 + 1))
                        for c in range(NC):
                            n = r * STEPS + (k * NC + c)
                            for b in range(4):
                                act.wait_ge(x_h, n * 4 + (b + 1))
                                nc.scalar.activation(mid[:, b, :], ps[:, b, :], ACT.Gelu,
                                                     bias=b1x[k % 2][:, b:b + 1]).then_inc(x_gelu, 1)
                            branch_act(act, r, (k * NC + c) // 8, (k * NC + c) % 8)

            @block.vector
            def _(dve):
                dve.sem_inc(x_t, T0)
                nc.vector.memset(decb, 0.0).then_inc(dcyb, 1)
                nc.vector.tensor_scalar(hbg, col("bg"), 0.5, None, ALU.mult).then_inc(dcyb, 1)
                nc.vector.tensor_scalar(wl0[:, 4, :], wl0[:, 4, :], 0.5, None, ALU.mult).then_inc(dcyb, 1)
                dve.wait_ge(dcy, 2)
                dve.wait_ge(dcyb, 3)
                nc.vector.tensor_scalar(decb, decb, dec[:, 1:2], None, ALU.add).then_inc(dcyb, 1)
                dve.wait_ge(dcyb, 4)
                with dve.Fori(0, NB) as r:
                    for k in range(EB):
                        dve.wait_ge(x_ld[k % 2], r * (XLD * EB // 2) + XLD * (k // 2 + 1))
                        dve.wait_ge(x_row[k % 2], r * (16 * EB // 2) + 16 * (k // 2 + 1))
                        for c in range(NC):
                            n = r * STEPS + (k * NC + c)
                            branch_dve(dve, r, (k * NC + c) // 8, (k * NC + c) % 8, n)
                            dve.wait_ge(x_y, n + 1)
                            nc.vector.scalar_tensor_tensor(tmp[:, c_of(c)], ps[:, 4 + c % 2, :], b2x[k % 2],
                                                           wbc[k % 2][:, c_of(c)], ALU.add, ALU.mult)\
                                .then_inc(x_t, 1)
                            dve.wait_ge(x_t, n + (T0 + 1))
                            nc.vector.tensor_tensor(acc[:, c_of(c)], acc[:, c_of(c)], tmp[:, c_of(c)], ALU.add)\
                                .then_inc(x_acc, 1)

        if stop == 4:
            return dump(nc, sem, acc, out)

        n5 = Norm(3, lambda c: acc[:, c_of(c)], lambda c: f[0][:, c_of(c)], lambda c: f[1][:, c_of(c)],
                  lambda c: h[:, c_of(c)], meanM, 0)
        low = f[4]
        lowk = f[5]
        cosq, sinq = xT[:, 0:T], xT[:, T:2 * T]
        cosk, sink = osb[:, 0, 0:CH], osb[:, 1, 0:CH]
        qs5 = Split("tq", lambda c: f[2][:, c_of(c)], lambda p, c: partb[:, 0, p, c_of(c)], qd[1], after=qs_)
        ks5 = Split("tk", lambda c: f[3][:, c_of(c)], lambda p, c: partb[:, 1, p, c_of(c)], kd[1], after=ks_)
        home1 = vst[:, 2, CH:2 * CH]
        tw = shortp[:, 2048:2048 + CH], shortp[:, 2048 + CH:2048 + 2 * CH]
        ld5, lo5, lc5, hi5, hk5, ra5, rk5, v5, ve5 = (
            sem(f"s5_{n}") for n in ("ld", "low", "low_copied", "high", "keys", "q_turned", "k_turned", "v",
                                     "v_copied"))
        lg5, ch5, mx5, ex5, pf5, tot5, w5r, w5t, w5c, w5s, lgc = (
            sem(f"r5_{n}") for n in ("logits", "chain", "less_max", "exp", "counts", "prefix", "weights",
                                     "turned", "copied", "stored", "logits_copied"))

        with nc.Block() as block:
            @block.sync
            def _(sp):
                sp.dma_start(cosq, t["rope"][:, 0, :]).then_inc(ld5, 16)
                sp.dma_start(sinq, t["rope"][:, 1, :]).then_inc(ld5, 16)
                sp.dma_start(cosk, t["ropek"][:, 0, :]).then_inc(ld5, 16)
                sp.dma_start(sink, t["ropek"][:, 1, :]).then_inc(ld5, 16)
                for c in range(NC):
                    split_store(sp, qs5, c)
                sp.wait_ge(ks5.lo, ks5.base + 1)
                for c in range(NC):
                    for p in range(PARTS):
                        sp.dma_start(kd[1][c // 2, :, p, :, (c % 2) * CH:(c % 2 + 1) * CH],
                                     ks5.parts(p, 0)[32 * c:32 * c + 32]).then_inc(ks5.stored, 16)
                sp.wait_ge(w5c, 1)
                sp.dma_start(wd[1].rearrange("e (t n) -> (e t) n", n=128), rt(11)).then_inc(w5s, 16)
                sp.wait_ge(w5s, 16)
                sp.wait_ge(qs5.stored, qs5.base_stored + 16 * PARTS * NC)
                sp.wait_ge(ks5.stored, ks5.base_stored + 16 * PARTS * NC)

            @block.scalar
            def _(act):
                nc.scalar.preload_act_table_set(LOG_EXP)
                norm_act(act, n5)
                for c in range(NC + 1):
                    if c < NC:
                        b = 4 * (c % 2)
                        act.wait_ge(lo5, c + 1)
                        nc.scalar.copy(low[0:QL, c_of(c)], ps[0:QL, b, :]).then_inc(lc5, 1)
                        nc.scalar.copy(lowk[0:KVL, c_of(c)], ps[0:KVL, b + 1, :]).then_inc(lc5, 1)
                    if c >= 1:
                        first_part(act, qs5, c - 1)
                        second_part(act, qs5, c - 1)
                first_part(act, ks5, 0)
                second_part(act, ks5, 0)
                act.wait_ge(mx5, 1)
                nc.scalar.activation(rt(5), rt(5), ACT.Exp).then_inc(ex5, 1)

            @block.vector
            def _(dve):
                norm_dve(dve, n5)
                dve.wait_ge(ld5, 64)
                for c in range(NC):
                    b = 4 * (c % 2)
                    half = slice((c % 2) * CH, (c % 2 + 1) * CH)
                    dve.wait_ge(hi5, c + 1)
                    nc.vector.tensor_tensor(qs5.f(c), ps[:, b, :], cosq[:, half], ALU.mult).then_inc(ra5, 1)
                    nc.vector.tensor_tensor(tw[0], ps[:, b + 1, :], sinq[:, half], ALU.mult).then_inc(ra5, 1)
                    dve.wait_ge(ra5, 2 * (c + 1))
                    nc.vector.tensor_tensor(qs5.f(c), qs5.f(c), tw[0], ALU.add).then_inc(qs5.full, 1)
                    remainder(dve, qs5, c)
                    if c == NC - 1:
                        dve.wait_ge(hk5, 1)
                        nc.vector.tensor_tensor(ks5.f(0), ps[:, 2, :], cosk, ALU.mult).then_inc(rk5, 1)
                        nc.vector.tensor_tensor(tw[1], ps[:, 3, :], sink, ALU.mult).then_inc(rk5, 1)
                        dve.wait_ge(rk5, 2)
                        nc.vector.tensor_tensor(ks5.f(0), ks5.f(0), tw[1], ALU.add).then_inc(ks5.full, 1)
                    last_part(dve, qs5, c)
                remainder(dve, ks5, 0)
                dve.wait_ge(v5, 1)
                nc.vector.tensor_copy(home1.rearrange("p (b g k d) -> p b g k d", b=NB, g=KVH, k=KB)[:, 0],
                                      ps[:, 6, 0:256].rearrange("p (k g d) -> p g k d", k=KB, g=KVH)).then_inc(ve5, 1)
                nc.vector.tensor_copy(home1.rearrange("p (b g k d) -> p b g k d", b=NB, g=KVH, k=KB)[:, 1],
                                      ps[:, 6, 256:512].rearrange("p (k g d) -> p g k d", k=KB, g=KVH)).then_inc(ve5, 1)
                last_part(dve, ks5, 0)
                steps = [0]

                def step(ins):
                    steps[0] += 1
                    ins.then_inc(ch5, 1)
                    dve.wait_ge(ch5, steps[0])

                dve.wait_ge(lg5, 1)
                gate, one1, one2, eq, sc, ex = rt(0), rt(1), rt(2), rt(3), rt(4), rt(5)
                m1, m2, cm, sm = (rs(k) for k in range(4))
                step(nc.vector.tensor_copy(gate, ps[:, 7, 0:128]))
                step(nc.vector.tensor_reduce(m1, v3(gate), AX.X, ALU.max))
                nc.vector.tensor_tensor(v3(ex), v3(gate), wide(m1), ALU.subtract).then_inc(mx5, 1)
                dve.wait_ge(ex5, 1)
                step(nc.vector.tensor_reduce(sm, v3(ex), AX.X, ALU.add))
                step(nc.vector.reciprocal(sm, sm))
                step(nc.vector.tensor_tensor(v3(gate), v3(ex), wide(sm), ALU.mult))
                top_one(step, gate, one1, m1, eq, sc, cm)
                step(nc.vector.scalar_tensor_tensor(ex, one1, -2.0, gate, ALU.mult, ALU.add))
                top_one(step, ex, one2, m2, eq, sc, cm)
                picked, run, run2 = rt(6), rt(7), rt(8)
                step(nc.vector.tensor_tensor(picked, one1, one2, ALU.add))
                step(nc.vector.memset(run, 0.0))
                step(nc.vector.tensor_copy(run[:, E:128], picked[:, 0:128 - E]))
                src, dst = run, run2
                for k in (1, 2, 4, 8):
                    step(nc.vector.tensor_copy(dst[:, 0:k * E], src[:, 0:k * E]))
                    step(nc.vector.tensor_tensor(dst[:, k * E:128], src[:, k * E:128], src[:, 0:128 - k * E], ALU.add))
                    src, dst = dst, src
                nc.vector.tensor_scalar(src, src, 1.0, None, ALU.mult).then_inc(pf5, 1)
                dve.wait_ge(tot5, 1)
                step(nc.vector.tensor_scalar(eq, ps[:, 7, 128:256], CAP, None, ALU.is_le))
                step(nc.vector.tensor_tensor(picked, picked, eq, ALU.mult))
                step(nc.vector.tensor_tensor(gate, gate, picked, ALU.mult))
                step(nc.vector.tensor_reduce(sm, v3(gate), AX.X, ALU.add))
                step(nc.vector.tensor_scalar(sm, sm, 1e-6, None, ALU.add))
                step(nc.vector.reciprocal(sm, sm))
                nc.vector.tensor_tensor(rt(10).rearrange("p (e t) -> p t e", t=TB), v3(gate), wide(sm), ALU.mult)\
                    .then_inc(w5r, 1)
                dve.wait_ge(w5t, 1)
                nc.vector.tensor_copy(rt(11), ps[:, 7, 256:384]).then_inc(w5c, 1)

            @block.tensor
            def _(pe):
                norm_pe(pe, n5)
                pe.wait_ge(s_log, n5.base + NC)
                for c in range(NC):
                    b = 4 * (c % 2)
                    pe.wait_ge(s_normed, n5.base + c + 1)
                    if c >= 2:
                        pe.wait_ge(ra5, 2 * (c - 1))
                    nc.tensor.matmul(ps[0:QL, b, :], wl1[:, 0:64], h[:, c_of(c)], start=True, stop=True)
                    nc.tensor.matmul(ps[0:KVL, b + 1, :], wl1[:, 320:352], h[:, c_of(c)], start=True, stop=True)\
                        .then_inc(lo5, 1)
                    pe.wait_ge(lc5, 2 * (c + 1))
                    ql, kl = low[0:QL, c_of(c)], lowk[0:KVL, c_of(c)]
                    nc.tensor.matmul(ps[:, b, :], wl1[0:QL, 64:192], ql, start=True, stop=True)
                    nc.tensor.matmul(ps[:, b + 1, :], wl1[0:QL, 192:320], ql, start=True, stop=True).then_inc(hi5, 1)
                    for k in range(2):
                        mm = nc.tensor.matmul(ps[32 * c:32 * c + 32, 2 + k, :], wl1[0:KVL, 352 + 32 * k:384 + 32 * k],
                                              kl, start=True, stop=True, tile_position=(0, 32 * c),
                                              skip_group_check=True)
                mm.then_inc(hk5, 1)
                for tb in range(TB):
                    mm = nc.tensor.matmul(ps[:, 6, tb * 32:(tb + 1) * 32], lowk[0:KVL, tb * 128:(tb + 1) * 128],
                                          wl1[0:KVL, 416:448], start=True, stop=True)
                mm.then_inc(v5, 1)
                for tb in range(TB):
                    mm = nc.tensor.matmul(ps[:, 7, tb * E:(tb + 1) * E], h[:, tb * 128:(tb + 1) * 128],
                                          wl1[:, 576:584], start=True, stop=True)
                mm.then_inc(lg5, 1)
                pe.wait_ge(pf5, 1)
                nc.tensor.matmul(ps[:, 7, 128:256], tri, rt(6), start=True, stop=False, skip_group_check=True)
                nc.tensor.matmul(ps[:, 7, 128:256], ones, rt(7), start=False, stop=True, skip_group_check=True)\
                    .then_inc(tot5, 1)
                pe.wait_ge(w5r, 1)
                nc.tensor.transpose(ps[:, 7, 256:384], rt(10), ident).then_inc(w5t, 1)

        if stop == 5:
            return dump(nc, sem, h, out)

        hidden = [xn, spare]
        wrow = [xT, xs]
        wds = [vst[:, k, 512:768].rearrange("p (k n) -> p k n", k=2) for k in range(2)]
        ztmp = osb[:, 0:2, :].rearrange("p s n -> p (s n)")
        Y_BANKS = (0, 1, 2, 4)
        Z0 = 4
        z_ld, z_h, z_silu, z_y, z_t, z_acc = (
            [sem("z_ld0"), sem("z_ld1")], sem("z_h"), sem("z_silu"), sem("z_y"), sem("z_tmp"), sem("z_acc"))

        class Experts1:
            AT = {0: 0, 1: 1, 3: 2, 4: 3, 6: 4, 7: 5, 9: 6, 10: 7}

            def sync(self, sp):
                def load(e, k):
                    sp.dma_start(wds[k], t["wdn"][bass.ds(e, 1)].rearrange("o p k n -> (o p) k n"))\
                        .then_inc(z_ld[k], 16)
                    sp.dma_start(wrow[k][:, :], wd[1][bass.ds(e, 1)].rearrange("o n -> (o n)")
                                 .partition_broadcast(128)).then_inc(z_ld[k], 16)
                load(0, 0)
                load(1, 1)
                with sp.Fori(1, E // 2) as r:
                    for k in range(2):
                        sp.wait_ge(z_t, r * (2 * NC) + ((k - 1) * NC + Z0))
                        load(r * 2 + k, k)

            def begin_pe(self, pe):
                for c in range(NC):
                    if c >= 2:
                        pe.wait_ge(z_silu, 2 * (c - 1))
                    for b in range(2):
                        nc.tensor.matmul(ps[:, 4 * (c % 2) + b, :], wl1[:, 584 + b * 128:584 + (b + 1) * 128],
                                         h[:, c_of(c)], start=True, stop=True).then_inc(z_h, 1)
                pe.wait_ge(z_silu, 2 * NC)

            def act(self, act):
                for c in range(NC):
                    for b in range(2):
                        act.wait_ge(z_h, 2 * c + b + 1)
                        nc.scalar.activation(hidden[b][:, c_of(c)], ps[:, 4 * (c % 2) + b, :], ACT.Silu)\
                            .then_inc(z_silu, 1)

            def pe(self, pe, r, tile):
                if tile not in self.AT:
                    return
                k, c = divmod(self.AT[tile], NC)
                n = r * (2 * NC) + (k * NC + c)
                if c == 0:
                    pe.wait_ge(z_ld[k], r * 32 + 32)
                pe.wait_ge(z_t, n + (Z0 - 3))
                for b in range(2):
                    mm = nc.tensor.matmul(ps[:, Y_BANKS[c], :], wds[k][:, b, :], hidden[b][:, c_of(c)],
                                          start=(b == 0), stop=(b == 1))
                mm.then_inc(z_y, 1)

            def end_pe(self, pe):
                pe.wait_ge(z_t, E * NC + Z0)

            def begin_dve(self, dve):
                dve.sem_inc(z_t, Z0)

            def end_dve(self, dve):
                dve.wait_ge(z_acc, E * NC + Z0)

            def dve(self, dve, r, tile):
                if tile not in self.AT:
                    return
                k, c = divmod(self.AT[tile], NC)
                n = r * (2 * NC) + (k * NC + c)
                if c == 0:
                    dve.wait_ge(z_ld[k], r * 32 + 32)
                dve.wait_ge(z_acc, n + (Z0 - 3))
                dve.wait_ge(z_y, n + 1)
                nc.vector.tensor_tensor(ztmp[:, c_of(c)], ps[:, Y_BANKS[c], :], wrow[k][:, c_of(c)], ALU.mult)\
                    .then_inc(z_t, 1)

            def pool(self, pool):
                pool.sem_inc(z_acc, Z0)
                with pool.Fori(0, E) as e:
                    for c in range(NC):
                        pool.wait_ge(z_t, e * NC + (c + 1 + Z0))
                        nc.gpsimd.tensor_tensor(acc[:, c_of(c)], acc[:, c_of(c)], ztmp[:, c_of(c)], ALU.add)\
                            .then_inc(z_acc, 1)

        attention(1, 1, 1, home1, Experts1())
        if stop == 6:
            return dump_yd(nc, sem, yd[1], pool_a, out)

        z_yn, z_wo, z_a, z_out = (sem(f"z_{n}") for n in ( "yn", "wo", "sum", "out"))

        with nc.Block() as block:
            @block.sync
            def _(sp):
                load_sums(sp, 1, 1)
                for c in range(NC):
                    sp.wait_ge(z_a, c + 1)
                    sp.dma_start(out[:, c_of(c)], acc[:, c_of(c)]).then_inc(z_out, 16)
                sp.wait_ge(z_out, 16 * NC)

            @block.scalar
            def _(act):
                invert_act(act, 1)

            @block.vector
            def _(dve):
                for c in range(NC):
                    dve.wait_ge(ld_y[1][c // 2], 32)
                    dve.wait_ge(s_inv_sum, NC + c + 1)
                    nc.vector.tensor_tensor(sums_chunk(c, 0), sums_chunk(c, 0), sums_chunk(c, 1), ALU.mult)\
                        .then_inc(z_yn, 1)
                    dve.wait_ge(z_wo, c + 1)
                    nc.vector.scalar_tensor_tensor(acc[:, c_of(c)], ps[:, 4 + c, :], col("bout"), acc[:, c_of(c)],
                                                   ALU.add, ALU.add).then_inc(z_a, 1)

            @block.tensor
            def _(pe):
                for c in range(NC):
                    pe.wait_ge(z_yn, c + 1)
                    nc.tensor.matmul(ps[:, 4 + c, :], wl1[:, 448:576], sums_chunk(c, 0), start=True, stop=True)\
                        .then_inc(z_wo, 1)


def dump(nc, sem, tensor, out):
    done = sem("dumped")
    with nc.Block() as block:
        @block.sync
        def _(sp):
            sp.dma_start(out, tensor[:, :]).then_inc(done, 16)
            sp.wait_ge(done, 16)


def dump_yd(nc, sem, yd, buf, out):
    ld, done, rc, ml = sem("dump_ld"), sem("dumped"), sem("dump_r"), sem("dump_m")
    with nc.Block() as block:
        @block.sync
        def _(sp):
            for b in range(NB):
                for k in range(2):
                    o = (2 * b + k) * T
                    sp.dma_start(buf[:, o:o + T], yd[b, :, k]).then_inc(ld, 16)
            sp.wait_ge(ml, 2)
            for b in range(NB):
                sp.dma_start(out[:, b * T:(b + 1) * T], buf[:, 2 * b * T:(2 * b + 1) * T]).then_inc(done, 16)
            sp.wait_ge(done, 32)

        @block.vector
        def _(dve):
            dve.wait_ge(ld, 64)
            for b in range(NB):
                y, w = buf[:, 2 * b * T:(2 * b + 1) * T], buf[:, (2 * b + 1) * T:(2 * b + 2) * T]
                nc.vector.reciprocal(w, w).then_inc(rc, 1)
                dve.wait_ge(rc, b + 1)
                nc.vector.tensor_tensor(y, y, w, ALU.mult).then_inc(ml, 1)


def kernel(**inputs):
    import numpy as _np
    import concourse.bacc as _bacc
    from concourse import mybir as _mybir
    from concourse.bass_utils import run_bass_kernel_spmd as _run

    a = {k: _np.asarray(v) for k, v in inputs.items()}
    f = _np.float32

    def stack(mats):
        return _np.ascontiguousarray(_np.stack(mats, axis=1))

    swap = _np.arange(128) ^ 1
    kv = a["L1_attn_Wkvb"].reshape(KVL, KVH * HD, 2)
    wl1 = _np.zeros((128, 848), f)
    wl1[:, 0:64] = a["L1_attn_Wqa"]
    wl1[0:QL, 64:192] = a["L1_attn_Wqb"]
    wl1[0:QL, 192:320] = a["L1_attn_Wqb"][:, swap]
    wl1[:, 320:352] = a["L1_attn_Wkva"]
    wl1[0:KVL, 352:384] = kv[:, :, 0]
    wl1[0:KVL, 384:416] = kv[:, swap[0:32], 0]
    wl1[0:KVL, 416:448] = kv[:, :, 1]
    wl1[:, 448:576] = a["L1_attn_Wout"]
    wl1[:, 576:584] = a["L1_ffn_w_router"].T
    wl1[:, 584:840] = a["L1_ffn_w_gate"].T
    wl1[:, 840:848] = a["L0_ffn_gate_W"]
    i = _np.arange(128)
    head = (i[:, None] // HD == i[None, :] // HD).astype(f) / f(HD)
    cst = stack([_np.full((128, 128), 1.0 / 128, f), head, _np.eye(128, dtype=f),
                 (i[:, None] <= i[None, :]).astype(f), _np.ones((128, 128), f)])
    mask = _np.where(i[None, :] > i[:, None], f(NEG), f(0.0)).astype(f)
    inv = (f(1.0) / f(10000.0) ** (_np.arange(0, HD, 2, dtype=f) / f(HD))).astype(f)
    ang = (_np.arange(T, dtype=f)[None, :] * inv[(i % HD) // 2][:, None]).astype(f).astype(_np.float64)
    cos, sin = _np.cos(ang), _np.sin(ang) * _np.where(i % 2 == 0, -1.0, 1.0)[:, None]
    rope = stack([(cos * SCALE).astype(f), (sin * SCALE).astype(f)])
    ropek = stack([_np.concatenate([tab.astype(f)[0:32, (c % 2) * CH:(c % 2 + 1) * CH] for c in range(NC)])
                   for tab in (cos, sin)])
    column = {"mg": "L0_attn_mg", "mr": "L0_attn_mr", "mk": "L0_attn_mk", "mv": "L0_attn_mv",
              "bg": "L0_attn_Wg_b", "br": "L0_attn_Wr_b", "bk": "L0_attn_Wk_b", "bv": "L0_attn_Wv_b",
              "bo": "L0_attn_Wo_b", "w": "L0_attn_w", "u": "L0_attn_u", "ln1g": "L0_ffn_ln1_g",
              "ln1b": "L0_ffn_ln1_b", "ln2g": "L0_ffn_ln2_g", "ln2b": "L0_ffn_ln2_b", "bq": "L0_ffn_bq",
              "bkf": "L0_ffn_bk", "bp": "L0_ffn_bp", "bout": "L1_attn_bout"}
    arrays = {
        "xT": _np.ascontiguousarray(a["L0_attn_x"].reshape(N, D).T),
        "cols": _np.ascontiguousarray(_np.stack([a[column[n]].reshape(128) for n in COLS], axis=1)),
        "wl0": stack([a[f"L0_attn_W{n}_w"].T for n in "grkvo"]),
        "wf": stack([a[f"L0_ffn_W{n}"] for n in "qkvp"]),
        "wl1": wl1, "cst": cst, "mask": stack([mask, mask.T]), "rope": rope, "ropek": ropek,
        "bv": a["L0_ffn_bv"], "gate_b": a["L0_ffn_gate_b"], "rev": (E - _np.arange(E)).astype(f),
        "w1": a["L0_ffn_exp_W1"],
        "w2": _np.ascontiguousarray(a["L0_ffn_exp_W2"].reshape(E, 4, 128, 128).transpose(0, 2, 1, 3)),
        "b1": _np.ascontiguousarray(a["L0_ffn_exp_b1"].reshape(E, 4, 128).transpose(0, 2, 1)),
        "b2": _np.ascontiguousarray(a["L0_ffn_exp_b2"].reshape(E, 128, 1)),
        "wdn": _np.ascontiguousarray(a["L1_ffn_w_down"].transpose(0, 2, 1).reshape(E, 2, 128, 128)
                                     .transpose(0, 2, 1, 3)),
    }
    nc = _bacc.Bacc("TRN2", target_bir_lowering=False, num_devices=1)
    t = {n: nc.dram_tensor(f"in_{n}", v.shape, _mybir.dt.from_np(v.dtype), kind="ExternalInput").ap()
         for n, v in arrays.items()}
    out = nc.dram_tensor("out_T", (128, N), F32, kind="ExternalOutput").ap()
    build_program(nc, t, out)
    r = _run(nc, [{f"in_{n}": v for n, v in arrays.items()}], core_ids=[0])
    return _np.ascontiguousarray(r.results[0]["out_T"].T).reshape(NB, T, D)
```

```python
from contextlib import ExitStack

import numpy as np

import concourse.bass as bass
from concourse import mybir

F32 = mybir.dt.float32
BF16 = mybir.dt.bfloat16
F32R = mybir.dt.float32r
ACT = mybir.ActivationFunctionType
ALU = mybir.AluOpType
AX = mybir.AxisListType

D = 128
NB, T = 2, 1024
N = NB * T
CH = 512
NC = N // CH
TB = N // 128
KB = T // 128
H, HD = 16, 8
G = 4
E = 8
HID0, HID1 = 512, 256
CAP = 320.0
KVH = 4
QL, KVL = 64, 32
PARTS = 3
ROWS = PARTS * PARTS * HD
MROWS = ROWS + PARTS
EPS = 1e-5
NEG = -1e30
SCALE = HD ** -0.5

LOG_EXP = "natural_log_exp_and_others"

COLS = ["mg", "mr", "mk", "mv", "bg", "br", "bk", "bv", "bo", "w", "u", "ln1g", "ln1b", "ln2g", "ln2b",
        "bq", "bkf", "bp", "bout"]
COL = {n: i for i, n in enumerate(COLS)}


def build_program(nc, t, out):
    ctx = ExitStack()
    with ctx:
        def sb(name, shape, dt=F32):
            return ctx.enter_context(nc.sbuf_tensor(name, shape, dt))

        def sem(name):
            return ctx.enter_context(nc.semaphore(name))

        ps = ctx.enter_context(nc.psum_tensor("ps", [128, 8, CH], F32))

        xT = sb("xT", [128, N])
        xn = sb("xn", [128, N])
        xs = sb("xs", [128, N])
        spare = sb("spare", [128, N])
        acc = sb("acc", [128, N])
        cols = sb("cols", [128, len(COLS)])
        wl0 = sb("wl0", [128, 5, 128])
        wf = sb("wf", [128, 4, 128])
        cst = sb("cst", [128, 5, 128])
        idb = sb("idb", [128, 128], BF16)
        mskb = sb("mskb", [128, 2, 128], BF16)
        eps = sb("eps", [128, 1])
        pool_a = sb("pool_a", [128, 8192])
        vst = sb("vst", [128, 3, KB * G * 32])
        osb = sb("osb", [128, 3, T])
        small = sb("small", [128, 1024])
        wl1 = sb("wl1", [128, 848])
        h = sb("h", [128, N])

        def attention_scratch(own, l):
            return (own.enter_context(nc.sbuf_tensor(f"shortp{l}", [128, 4096], F32)),
                    own.enter_context(nc.sbuf_tensor(f"pool_b{l}", [128, 12288], F32)))
        region = ExitStack()
        shortp, pool_b = attention_scratch(region, 0)

        meanM, headM, ident, later, ones = (cst[:, i, :] for i in range(5))

        def dram(name, shape, dt=F32):
            return nc.dram_tensor(name, shape, dt, kind="Internal").ap()
        qd = [dram(f"qd{l}", [NB, H, PARTS, HD, T], BF16) for l in range(2)]
        kd = [dram("kd0", [NB, H, PARTS, HD, T], BF16), dram("kd1", [NB, KVH, PARTS, HD, T], BF16)]
        yd = [dram(f"yd{l}", [NB, H, 2, HD, T]) for l in range(2)]
        wd = [dram(f"wd{l}", [E, N]) for l in range(2)]

        def c_of(c):
            return slice(c * CH, (c + 1) * CH)

        def full(buf, k):
            return buf[:, k * N:(k + 1) * N]

        def xn_chunk(c):
            return xn[:, c_of(c)]

        def col(name):
            return cols[:, COL[name]:COL[name] + 1]

        s_mean, s_cent, s_sq, s_var, s_log, s_inv, s_normed, s_scaled = (
            sem(f"norm_{n}") for n in ("mean", "centred", "squared", "variance", "log_variance", "inverse", "done",
                                       "scaled"))

        class Norm:
            def __init__(self, k, src, cen, sq, dst, matrix, banks, gain=None, bias=None, scaled=0):
                self.base = NC * k
                self.scaled = NC * scaled
                self.src, self.cen, self.sq, self.dst, self.matrix = src, cen, sq, dst, matrix
                self.banks, self.gain, self.bias = banks, gain, bias

        def norm_pe(pe, L, ready=None):
            for c in range(NC):
                if ready is not None:
                    pe.wait_ge(ready, c + 1)
                if c >= 2:
                    pe.wait_ge(s_cent, L.base + c - 1)
                nc.tensor.matmul(ps[:, L.banks + c % 2, :], L.matrix, L.src(c), start=True, stop=True)\
                    .then_inc(s_mean, 1)
            for c in range(NC):
                pe.wait_ge(s_sq, L.base + c + 1)
                if c >= 2:
                    pe.wait_ge(s_log, L.base + c - 1)
                nc.tensor.matmul(ps[:, L.banks + 2 + c % 2, :], L.matrix, L.sq(c), start=True, stop=True)\
                    .then_inc(s_var, 1)

        def norm_dve(dve, L):
            for c in range(NC):
                dve.wait_ge(s_mean, L.base + c + 1)
                nc.vector.tensor_tensor(L.cen(c), L.src(c), ps[:, L.banks + c % 2, :], ALU.subtract)\
                    .then_inc(s_cent, 1)
            for c in range(NC):
                dve.wait_ge(s_inv, L.base + c + 1)
                if L.gain is None:
                    nc.vector.tensor_tensor(L.dst(c), L.cen(c), L.sq(c), ALU.mult).then_inc(s_normed, 1)
                else:
                    nc.vector.scalar_tensor_tensor(L.dst(c), L.cen(c), L.gain, L.sq(c), ALU.mult, ALU.mult)\
                        .then_inc(s_scaled, 1)
                    dve.wait_ge(s_scaled, L.scaled + c + 1)
                    nc.vector.tensor_scalar(L.dst(c), L.dst(c), L.bias, None, ALU.add).then_inc(s_normed, 1)

        def norm_act(act, L):
            for c in range(NC):
                act.wait_ge(s_cent, L.base + c + 1)
                nc.scalar.activation(L.sq(c), L.cen(c), ACT.Square).then_inc(s_sq, 1)
            for c in range(NC + 1):
                if c < NC:
                    act.wait_ge(s_var, L.base + c + 1)
                    nc.scalar.activation(L.sq(c), ps[:, L.banks + 2 + c % 2, :], ACT.Ln, bias=eps[:, 0:1])\
                        .then_inc(s_log, 1)
                if c >= 1:
                    act.wait_ge(s_log, L.base + c)
                    nc.scalar.activation(L.sq(c - 1), L.sq(c - 1), ACT.Exp, scale=-0.5).then_inc(s_inv, 1)

        class Split:
            def __init__(self, name, f, parts, dst, after=None):
                self.f, self.parts, self.dst = f, parts, dst
                self.base, self.base_stored = (NC, 16 * PARTS * NC) if after else (0, 0)
                self.full, self.hi, self.r1, self.mid, self.lo, self.stored = (
                    (after.full, after.hi, after.r1, after.mid, after.lo, after.stored) if after else
                    (sem(f"{name}_{s}") for s in ("full", "hi", "r1", "mid", "lo", "stored")))

        def remainder(dve, S, c):
            dve.wait_ge(S.hi, S.base + c + 1)
            nc.vector.tensor_tensor(S.f(c), S.f(c), S.parts(0, c), ALU.subtract).then_inc(S.r1, 1)

        def last_part(dve, S, c):
            dve.wait_ge(S.mid, S.base + c + 1)
            nc.vector.tensor_tensor(S.parts(2, c), S.f(c), S.parts(1, c), ALU.subtract).then_inc(S.lo, 1)

        def first_part(act, S, c):
            act.wait_ge(S.full, S.base + c + 1)
            nc.scalar.copy(S.parts(0, c), S.f(c)).then_inc(S.hi, 1)

        def second_part(act, S, c):
            act.wait_ge(S.r1, S.base + c + 1)
            nc.scalar.copy(S.parts(1, c), S.f(c)).then_inc(S.mid, 1)

        def split_store(sp, S, c):
            sp.wait_ge(S.lo, S.base + c + 1)
            half = slice((c % 2) * CH, (c % 2 + 1) * CH)
            for p in range(PARTS):
                sp.dma_start(S.dst[c // 2, :, p, :, half], S.parts(p, c)).then_inc(S.stored, 16)

        ROLL = 3
        UNITS = NB * G
        BLOCKS = [(PARTS * HD * j, j, PARTS - j) for j in range(PARTS)] + \
                 [(PARTS * HD * j + HD * (PARTS - j), 0, j) for j in range(1, PARTS)]
        NLOAD = PARTS + len(BLOCKS)

        def attention_semaphores(l):
            return {n: sem(f"a{l}_{n}") for n in (
                "a_mm", "a_red", "folded", "hi", "r1", "mid", "parts", "turned", "m_copied",
                "m_set0", "m_set1", "m_set2", "v_set", "b_mm", "exp", "pv", "evac",
                "st0", "st1", "st2", "ld0", "ld1", "ld2")}

        def stacks():
            return (pool_b[:, 0:6144].bitcast(BF16).rearrange("p (s i n) -> p s i n", s=ROLL, i=G),
                    pool_b[:, 6144:12288].bitcast(BF16).rearrange("p (s i n) -> p s i n", s=ROLL, i=G))

        def load_stacks(sp, l, kh, s, u, slot):
            qst, kst = stacks()
            qrows = qd[l].rearrange("b h a d n -> (b h a d) n")
            krows = kd[l].rearrange("b h a d n -> (b h a d) n")
            for j in range(PARTS):
                r = PARTS * HD * j
                sp.dma_start(qst[r:r + PARTS * HD, slot],
                             qrows[bass.ds(u * (G * PARTS * HD), G * PARTS * HD), :]
                             .rearrange("(i x) n -> x i n", i=G)).then_inc(s[f"ld{slot}"], 16)
            for r, part, parts in BLOCKS:
                sp.dma_start(kst[r:r + parts * HD, slot, 0:kh],
                             krows[bass.ds(u * (kh * PARTS * HD), kh * PARTS * HD), :]
                             .rearrange("(i x) n -> x i n", i=kh)[HD * part:HD * (part + parts)])\
                    .then_inc(s[f"ld{slot}"], 16)

        sems0 = attention_semaphores(0)

        f = [full(pool_b, k) for k in range(6)]
        fa = [full(pool_a, k) for k in range(4)]
        k_ones = sem("k_ones")
        shifted = sem("shifted")
        n0 = Norm(0, lambda c: xT[:, c_of(c)], lambda c: f[0][:, c_of(c)], lambda c: f[1][:, c_of(c)],
                  xn_chunk, meanM, 0)
        n1 = Norm(1, xn_chunk, lambda c: f[0][:, c_of(c)], lambda c: f[1][:, c_of(c)],
                  lambda c: h[:, c_of(c)], meanM, 0, gain=col("ln1g"), bias=col("ln1b"), scaled=0)
        partb = pool_a[:, 0:PARTS * N].bitcast(BF16).rearrange("p (k a n) -> p k a n", k=2, a=PARTS)
        qs_ = Split("sq", lambda c: f[2][:, c_of(c)], lambda p, c: partb[:, 0, p, c_of(c)], qd[0])
        ks_ = Split("sk", lambda c: fa[3][:, c_of(c)], lambda p, c: partb[:, 1, p, c_of(c)], kd[0])
        bvb, gbb, rev = small[:, 0:128], small[:, 128:136], small[:, 136:144]
        dec, hbg = small[:, 144:146], small[:, 146:147]
        msk32 = osb[:, 1, 0:256].rearrange("p (k n) -> p k n", k=2)

        ld_x, ld_w, one_eps = sem("ld_x"), sem("ld_w"), sem("eps_set")
        NLD = 8
        qk_mm, v_mm = sem("qk_mm"), sem("v_mm")
        v_ones = sem("v_ones")
        home0 = acc[:, :].rearrange("p (b g k x) -> p b g k x", b=NB, g=G, k=KB)

        with nc.Block() as block:
            @block.sync
            def _(sp):
                for c in range(NC):
                    sp.dma_start(xT[:, c_of(c)], t["xT"][:, c_of(c)]).then_inc(ld_x, 16)
                sp.wait_ge(ld_x, 16 * (NC + 1))
                sp.dma_start(wf[:, :, :], t["wf"]).then_inc(ld_w, 16)
                sp.dma_start(bvb, t["bv"].partition_broadcast(128)).then_inc(ld_w, 16)
                sp.dma_start(gbb, t["gate_b"].partition_broadcast(128)).then_inc(ld_w, 16)
                sp.dma_start(rev, t["rev"].partition_broadcast(128)).then_inc(ld_w, 16)
                for c in range(NC):
                    if c == NC // NB:
                        sp.wait_ge(qs_.stored, 16 * PARTS * c)
                        sp.wait_ge(ks_.stored, 16 * PARTS * c)
                        sp.wait_ge(v_ones, 2)
                        load_stacks(sp, 0, G, sems0, 0, 0)
                    split_store(sp, qs_, c)
                    split_store(sp, ks_, c)
                sp.wait_ge(qs_.stored, 16 * PARTS * NC)
                sp.wait_ge(ks_.stored, 16 * PARTS * NC)

            @block.gpsimd
            def _(pool):
                nc.gpsimd.memset(vst[:, :, :], 1.0).then_inc(v_ones, 1)
                pool.wait_ge(v_ones, 1)
                nc.gpsimd.memset(pool_b[64:MROWS, 6144:12288].bitcast(BF16), 1.0).then_inc(v_ones, 1)

            @block.scalar
            def _(act):
                act.dma_start(cst[:, :, :], t["cst"]).then_inc(ld_x, 16)
                act.wait_ge(ld_x, 16 * (NC + 1))
                act.dma_start(cols[:, :], t["cols"]).then_inc(ld_w, 16)
                act.dma_start(wl0[:, :, :], t["wl0"]).then_inc(ld_w, 16)
                act.dma_start(wl1[:, :], t["wl1"]).then_inc(ld_w, 16)
                act.dma_start(msk32, t["mask"]).then_inc(ld_w, 16)
                nc.scalar.preload_act_table_set(LOG_EXP)
                act.wait_ge(one_eps, 1)
                norm_act(act, n0)
                norm_act(act, n1)
                for c in range(NC):
                    act.wait_ge(qk_mm, c + 1)
                    nc.scalar.activation(ks_.f(c), ps[:, 2 * (c % 2) + 1, :], ACT.Identity, bias=col("bkf"))\
                        .then_inc(ks_.full, 1)
                    for part in (first_part, second_part):
                        for S in (qs_, ks_):
                            part(act, S, c)

            @block.vector
            def _(dve):
                nc.vector.memset(eps[:, :], EPS).then_inc(one_eps, 1)
                dve.wait_ge(ld_x, 16 * (NC + 1))
                norm_dve(dve, n0)
                dve.wait_ge(ld_w, 16 * NLD)
                nc.vector.tensor_copy(idb[:, :], ident)
                nc.vector.tensor_copy(mskb[:, :, :], msk32)
                norm_dve(dve, n1)
                for c in range(NC):
                    b = 2 * (c % 2)
                    dve.wait_ge(qk_mm, c + 1)
                    nc.vector.tensor_scalar(qs_.f(c), ps[:, b, :], col("bq"), SCALE, ALU.add, ALU.mult)\
                        .then_inc(qs_.full, 1)
                    remainder(dve, qs_, c)
                    remainder(dve, ks_, c)
                    dve.wait_ge(v_mm, c + 1)
                    nc.vector.tensor_tensor(home0[:, c // 2, :, 4 * (c % 2):4 * (c % 2 + 1), :],
                                            ps[:, 4 + c, :].rearrange("p (k g x) -> p g k x", k=4, g=G),
                                            bvb.rearrange("p (g x) -> p g x", g=G).unsqueeze(2)
                                            .to_broadcast([128, G, 4, 32]), ALU.add)
                    last_part(dve, qs_, c)
                    last_part(dve, ks_, c)

            @block.tensor
            def _(pe):
                pe.wait_ge(ld_x, 16 * (NC + 1))
                norm_pe(pe, n0)
                pe.wait_ge(s_log, n0.base + NC)
                norm_pe(pe, n1, ready=s_normed)
                pe.wait_ge(s_log, n1.base + NC)
                pe.wait_ge(ld_w, 16 * NLD)
                for c in range(NC):
                    b = 2 * (c % 2)
                    pe.wait_ge(s_normed, n1.base + c + 1)
                    if c >= 2:
                        pe.wait_ge(ks_.full, c - 1)
                        pe.wait_ge(qs_.full, c - 1)
                    for j in range(2):
                        ins = nc.tensor.matmul(ps[:, b + j, :], wf[:, j, :], h[:, c_of(c)], start=True, stop=True)
                    ins.then_inc(qk_mm, 1)
                    for k in range(4):
                        tb = 4 * c + k
                        ins = nc.tensor.matmul(ps[:, 4 + c, k * 128:(k + 1) * 128], h[:, tb * 128:(tb + 1) * 128],
                                               wf[:, 2, :], start=True, stop=True)
                    ins.then_inc(v_mm, 1)


        def sums(b):
            buf = (h[:, :], fa[0])[b]
            return buf[:, 0:T], buf[:, T:2 * T]

        ld_y = [[sem(f"ld_y{l}{b}") for b in range(NB)] for l in range(2)]

        def load_sums(sp, l, b):
            for k, dst in enumerate(sums(b)):
                sp.dma_start(dst, yd[l][b, :, k]).then_inc(ld_y[l][b], 16)

        def sums_chunk(c, k):
            return sums(c // 2)[k][:, (c % 2) * CH:(c % 2 + 1) * CH]

        def attention(l, kh, vw, home, s, beside=None):
            qst, kst = stacks()
            prob = (pool_a[:, :].rearrange("p (s i n) -> p s i n", s=2, i=G),
                    shortp[:, :].rearrange("p (s i n) -> p s i n", s=2, i=G))
            vals = vst[:, :, 0:KB * vw * 32].rearrange("p s (k i w) -> p s k i w", k=KB, i=vw)
            lowmax = small[:, 256:288]
            highmax = small[:, 288:304]
            rem = small[:, 304:336]
            mpart = small[:, 336:384].bitcast(BF16).rearrange("p (a c) -> p a c", a=PARTS)
            mT = small[:, 384:576].bitcast(BF16).rearrange("p (s n) -> p s n", s=ROLL)
            turned = ps[:, 6, 0:64].bitcast(BF16)
            TILES = [(i, qb, hf) for i in range(G) for qb in range(KB) for hf in range(1 + qb // 4)]
            NT = len(TILES)
            A_BANKS = (3, 6, 7)
            RING = len(A_BANKS)
            NP = KB // 2
            NE = KB * G
            A_SPREAD = 27
            TURN = NE - 1
            PV0, EXP0, EVAC0, RED0 = 4, 2, 1, 3
            NH = NT // G
            PEEL = UNITS // ROLL * ROLL

            def all_units(eng, body):
                with eng.Fori(0, UNITS // ROLL) as r:
                    for k in range(ROLL):
                        body(r * ROLL + k, k, r, False)
                for k in range(UNITS - PEEL):
                    body(PEEL + k, k, UNITS // ROLL, k == UNITS - PEEL - 1)

            with nc.Block() as block:
                @block.sync
                def _(sp):
                    yrows = yd[l].rearrange("b h k d n -> (b h k d) n")

                    def set_max(u, slot):
                        sp.wait_ge(s["m_copied"], u + 1)
                        sp.dma_start(qst[ROWS:MROWS, slot].rearrange("a i n -> a (i n)"), mT[0:96, slot, :])\
                            .then_inc(s[f"m_set{slot}"], 16)

                    for k in range(ROLL):
                        sp.sem_inc(s[f"st{k}"], 16)
                    if beside:
                        beside.sync(sp)
                    set_max(0, 0)

                    def body(u, slot, r, last):
                        if not isinstance(u, int):
                            sp.wait_ge(s["pv"], u * KB + PV0)
                            load_stacks(sp, l, kh, s, u + 2, (slot + 2) % ROLL)
                        if not last:
                            set_max(u + 1, (slot + 1) % ROLL)
                        if last:
                            for k in range(ROLL):
                                sp.wait_ge(s[f"st{k}"], 16 + 16 * G * ((G - k + ROLL - 1) // ROLL))
                            load_sums(sp, l, 0)
                        sp.wait_ge(s["evac"], u + (EVAC0 + 1))
                        for i in range(G):
                            sp.dma_start(yrows[bass.ds(u * (G * 2 * HD) + i * 2 * HD, 2 * HD), :],
                                         osb[32 * i:32 * i + 2 * HD, slot, :]).then_inc(s[f"st{slot}"], 16)
                    all_units(sp, body)
                    for k in range(ROLL):
                        sp.wait_ge(s[f"st{k}"], 16 + 16 * G * ((UNITS - k + ROLL - 1) // ROLL))

                @block.gpsimd
                def _(pool):
                    if l == 0:
                        for b in range(NB):
                            o = b * T
                            nc.gpsimd.tensor_copy(xs[:, o + 1:o + T], xn[:, o:o + T - 1]).then_inc(shifted, 1)
                            pool.wait_ge(shifted, 2 * b + 1)
                            nc.gpsimd.tensor_copy(xs[:, o:o + 1], xn[:, o + T - 1:o + T]).then_inc(shifted, 1)
                            pool.wait_ge(shifted, 2 * b + 2)

                    if beside:
                        beside.pool(pool)

                @block.scalar
                def _(act):
                    nc.scalar.preload_act_table_set(LOG_EXP)
                    load_stacks(act, l, kh, s, 1, 1)
                    act.sem_inc(s["exp"], EXP0)

                    def set_values(u, slot):
                        n = KB * vw
                        nc.scalar.copy(vst[:, slot, 0:n * 32].rearrange("p (k w) -> p k w", k=n)[:, :, 0:HD],
                                       home[:, bass.ds(u * (n * HD), n * HD)].rearrange("p (k w) -> p k w", k=n))\
                            .then_inc(s["v_set"], 1)
                    set_values(0, 0)
                    set_values(1, 1)

                    def body(u, slot, r, last):
                        if not isinstance(u, int):
                            act.wait_ge(s["pv"], u * KB + PV0)
                            set_values(u + 2, (slot + 2) % ROLL)
                        for e in range(NE):
                            p, i, kind = e // (2 * G), e // 2 % G, e % 2
                            if i == 0:
                                act.wait_ge(s["pv"], u * KB + (2 * p + 1 + kind))
                            w = T - 128 * (KB - 1 - p if kind else p)
                            act.wait_ge(s["b_mm"], u * NE + (e + 1))
                            nc.scalar.activation(
                                prob[kind][:, p % 2, i, 0:w],
                                ps[:, 2 * kind:2 * kind + 2, :].rearrange("p b n -> p (b n)")[:, 0:w],
                                ACT.Exp).then_inc(s["exp"], 1)
                    all_units(act, body)

                @block.vector
                def _(dve):
                    def tile_max(count, n, low, high):
                        i, qb, hf = TILES[n]
                        w = min(CH, (qb + 1) * 128 - hf * CH)
                        dve.wait_ge(s["a_mm"], count + (n + 1))
                        nc.vector.tensor_reduce(high(i, qb - 4) if hf else low(i, qb), ps[:, A_BANKS[n % RING], 0:w],
                                                AX.X, ALU.max, negate=True).then_inc(s["a_red"], 1)

                    def split_max(u, slot):
                        dve.wait_ge(s["a_red"], u * NT + (NT + RED0))
                        late = lowmax.rearrange("p (i k) -> p i k", i=G)[:, :, 4:KB]
                        nc.vector.tensor_tensor(late, late, highmax.rearrange("p (i k) -> p i k", i=G), ALU.min)\
                            .then_inc(s["folded"], 1)
                        dve.wait_ge(s["folded"], u + 1)
                        nc.vector.tensor_copy(mpart[:, 0, :], lowmax).then_inc(s["hi"], 1)
                        dve.wait_ge(s["hi"], u + 1)
                        nc.vector.tensor_tensor(rem, lowmax, mpart[:, 0, :], ALU.subtract).then_inc(s["r1"], 1)
                        dve.wait_ge(s["r1"], u + 1)
                        nc.vector.tensor_copy(mpart[:, 1, :], rem).then_inc(s["mid"], 1)
                        dve.wait_ge(s["mid"], u + 1)
                        nc.vector.tensor_tensor(mpart[:, 2, :], rem, mpart[:, 1, :], ALU.subtract)\
                            .then_inc(s["parts"], 1)
                        dve.wait_ge(s["turned"], u + 1)
                        nc.vector.tensor_copy(mT[0:96, slot, :], turned[0:96, :]).then_inc(s["m_copied"], 1)

                    dve.sem_inc(s["evac"], EVAC0)
                    dve.sem_inc(s["a_red"], RED0)
                    if beside:
                        beside.begin_dve(dve)
                    with dve.Fori(0, G) as i:
                        for n in range(NH):
                            tile_max(i * NH, n, lambda _, qb: lowmax[:, bass.ds(i * KB + qb, 1)],
                                     lambda _, qb: highmax[:, bass.ds(i * 4 + qb, 1)])
                            if beside:
                                beside.dve(dve, i, n)
                    split_max(0, 0)
                    if beside:
                        beside.end_dve(dve)

                    def body(u, slot, r, last):
                        if not last:
                            for n in range(NT):
                                tile_max((u + 1) * NT, n, lambda i, qb: lowmax[:, i * KB + qb:i * KB + qb + 1],
                                         lambda i, qb: highmax[:, i * 4 + qb:i * 4 + qb + 1])
                            split_max(u + 1, (slot + 1) % ROLL)
                        dve.wait_ge(s[f"st{slot}"], r * (16 * G) + 16)
                        dve.wait_ge(s["pv"], u * KB + (KB + PV0))
                        nc.vector.tensor_copy(osb[:, slot, :], ps[:, 4:6, :].rearrange("p b n -> p (b n)"))\
                            .then_inc(s["evac"], 1)
                    all_units(dve, body)

                @block.tensor
                def _(pe):
                    def tile_a(count, slot, head, n):
                        _, qb, hf = TILES[n]
                        w = min(CH, (qb + 1) * 128 - hf * CH)
                        pe.wait_ge(s["a_red"], count + (n - RING + 1 + RED0))
                        diagonal = hf == qb // 4
                        bank = A_BANKS[n % RING]
                        if isinstance(head, int):
                            queries = qst[0:ROWS, slot, head, qb * 128:(qb + 1) * 128]
                            keys = kst[0:ROWS, slot, head if kh > 1 else 0, hf * CH:hf * CH + w]
                        else:
                            flat = lambda st: st[0:ROWS, slot].rearrange("p i n -> p (i n)")
                            queries = flat(qst)[:, bass.ds(head * T + qb * 128, 128)]
                            keys = flat(kst)[:, bass.ds(head * T + hf * CH, w)] if kh > 1 else \
                                kst[0:ROWS, slot, 0, hf * CH:hf * CH + w]
                        mm = nc.tensor.matmul(ps[:, bank, 0:w], queries, keys, start=True, stop=True)
                        if diagonal:
                            mm = nc.tensor.matmul(ps[:, bank, w - 128:w], idb[:, :], mskb[:, 0, :],
                                                  start=False, stop=True, skip_group_check=True)
                        mm.then_inc(s["a_mm"], 1)

                    def turn(u):
                        pe.wait_ge(s["parts"], u + 1)
                        nc.tensor.transpose(turned[0:96, :], mpart.rearrange("p a c -> p (a c)"), idb[:, :])\
                            .then_inc(s["turned"], 1)

                    def multiply(u, slot, p, kind, halves=(0, 1)):
                        kb = KB - 1 - p if kind else p
                        if p == 0 and kind == 0 and halves[0] == 0:
                            pe.wait_ge(s["evac"], u + EVAC0)
                        if halves[0] == 0:
                            pe.wait_ge(s["exp"], u * NE + (2 * G * p + 2 * G - 1 + kind + EXP0))
                        for hf in halves if kind == 0 else (1,):
                            lo = max(0, kb * 128 - hf * CH)
                            for i in range(G):
                                p0 = hf * CH + lo - kb * 128
                                mm = nc.tensor.matmul(ps[32 * i:32 * i + 32, 4 + hf, lo:CH],
                                                      vals[:, slot, kb, i if vw > 1 else 0, :],
                                                      prob[kind][:, p % 2, i, p0:p0 + CH - lo],
                                                      start=(kb == 0), stop=(kb == (4 if hf else 3)),
                                                      tile_position=(0, 32 * i), skip_group_check=True)
                        if kind or halves[-1] == 1:
                            mm.then_inc(s["pv"], 1)

                    pe.sem_inc(s["pv"], PV0)
                    pe.wait_ge(s["ld0"], 16 * NLOAD)
                    with pe.Fori(0, G) as i:
                        for n in range(NH):
                            tile_a(i * NH, 0, i, n)
                            if beside:
                                beside.pe(pe, i, n)
                    turn(0)
                    if beside:
                        beside.end_pe(pe)

                    def body(u, slot, r, last):
                        nxt = (slot + 1) % ROLL
                        if not last:
                            pe.wait_ge(s[f"ld{nxt}"], (r + (2 if nxt == 0 else 1)) * (16 * NLOAD))
                            pe.wait_ge(s["m_copied"], u + 1)
                        pe.wait_ge(s[f"m_set{slot}"], r * 16 + 16)
                        pe.wait_ge(s["v_set"], u + 1)
                        for e in range(NE):
                            p, i, kind = e // (2 * G), e // 2 % G, e % 2
                            kb = KB - 1 - p if kind else p
                            w = T - 128 * kb
                            pe.wait_ge(s["exp"], u * NE + (e - 1 + EXP0))
                            for c0 in range(0, w, CH):
                                cw = min(CH, w - c0)
                                mm = nc.tensor.matmul(
                                    ps[:, 2 * kind + c0 // CH, 0:cw],
                                    kst[0:MROWS, slot, i if kh > 1 else 0, kb * 128:(kb + 1) * 128],
                                    qst[0:MROWS, slot, i, kb * 128 + c0:kb * 128 + c0 + cw], start=True, stop=True)
                                if c0 == 0:
                                    mm = nc.tensor.matmul(ps[:, 2 * kind, 0:128], idb[:, :], mskb[:, 1, :],
                                                          start=False, stop=True, skip_group_check=True)
                            mm.then_inc(s["b_mm"], 1)
                            if not last:
                                for n in range(e * NT // A_SPREAD, min((e + 1) * NT // A_SPREAD, NT)):
                                    tile_a((u + 1) * NT, nxt, TILES[n][0], n)
                                if e == TURN:
                                    turn(u + 1)
                            if p >= 1 and kind and i in (1, 2):
                                multiply(u, slot, p - 1, 0, (i - 1,))
                            if 1 <= p < NP - 1 and kind and i == 3:
                                multiply(u, slot, p - 1, 1)
                        multiply(u, slot, NP - 2, 1)
                        multiply(u, slot, NP - 1, 0)
                        multiply(u, slot, NP - 1, 1)
                    all_units(pe, body)

        attention(0, G, G, acc, sems0)
        region.close()
        region = ExitStack()

        def typed(name, shape, dt=F32R):
            return region.enter_context(nc.sbuf_tensor(name, shape, dt))
        h_round, h_rest = typed("h_round", [128, N]), typed("h_rest", [128, N])
        mid_round, mid_rest = typed("mid_round", [128, 4, CH]), typed("mid_rest", [128, 4, CH])
        w_parts = typed("w_parts", [128, 2, 4, 512])
        wbc = [typed(f"wbc{k}", [128, N], F32) for k in range(2)]

        def top_one(dve_step, values, onehot, m, eq, sc, cm):
            v3 = lambda ap: ap.rearrange("p (t e) -> p t e", e=E)
            wide = lambda ap: ap.unsqueeze(2).to_broadcast([128, TB, E])
            dve_step(nc.vector.tensor_reduce(m, v3(values), AX.X, ALU.max))
            dve_step(nc.vector.tensor_tensor(v3(eq), v3(values), wide(m), ALU.is_equal))
            dve_step(nc.vector.tensor_tensor(v3(sc), v3(eq), rev.unsqueeze(1).to_broadcast([128, TB, E]), ALU.mult))
            dve_step(nc.vector.tensor_reduce(cm, v3(sc), AX.X, ALU.max))
            dve_step(nc.vector.tensor_tensor(v3(onehot), v3(sc), wide(cm), ALU.is_equal))

        rt = lambda k: osb[:, :, :].rearrange("p s n -> p (s n)")[:, 128 * k:128 * (k + 1)]
        rs = lambda k: small[:, 640 + TB * k:640 + TB * (k + 1)]
        v3 = lambda ap: ap.rearrange("p (t e) -> p t e", e=E)
        wide = lambda ap: ap.unsqueeze(2).to_broadcast([128, TB, E])

        def route_pe(pe, weight, done):
            for tb in range(TB):
                mm = nc.tensor.matmul(ps[:, 0, tb * E:(tb + 1) * E], h[:, tb * 128:(tb + 1) * 128], weight,
                                      start=True, stop=True)
            mm.then_inc(done, 1)

        def invert_act(act, l):
            for c in range(NC + 1):
                if c < NC:
                    w = sums_chunk(c, 1)
                    act.wait_ge(ld_y[l][c // 2], 32)
                    nc.scalar.activation(w, w, ACT.Ln).then_inc(s_log_sum, 1)
                if c >= 1:
                    w = sums_chunk(c - 1, 1)
                    act.wait_ge(s_log_sum, l * NC + c)
                    nc.scalar.activation(w, w, ACT.Exp, scale=-1.0).then_inc(s_inv_sum, 1)

        w1s = [spare[:, k * HID0:(k + 1) * HID0] for k in range(2)]
        w2s = [spare[:, N // 2 + k * 512:N // 2 + (k + 1) * 512] for k in range(2)]
        b1x = [small[:, 736 + 4 * k:740 + 4 * k] for k in range(2)]
        b2x = [small[:, 744 + k:745 + k] for k in range(2)]
        h_rd, w_rd, w_rs = (sem(n) for n in ("h_round", "w_round", "w_rest"))

        def weights_round(act, k):
            nc.scalar.copy(w_parts[:, k, 0, :], w1s[k]).then_inc(w_rd, 1)
            nc.scalar.copy(w_parts[:, k, 2, :], w2s[k]).then_inc(w_rd, 1)

        def weights_rest(pool, k, before):
            for j, src in enumerate((w1s[k], w2s[k])):
                pool.wait_ge(w_rd, before + (j + 1))
                nc.gpsimd.tensor_tensor(w_parts[:, k, 2 * j + 1, :], src, w_parts[:, k, 2 * j, :], ALU.subtract)\
                    .then_inc(w_rs, 1)
        x_ld = [sem("x_ld0"), sem("x_ld1")]
        XLD = 4 * 16

        def load_weights(sp, e, k):
            for dst, src in ((w1s[k], t["w1"][bass.ds(e, 1)].rearrange("o p n -> (o p) n")),
                             (w2s[k], t["w2"][bass.ds(e, 1)].rearrange("o p k n -> (o p) (k n)")),
                             (b1x[k], t["b1"][bass.ds(e, 1)].rearrange("o p k -> (o p) k")),
                             (b2x[k], t["b2"][bass.ds(e, 1)].rearrange("o p k -> (o p) k"))):
                sp.dma_start(dst, src).then_inc(x_ld[k], 16)

        n3 = Norm(2, lambda c: fa[3][:, c_of(c)], lambda c: fa[1][:, c_of(c)], lambda c: fa[2][:, c_of(c)],
                  lambda c: h[:, c_of(c)], meanM, 0, gain=col("ln2g"), bias=col("ln2b"), scaled=1)
        s_log_sum, s_inv_sum, yn3, wp3, xa3, lg3, ch3, gap3, ex3, w3r, w3t, w3c, w3s = (
            sem(f"s3_{n}") for n in ("log_sum", "inverse_sum", "y", "wp", "xa", "logits", "chain", "gap", "exp",
                                     "weights", "turned", "copied", "stored"))

        with nc.Block() as block:
            @block.sync
            def _(sp):
                load_sums(sp, 0, 1)
                load_weights(sp, 0, 0)
                load_weights(sp, 1, 1)
                sp.wait_ge(w3c, 1)
                sp.dma_start(wd[0].rearrange("e (t n) -> (e t) n", n=128), rt(11)).then_inc(w3s, 16)
                sp.wait_ge(w3s, 16)

            @block.gpsimd
            def _(pool):
                weights_rest(pool, 0, 0)
                for c in range(NC):
                    pool.wait_ge(h_rd, c + 1)
                    nc.gpsimd.tensor_tensor(h_rest[:, c_of(c)], h[:, c_of(c)], h_round[:, c_of(c)], ALU.subtract)

            @block.vector
            def _(dve):
                for c in range(NC):
                    dve.wait_ge(ld_y[0][c // 2], 32)
                    dve.wait_ge(s_inv_sum, c + 1)
                    nc.vector.tensor_tensor(sums_chunk(c, 0), sums_chunk(c, 0), sums_chunk(c, 1), ALU.mult)\
                        .then_inc(yn3, 1)
                for c in range(NC):
                    dve.wait_ge(wp3, c + 1)
                    nc.vector.scalar_tensor_tensor(fa[3][:, c_of(c)], ps[:, 4 + c, :], col("bp"), xn_chunk(c),
                                                   ALU.add, ALU.add).then_inc(xa3, 1)
                    dve.wait_ge(xa3, c + 1)
                    nc.vector.tensor_tensor(acc[:, c_of(c)], xT[:, c_of(c)], fa[3][:, c_of(c)], ALU.add)
                norm_dve(dve, n3)
                steps = [0]

                def step(ins):
                    steps[0] += 1
                    ins.then_inc(ch3, 1)
                    dve.wait_ge(ch3, steps[0])

                dve.wait_ge(lg3, 1)
                logit, one1, one2, eq, sc = rt(0), rt(1), rt(2), rt(3), rt(4)
                m1, m2, cm, ew, w1, w2 = (rs(k) for k in range(6))
                step(nc.vector.tensor_tensor(v3(logit), v3(ps[:, 0, 0:128]),
                                             gbb.unsqueeze(1).to_broadcast([128, TB, E]), ALU.add))
                top_one(step, logit, one1, m1, eq, sc, cm)
                step(nc.vector.scalar_tensor_tensor(logit, one1, -3e38, logit, ALU.mult, ALU.add))
                top_one(step, logit, one2, m2, eq, sc, cm)
                nc.vector.tensor_tensor(m2, m2, m1, ALU.subtract).then_inc(gap3, 1)
                dve.wait_ge(ex3, 1)
                step(nc.vector.tensor_scalar(w1, ew, 1.0, None, ALU.add))
                step(nc.vector.reciprocal(w1, w1))
                step(nc.vector.tensor_tensor(w2, ew, w1, ALU.mult))
                step(nc.vector.tensor_tensor(v3(one1), v3(one1), wide(w1), ALU.mult))
                step(nc.vector.tensor_tensor(v3(one2), v3(one2), wide(w2), ALU.mult))
                nc.vector.tensor_tensor(rt(10).rearrange("p (e t) -> p t e", t=TB), v3(one1), v3(one2), ALU.add)\
                    .then_inc(w3r, 1)
                dve.wait_ge(w3t, 1)
                nc.vector.tensor_copy(rt(11), ps[:, 1, 0:128]).then_inc(w3c, 1)

            @block.scalar
            def _(act):
                invert_act(act, 0)
                norm_act(act, n3)
                act.wait_ge(x_ld[0], XLD)
                weights_round(act, 0)
                for c in range(NC):
                    act.wait_ge(s_normed, n3.base + c + 1)
                    nc.scalar.copy(h_round[:, c_of(c)], h[:, c_of(c)]).then_inc(h_rd, 1)
                act.wait_ge(gap3, 1)
                nc.scalar.activation(rs(3), rs(1), ACT.Exp).then_inc(ex3, 1)

            @block.tensor
            def _(pe):
                for c in range(NC):
                    pe.wait_ge(yn3, c + 1)
                    nc.tensor.matmul(ps[:, 4 + c, :], wf[:, 3, :], sums_chunk(c, 0), start=True, stop=True)\
                        .then_inc(wp3, 1)
                norm_pe(pe, n3, ready=xa3)
                pe.wait_ge(s_normed, n3.base + NC)
                route_pe(pe, wl1[:, 840:848], lg3)
                pe.wait_ge(w3r, 1)
                nc.tensor.transpose(ps[:, 1, 0:128], rt(10), ident).then_inc(w3t, 1)

        mid = pool_a[:, 0:4 * CH].rearrange("p (k n) -> p k n", k=4)
        tmp = h
        A0 = NC
        x_mr, x_ms, x_ms0 = (sem(f"x_{n}") for n in ("mid_round", "mid_rest", "mid_rest0"))
        x_row, x_h, x_gelu, x_y, x_t, x_acc = ([sem("x_row0"), sem("x_row1")], sem("x_h"), sem("x_gelu"),
                                              sem("x_y"), sem("x_tmp"), sem("x_acc"))
        EB = E // NB
        STEPS = EB * NC
        T0 = 2
        rb = [pool_a[:, N + CH * k:N + CH * (k + 1)] for k in range(12)]
        dlt_, mix_, v_, kv_, rw_, gate_, cen_, sq_ = rb[0], rb[1:5], rb[5], rb[6], rb[8], rb[9], rb[10], rb[11]
        scan_ = [rb[7], osb[:, 0, CH:2 * CH]]
        decb = osb[:, 0, 0:CH]
        dcy, dcyb, dlt, mixed, kv_mm, vsb, kvd, scd, t2d, rg_mm, sgd, rwd = (
            sem(n) for n in ("decay", "decay_wide", "difference", "mixed", "kv_mm", "v_there", "kv_done",
                             "scan_done", "bonus_done", "rg_mm", "gate_done", "rw_done"))
        rmean, rcen, rsq, rvar, rlog, rinv, rgated, rnorm, wo_mm, wo_ev = (
            sem(f"branch_{n}") for n in ("mean", "centred", "squared", "variance", "log_variance", "inverse",
                                         "gated", "normed", "wo_mm", "added"))

        def branch_tokens(r, q):
            return bass.ds(r * T + q * CH, CH)

        def branch_dve(dve, r, q, t, n):
            m = r * 2 + q
            tok = branch_tokens(r, q)
            if t == 0:
                nc.vector.tensor_tensor(dlt_, xn[:, tok], xs[:, tok], ALU.subtract).then_inc(dlt, 1)
                dve.wait_ge(dlt, m + 1)
                for j, name in enumerate(("mk", "mv", "mr", "mg")):
                    nc.vector.scalar_tensor_tensor(mix_[j], dlt_, col(name), xs[:, tok], ALU.mult, ALU.add)\
                        .then_inc(mixed, 1)
            if t == 1:
                dve.wait_ge(vsb, m + 1)
                nc.vector.scalar_tensor_tensor(kv_, ps[:, 6, :], col("bk"), v_, ALU.add, ALU.mult)\
                    .then_inc(kvd, 1)
                dve.wait_ge(kvd, m + 1)
                init = scan_[0][:, CH - 1:CH] if q else 0.0
                nc.vector.tensor_tensor_scan(scan_[q], decb, kv_, init, ALU.mult, ALU.add).then_inc(scd, 1)
                dve.wait_ge(scd, m + 1)
                nc.vector.scalar_tensor_tensor(kv_, kv_, col("u"), scan_[q], ALU.mult, ALU.add)\
                    .then_inc(t2d, 1)
            if t == 2:
                dve.wait_ge(rg_mm, m + 1)
                dve.wait_ge(t2d, m + 1)
                nc.vector.scalar_tensor_tensor(rw_, ps[:, 6, :], col("br"), kv_, ALU.add, ALU.mult)\
                    .then_inc(rwd, 1)
            if t == 3:
                dve.wait_ge(rmean, m + 1)
                nc.vector.tensor_tensor(cen_, rw_, ps[:, 6, :], ALU.subtract).then_inc(rcen, 1)
            if t == 5:
                dve.wait_ge(rinv, m + 1)
                nc.vector.scalar_tensor_tensor(sq_, gate_, 1.0, sq_, ALU.add, ALU.mult).then_inc(rgated, 1)
                dve.wait_ge(rgated, m + 1)
                nc.vector.tensor_tensor(rw_, cen_, sq_, ALU.mult).then_inc(rnorm, 1)
            if t == 6:
                dve.wait_ge(wo_mm, m + 1)
                dve.wait_ge(x_acc, n + A0)
                nc.vector.scalar_tensor_tensor(acc[:, tok], ps[:, 6, :], col("bo"), acc[:, tok], ALU.add, ALU.add)\
                    .then_inc(wo_ev, 1)
                dve.wait_ge(wo_ev, m + 1)

        def branch_act(act, r, q, t):
            m = r * 2 + q
            if t == 1:
                act.wait_ge(kv_mm, m + 1)
                nc.scalar.activation(v_, ps[:, 7, :], ACT.Identity, bias=col("bv")).then_inc(vsb, 1)
            if t == 2:
                act.wait_ge(dcyb, 3)
                act.wait_ge(rg_mm, m + 1)
                nc.scalar.activation(gate_, ps[:, 7, :], ACT.Tanh, bias=hbg, scale=0.5).then_inc(sgd, 1)
            if t == 3:
                act.wait_ge(rcen, m + 1)
                nc.scalar.activation(sq_, cen_, ACT.Square).then_inc(rsq, 1)
            if t == 4:
                nc.scalar.preload_act_table_set(LOG_EXP)
                act.wait_ge(rvar, m + 1)
                nc.scalar.activation(sq_, ps[:, 7, :], ACT.Ln, bias=eps[:, 0:1]).then_inc(rlog, 1)
                act.wait_ge(rlog, m + 1)
                nc.scalar.activation(sq_, sq_, ACT.Exp, scale=-0.5).then_inc(rinv, 1)

        def branch_pe(pe, r, q, t):
            m = r * 2 + q

            def product(bank, weight, operand, done):
                mm = nc.tensor.matmul(ps[:, bank, :], weight, operand, start=True, stop=True)
                if done is not None:
                    mm.then_inc(done, 1)
            if t == 1:
                pe.wait_ge(mixed, m * 4 + 4)
                product(6, wl0[:, 2, :], mix_[0], None)
                product(7, wl0[:, 3, :], mix_[1], kv_mm)
            if t == 2:
                pe.wait_ge(kvd, m + 1)
                product(6, wl0[:, 1, :], mix_[2], None)
                product(7, wl0[:, 0, :], mix_[3], rg_mm)
            if t == 3:
                pe.wait_ge(rwd, m + 1)
                product(6, headM, rw_, rmean)
            if t == 4:
                pe.wait_ge(rsq, m + 1)
                pe.wait_ge(sgd, m + 1)
                product(7, headM, sq_, rvar)
            if t == 6:
                pe.wait_ge(dcyb, 3)
                pe.wait_ge(rnorm, m + 1)
                product(6, wl0[:, 4, :], rw_, wo_mm)

        with nc.Block() as block:
            @block.sync
            def _(sp):
                def load_row(e, k):
                    sp.dma_start(wbc[k][:, :], wd[0][bass.ds(e, 1)].rearrange("o n -> (o n)").partition_broadcast(128))\
                        .then_inc(x_row[k], 16)
                load_row(0, 0)
                load_row(1, 1)
                with sp.Fori(1, E // 2) as r:
                    for k in range(2):
                        sp.wait_ge(x_acc, r * (2 * NC) + ((k - 1) * NC + A0))
                        load_weights(sp, r * 2 + k, k)
                        load_row(r * 2 + k, k)
                sp.wait_ge(x_ld[0], XLD * E // 2)
                sp.sem_inc(x_ld[0], XLD)

            @block.tensor
            def _(pe):
                def expert_products(out, parts, b, round_, rest, which, first, last):
                    for j in which:
                        left = parts[1 if j == 1 else 0][:, b * 128:(b + 1) * 128]
                        mm = nc.tensor.matmul(out, left, rest if j == 2 else round_,
                                              start=first and j == which[0], stop=last and j == which[-1])
                    return mm

                with pe.Fori(0, NB) as r:
                    for k in range(EB):
                        w = w_parts[:, k % 2]
                        w1, w2 = (w[:, 0], w[:, 1]), (w[:, 2], w[:, 3])
                        pe.wait_ge(w_rs, r * (2 * EB) + 2 * (k + 1))
                        for c in range(NC):
                            n = r * STEPS + (k * NC + c)
                            hr, hs = h_round[:, c_of(c)], h_rest[:, c_of(c)]
                            pe.wait_ge(x_gelu, n * 4 + 1)
                            for b in range(4):
                                expert_products(ps[:, b, :], w1, b, hr, hs, (0, 1, 2), True, True).then_inc(x_h, 1)
                            branch_pe(pe, r, (k * NC + c) // 8, (k * NC + c) % 8)
                            pe.wait_ge(x_t, n + (T0 - 1))
                            y = ps[:, 4 + c % 2, :]
                            for b in range(4):
                                pe.wait_ge(x_mr, n * 4 + (b + 1))
                                expert_products(y, w2, b, mid_round[:, b, :], None, (0, 1), b == 0, False)
                            for b in range(4):
                                if b == 0:
                                    pe.wait_ge(x_ms0, n + 1)
                                else:
                                    pe.wait_ge(x_ms, n * 3 + b)
                                mm = expert_products(y, w2, b, None, mid_rest[:, b, :], (2,), False, b == 3)
                            mm.then_inc(x_y, 1)

            @block.scalar
            def _(act):
                act.sem_inc(x_gelu, 1)
                nc.scalar.activation(dec[:, 0:1], col("w"), ACT.Exp).then_inc(dcy, 1)
                act.wait_ge(dcy, 1)
                nc.scalar.activation(dec[:, 1:2], dec[:, 0:1], ACT.Exp, scale=-1.0).then_inc(dcy, 1)
                with act.Fori(0, NB) as r:
                    for k in range(EB):
                        for c in range(NC):
                            n = r * STEPS + (k * NC + c)
                            for b in range(4):
                                act.wait_ge(x_h, n * 4 + (b + 1))
                                nc.scalar.activation(mid[:, b, :], ps[:, b, :], ACT.Gelu,
                                                     bias=b1x[k % 2][:, b:b + 1]).then_inc(x_gelu, 1)
                            if c == 1:
                                nxt = (k + 1) % 2
                                act.wait_ge(x_ld[nxt], r * (XLD * EB // 2) + XLD * ((k + 1) // 2 + 1))
                                weights_round(act, nxt)
                            branch_act(act, r, (k * NC + c) // 8, (k * NC + c) % 8)

            @block.gpsimd
            def _(pool):
                pool.sem_inc(x_acc, A0)
                with pool.Fori(0, NB) as r:
                    for k in range(EB):
                        for c in range(NC):
                            n = r * STEPS + (k * NC + c)
                            pool.wait_ge(x_mr, n * 4 + 1)
                            nc.gpsimd.tensor_tensor(mid_rest[:, 0, :], mid[:, 0, :], mid_round[:, 0, :], ALU.subtract)\
                                .then_inc(x_ms0, 1)
                            if c == 1:
                                weights_rest(pool, (k + 1) % 2, r * (2 * EB) + 2 * (k + 1))
                            pool.wait_ge(x_t, n + (T0 + 1))
                            nc.gpsimd.tensor_tensor(acc[:, c_of(c)], acc[:, c_of(c)], tmp[:, c_of(c)], ALU.add)\
                                .then_inc(x_acc, 1)

            @block.vector
            def _(dve):
                dve.sem_inc(x_t, T0)
                nc.vector.memset(decb, 0.0).then_inc(dcyb, 1)
                nc.vector.tensor_scalar(hbg, col("bg"), 0.5, None, ALU.mult).then_inc(dcyb, 1)
                nc.vector.tensor_scalar(wl0[:, 4, :], wl0[:, 4, :], 0.5, None, ALU.mult).then_inc(dcyb, 1)
                dve.wait_ge(dcy, 2)
                dve.wait_ge(dcyb, 3)
                nc.vector.tensor_scalar(decb, decb, dec[:, 1:2], None, ALU.add).then_inc(dcyb, 1)
                dve.wait_ge(dcyb, 4)
                with dve.Fori(0, NB) as r:
                    for k in range(EB):
                        for c in range(NC):
                            n = r * STEPS + (k * NC + c)
                            for b in range(4):
                                dve.wait_ge(x_gelu, n * 4 + (b + 2))
                                nc.vector.tensor_copy(mid_round[:, b, :], mid[:, b, :]).then_inc(x_mr, 1)
                                if b >= 1:
                                    dve.wait_ge(x_mr, n * 4 + (b + 1))
                                    nc.vector.tensor_tensor(mid_rest[:, b, :], mid[:, b, :], mid_round[:, b, :],
                                                            ALU.subtract).then_inc(x_ms, 1)
                            branch_dve(dve, r, (k * NC + c) // 8, (k * NC + c) % 8, n)
                            if c == 0:
                                dve.wait_ge(x_row[k % 2], r * (16 * EB // 2) + 16 * (k // 2 + 1))
                            dve.wait_ge(x_acc, n + 1)
                            dve.wait_ge(x_y, n + 1)
                            nc.vector.scalar_tensor_tensor(tmp[:, c_of(c)], ps[:, 4 + c % 2, :], b2x[k % 2],
                                                           wbc[k % 2][:, c_of(c)], ALU.add, ALU.mult)\
                                .then_inc(x_t, 1)

        region.close()
        region = ctx.enter_context(ExitStack())
        shortp, pool_b = attention_scratch(region, 1)
        f = [full(pool_b, k) for k in range(6)]

        sems1 = attention_semaphores(1)

        n5 = Norm(3, lambda c: acc[:, c_of(c)], lambda c: f[0][:, c_of(c)], lambda c: f[1][:, c_of(c)],
                  lambda c: h[:, c_of(c)], meanM, 0)
        low = f[4]
        lowk = f[5]
        cosq, sinq = xT[:, 0:T], xT[:, T:2 * T]
        cosk, sink = shortp[:, 0:CH], shortp[:, CH:2 * CH]
        qs5 = Split("tq", lambda c: f[2][:, c_of(c)], lambda p, c: partb[:, 0, p, c_of(c)], qd[1], after=qs_)
        ks5 = Split("tk", lambda c: f[3][:, c_of(c)], lambda p, c: partb[:, 1, p, c_of(c)], kd[1], after=ks_)
        hidden = [xn, spare]
        z_ld, z_h, z_silu = [sem("z_ld0"), sem("z_ld1")], sem("z_h"), sem("z_silu")
        wds = [vst[:, k, 512:768].rearrange("p (k n) -> p k n", k=2) for k in range(2)]

        def load_down(sp, e, k):
            sp.dma_start(wds[k], t["wdn"][bass.ds(e, 1)].rearrange("o p k n -> (o p) k n")).then_inc(z_ld[k], 16)

        home1 = vst[:, 2, CH:2 * CH]
        tw = shortp[:, 2048:2048 + CH], shortp[:, 2048 + CH:2048 + 2 * CH]
        ld5, lo5, lc5, hi5, hk5, ra5, rk5, v5 = (
            sem(f"s5_{n}") for n in ("ld", "low", "low_copied", "high", "keys", "q_turned", "k_turned", "v"))
        lg5, ch5, mx5, ex5, pf5, tot5, w5r, w5t, w5c, w5s = (
            sem(f"r5_{n}") for n in ("logits", "chain", "less_max", "exp", "counts", "prefix", "weights",
                                     "turned", "copied", "stored"))

        with nc.Block() as block:
            @block.sync
            def _(sp):
                sp.dma_start(cosq, t["rope"][:, 0, :]).then_inc(ld5, 16)
                sp.dma_start(sinq, t["rope"][:, 1, :]).then_inc(ld5, 16)
                sp.dma_start(cosk, t["ropek"][:, 0, :]).then_inc(ld5, 16)
                sp.dma_start(sink, t["ropek"][:, 1, :]).then_inc(ld5, 16)
                for c in range(NC):
                    split_store(sp, qs5, c)
                for k in range(2):
                    load_down(sp, k, k)
                for p, there in enumerate((ks5.hi, ks5.mid, ks5.lo)):
                    sp.wait_ge(there, ks5.base + 1)
                    for c in range(NC):
                        sp.dma_start(kd[1][c // 2, :, p, :, (c % 2) * CH:(c % 2 + 1) * CH],
                                     ks5.parts(p, 0)[32 * c:32 * c + 32]).then_inc(ks5.stored, 16)
                sp.wait_ge(qs5.stored, qs5.base_stored + 16 * PARTS * NC)
                sp.wait_ge(ks5.stored, ks5.base_stored + 16 * PARTS * NC)
                sp.wait_ge(k_ones, 1)
                load_stacks(sp, 1, 1, sems1, 0, 0)
                sp.wait_ge(w5c, 1)
                sp.dma_start(wd[1].rearrange("e (t n) -> (e t) n", n=128), rt(11)).then_inc(w5s, 16)
                sp.wait_ge(w5s, 16)

            @block.gpsimd
            def _(pool):
                pool.wait_ge(ks5.lo, ks5.base + 1)
                nc.gpsimd.memset(stacks()[1][64:MROWS, :, 0:1], 1.0).then_inc(k_ones, 1)

            @block.scalar
            def _(act):
                nc.scalar.preload_act_table_set(LOG_EXP)
                norm_act(act, n5)
                for c in range(NC + 1):
                    if c < NC:
                        b = 4 * (c % 2)
                        act.wait_ge(lo5, c + 1)
                        nc.scalar.copy(low[0:QL, c_of(c)], ps[0:QL, b, :]).then_inc(lc5, 1)
                        nc.scalar.copy(lowk[0:KVL, c_of(c)], ps[0:KVL, b + 1, :]).then_inc(lc5, 1)
                    if c >= 1:
                        first_part(act, qs5, c - 1)
                        second_part(act, qs5, c - 1)
                first_part(act, ks5, 0)
                second_part(act, ks5, 0)
                act.wait_ge(mx5, 1)
                nc.scalar.activation(rt(5), rt(5), ACT.Exp).then_inc(ex5, 1)
                for c in range(NC):
                    for b in range(2):
                        act.wait_ge(z_h, 2 * c + b + 1)
                        nc.scalar.activation(hidden[b][:, c_of(c)], ps[:, 4 * (c % 2) + b, :], ACT.Silu)\
                            .then_inc(z_silu, 1)

            @block.vector
            def _(dve):
                norm_dve(dve, n5)
                dve.wait_ge(ld5, 64)
                for c in range(NC):
                    b = 4 * (c % 2)
                    half = slice((c % 2) * CH, (c % 2 + 1) * CH)
                    dve.wait_ge(hi5, c + 1)
                    nc.vector.tensor_tensor(qs5.f(c), ps[:, b, :], cosq[:, half], ALU.mult).then_inc(ra5, 1)
                    nc.vector.tensor_tensor(tw[0], ps[:, b + 1, :], sinq[:, half], ALU.mult).then_inc(ra5, 1)
                    dve.wait_ge(ra5, 2 * (c + 1))
                    nc.vector.tensor_tensor(qs5.f(c), qs5.f(c), tw[0], ALU.add).then_inc(qs5.full, 1)
                    remainder(dve, qs5, c)
                    if c == NC - 1:
                        dve.wait_ge(hk5, 1)
                        nc.vector.tensor_tensor(ks5.f(0), ps[:, 2, :], cosk, ALU.mult).then_inc(rk5, 1)
                        nc.vector.tensor_tensor(tw[1], ps[:, 3, :], sink, ALU.mult).then_inc(rk5, 1)
                        dve.wait_ge(rk5, 2)
                        nc.vector.tensor_tensor(ks5.f(0), ks5.f(0), tw[1], ALU.add).then_inc(ks5.full, 1)
                    last_part(dve, qs5, c)
                remainder(dve, ks5, 0)
                dve.wait_ge(v5, 1)
                nc.vector.tensor_copy(home1.rearrange("p (b g k d) -> p b g k d", b=NB, g=KVH, k=KB)[:, 0],
                                      ps[:, 6, 0:256].rearrange("p (k g d) -> p g k d", k=KB, g=KVH))
                nc.vector.tensor_copy(home1.rearrange("p (b g k d) -> p b g k d", b=NB, g=KVH, k=KB)[:, 1],
                                      ps[:, 6, 256:512].rearrange("p (k g d) -> p g k d", k=KB, g=KVH))
                last_part(dve, ks5, 0)
                steps = [0]

                def step(ins):
                    steps[0] += 1
                    ins.then_inc(ch5, 1)
                    dve.wait_ge(ch5, steps[0])

                dve.wait_ge(lg5, 1)
                gate, one1, one2, eq, sc, ex = rt(0), rt(1), rt(2), rt(3), rt(4), rt(5)
                m1, m2, cm, sm = (rs(k) for k in range(4))
                step(nc.vector.memset(rt(8), 1.0))
                step(nc.vector.memset(rt(8).rearrange("p (e t) -> p e t", e=E)[:, :, 0:1], 0.0))
                step(nc.vector.tensor_copy(gate, ps[:, 7, 0:128]))
                step(nc.vector.tensor_reduce(m1, v3(gate), AX.X, ALU.max))
                nc.vector.tensor_tensor(v3(ex), v3(gate), wide(m1), ALU.subtract).then_inc(mx5, 1)
                dve.wait_ge(ex5, 1)
                step(nc.vector.tensor_reduce(sm, v3(ex), AX.X, ALU.add))
                step(nc.vector.reciprocal(sm, sm))
                step(nc.vector.tensor_tensor(v3(gate), v3(ex), wide(sm), ALU.mult))
                top_one(step, gate, one1, m1, eq, sc, cm)
                step(nc.vector.scalar_tensor_tensor(ex, one1, -2.0, gate, ALU.mult, ALU.add))
                top_one(step, ex, one2, m2, eq, sc, cm)
                picked, run, same = rt(6), rt(7), rt(8)
                by_block = lambda ap: ap.rearrange("p (e t) -> p t e", e=E)
                step(nc.vector.tensor_tensor(by_block(picked), v3(one1), v3(one2), ALU.add))
                nc.vector.tensor_tensor_scan(run, same, picked, 0.0, ALU.mult, ALU.add).then_inc(pf5, 1)
                dve.wait_ge(tot5, 1)
                step(nc.vector.tensor_scalar(eq, ps[:, 7, 128:256], CAP, None, ALU.is_le))
                step(nc.vector.tensor_tensor(v3(eq), v3(eq), by_block(picked), ALU.mult))
                step(nc.vector.tensor_tensor(gate, gate, eq, ALU.mult))
                step(nc.vector.tensor_reduce(sm, v3(gate), AX.X, ALU.add))
                step(nc.vector.tensor_scalar(sm, sm, 1e-6, None, ALU.add))
                step(nc.vector.reciprocal(sm, sm))
                nc.vector.tensor_tensor(rt(10).rearrange("p (e t) -> p t e", t=TB), v3(gate), wide(sm), ALU.mult)\
                    .then_inc(w5r, 1)
                dve.wait_ge(w5t, 1)
                nc.vector.tensor_copy(rt(11), ps[:, 7, 256:384]).then_inc(w5c, 1)

            @block.tensor
            def _(pe):
                norm_pe(pe, n5)
                pe.wait_ge(s_log, n5.base + NC)
                for c in range(NC):
                    b = 4 * (c % 2)
                    pe.wait_ge(s_normed, n5.base + c + 1)
                    if c >= 2:
                        pe.wait_ge(ra5, 2 * (c - 1))
                    nc.tensor.matmul(ps[0:QL, b, :], wl1[:, 0:64], h[:, c_of(c)], start=True, stop=True)
                    nc.tensor.matmul(ps[0:KVL, b + 1, :], wl1[:, 320:352], h[:, c_of(c)], start=True, stop=True)\
                        .then_inc(lo5, 1)
                    pe.wait_ge(lc5, 2 * (c + 1))
                    ql, kl = low[0:QL, c_of(c)], lowk[0:KVL, c_of(c)]
                    nc.tensor.matmul(ps[:, b, :], wl1[0:QL, 64:192], ql, start=True, stop=True)
                    nc.tensor.matmul(ps[:, b + 1, :], wl1[0:QL, 192:320], ql, start=True, stop=True).then_inc(hi5, 1)
                    for k in range(2):
                        mm = nc.tensor.matmul(ps[32 * c:32 * c + 32, 2 + k, :], wl1[0:KVL, 352 + 32 * k:384 + 32 * k],
                                              kl, start=True, stop=True, tile_position=(0, 32 * c),
                                              skip_group_check=True)
                mm.then_inc(hk5, 1)
                for tb in range(TB):
                    mm = nc.tensor.matmul(ps[:, 6, tb * 32:(tb + 1) * 32], lowk[0:KVL, tb * 128:(tb + 1) * 128],
                                          wl1[0:KVL, 416:448], start=True, stop=True)
                mm.then_inc(v5, 1)
                for tb in range(TB):
                    mm = nc.tensor.matmul(ps[:, 7, tb * E:(tb + 1) * E], h[:, tb * 128:(tb + 1) * 128],
                                          wl1[:, 576:584], start=True, stop=True)
                mm.then_inc(lg5, 1)
                pe.wait_ge(ra5, 2 * NC)
                for c in range(NC):
                    if c == 3:
                        pe.wait_ge(pf5, 1)
                        by_block = lambda ap: ap.rearrange("p (e t) -> p t e", e=E)
                        nc.tensor.matmul(ps[:, 7, 128:256], later, by_block(rt(6)), start=True, stop=False,
                                         skip_group_check=True)
                        nc.tensor.matmul(ps[:, 7, 128:256], ones, by_block(rt(7)), start=False, stop=True,
                                         skip_group_check=True).then_inc(tot5, 1)
                    if c >= 2:
                        pe.wait_ge(z_silu, 2 * (c - 1))
                    for b in range(2):
                        nc.tensor.matmul(ps[:, 4 * (c % 2) + b, :], wl1[:, 584 + b * 128:584 + (b + 1) * 128],
                                         h[:, c_of(c)], start=True, stop=True).then_inc(z_h, 1)
                pe.wait_ge(w5r, 1)
                nc.tensor.transpose(ps[:, 7, 256:384], rt(10), ident).then_inc(w5t, 1)

        wrow = [xT, xs]
        ztmp = osb[:, 0:2, :].rearrange("p s n -> p (s n)")
        Y_BANKS = (0, 1, 2, 4)
        Z0 = 4
        z_y, z_t, z_acc = sem("z_y"), sem("z_tmp"), sem("z_acc")

        class Experts1:
            AT = {2: 0, 3: 1, 5: 2, 6: 3, 7: 4, 9: 5, 10: 6, 11: 7}

            def sync(self, sp):
                def load_row(e, k):
                    sp.dma_start(wrow[k][:, :], wd[1][bass.ds(e, 1)].rearrange("o n -> (o n)")
                                 .partition_broadcast(128)).then_inc(z_ld[k], 16)
                load_row(0, 0)
                load_row(1, 1)
                with sp.Fori(1, E // 2) as r:
                    for k in range(2):
                        sp.wait_ge(z_t, r * (2 * NC) + ((k - 1) * NC + Z0))
                        load_down(sp, r * 2 + k, k)
                        load_row(r * 2 + k, k)

            def pe(self, pe, r, tile):
                if tile not in self.AT:
                    return
                k, c = divmod(self.AT[tile], NC)
                n = r * (2 * NC) + (k * NC + c)
                if c == 0:
                    pe.wait_ge(z_ld[k], r * 32 + 32)
                pe.wait_ge(z_t, n + (Z0 - 3))
                for b in range(2):
                    mm = nc.tensor.matmul(ps[:, Y_BANKS[c], :], wds[k][:, b, :], hidden[b][:, c_of(c)],
                                          start=(b == 0), stop=(b == 1))
                mm.then_inc(z_y, 1)

            def end_pe(self, pe):
                pe.wait_ge(z_t, E * NC + Z0)

            def begin_dve(self, dve):
                dve.sem_inc(z_t, Z0)

            def end_dve(self, dve):
                dve.wait_ge(z_acc, E * NC + Z0)

            def dve(self, dve, r, tile):
                if tile not in self.AT:
                    return
                k, c = divmod(self.AT[tile], NC)
                n = r * (2 * NC) + (k * NC + c)
                if c == 0:
                    dve.wait_ge(z_ld[k], r * 32 + 32)
                dve.wait_ge(z_acc, n + (Z0 - 3))
                dve.wait_ge(z_y, n + 1)
                nc.vector.tensor_tensor(ztmp[:, c_of(c)], ps[:, Y_BANKS[c], :], wrow[k][:, c_of(c)], ALU.mult)\
                    .then_inc(z_t, 1)

            def pool(self, pool):
                pool.sem_inc(z_acc, Z0)
                with pool.Fori(0, E) as e:
                    for c in range(NC):
                        pool.wait_ge(z_t, e * NC + (c + 1 + Z0))
                        nc.gpsimd.tensor_tensor(acc[:, c_of(c)], acc[:, c_of(c)], ztmp[:, c_of(c)], ALU.add)\
                            .then_inc(z_acc, 1)

        attention(1, 1, 1, home1, sems1, Experts1())
        z_yn, z_wo, z_a, z_out = (sem(f"z_{n}") for n in ( "yn", "wo", "sum", "out"))

        with nc.Block() as block:
            @block.sync
            def _(sp):
                load_sums(sp, 1, 1)
                for c in range(NC):
                    sp.wait_ge(z_a, c + 1)
                    sp.dma_start(out[:, c_of(c)], acc[:, c_of(c)]).then_inc(z_out, 16)
                sp.wait_ge(z_out, 16 * NC)

            @block.scalar
            def _(act):
                invert_act(act, 1)

            @block.vector
            def _(dve):
                for c in range(NC):
                    dve.wait_ge(ld_y[1][c // 2], 32)
                    dve.wait_ge(s_inv_sum, NC + c + 1)
                    nc.vector.tensor_tensor(sums_chunk(c, 0), sums_chunk(c, 0), sums_chunk(c, 1), ALU.mult)\
                        .then_inc(z_yn, 1)
                    dve.wait_ge(z_wo, c + 1)
                    nc.vector.scalar_tensor_tensor(acc[:, c_of(c)], ps[:, 4 + c, :], col("bout"), acc[:, c_of(c)],
                                                   ALU.add, ALU.add).then_inc(z_a, 1)

            @block.tensor
            def _(pe):
                for c in range(NC):
                    pe.wait_ge(z_yn, c + 1)
                    nc.tensor.matmul(ps[:, 4 + c, :], wl1[:, 448:576], sums_chunk(c, 0), start=True, stop=True)\
                        .then_inc(z_wo, 1)


def kernel(**inputs):
    import numpy as _np
    import concourse.bacc as _bacc
    from concourse import mybir as _mybir
    from concourse.bass_utils import run_bass_kernel_spmd as _run

    a = {k: _np.asarray(v) for k, v in inputs.items()}
    f = _np.float32

    def stack(mats):
        return _np.ascontiguousarray(_np.stack(mats, axis=1))

    swap = _np.arange(128) ^ 1
    kv = a["L1_attn_Wkvb"].reshape(KVL, KVH * HD, 2)
    wl1 = _np.zeros((128, 848), f)
    wl1[:, 0:64] = a["L1_attn_Wqa"]
    wl1[0:QL, 64:192] = a["L1_attn_Wqb"]
    wl1[0:QL, 192:320] = a["L1_attn_Wqb"][:, swap]
    wl1[:, 320:352] = a["L1_attn_Wkva"]
    wl1[0:KVL, 352:384] = kv[:, :, 0]
    wl1[0:KVL, 384:416] = kv[:, swap[0:32], 0]
    wl1[0:KVL, 416:448] = kv[:, :, 1]
    wl1[:, 448:576] = a["L1_attn_Wout"]
    wl1[:, 576:584] = a["L1_ffn_w_router"].T
    wl1[:, 584:840] = a["L1_ffn_w_gate"].T
    wl1[:, 840:848] = a["L0_ffn_gate_W"]
    i = _np.arange(128)
    head = (i[:, None] // HD == i[None, :] // HD).astype(f) / f(HD)
    cst = stack([_np.full((128, 128), 1.0 / 128, f), head, _np.eye(128, dtype=f),
                 -(i[:, None] > i[None, :]).astype(f), _np.ones((128, 128), f)])
    mask = _np.where(i[None, :] > i[:, None], f(NEG), f(0.0)).astype(f)
    inv = (f(1.0) / f(10000.0) ** (_np.arange(0, HD, 2, dtype=f) / f(HD))).astype(f)
    ang = (_np.arange(T, dtype=f)[None, :] * inv[(i % HD) // 2][:, None]).astype(f).astype(_np.float64)
    cos, sin = _np.cos(ang), _np.sin(ang) * _np.where(i % 2 == 0, -1.0, 1.0)[:, None]
    rope = stack([(cos * SCALE).astype(f), (sin * SCALE).astype(f)])
    ropek = stack([_np.concatenate([tab.astype(f)[0:32, (c % 2) * CH:(c % 2 + 1) * CH] for c in range(NC)])
                   for tab in (cos, sin)])
    column = {"mg": "L0_attn_mg", "mr": "L0_attn_mr", "mk": "L0_attn_mk", "mv": "L0_attn_mv",
              "bg": "L0_attn_Wg_b", "br": "L0_attn_Wr_b", "bk": "L0_attn_Wk_b", "bv": "L0_attn_Wv_b",
              "bo": "L0_attn_Wo_b", "w": "L0_attn_w", "u": "L0_attn_u", "ln1g": "L0_ffn_ln1_g",
              "ln1b": "L0_ffn_ln1_b", "ln2g": "L0_ffn_ln2_g", "ln2b": "L0_ffn_ln2_b", "bq": "L0_ffn_bq",
              "bkf": "L0_ffn_bk", "bp": "L0_ffn_bp", "bout": "L1_attn_bout"}
    arrays = {
        "xT": _np.ascontiguousarray(a["L0_attn_x"].reshape(N, D).T),
        "cols": _np.ascontiguousarray(_np.stack([a[column[n]].reshape(128) for n in COLS], axis=1)),
        "wl0": stack([a[f"L0_attn_W{n}_w"].T for n in "grkvo"]),
        "wf": stack([a[f"L0_ffn_W{n}"] for n in "qkvp"]),
        "wl1": wl1, "cst": cst, "mask": stack([mask, mask.T]), "rope": rope, "ropek": ropek,
        "bv": a["L0_ffn_bv"], "gate_b": a["L0_ffn_gate_b"], "rev": (E - _np.arange(E)).astype(f),
        "w1": a["L0_ffn_exp_W1"],
        "w2": _np.ascontiguousarray(a["L0_ffn_exp_W2"].reshape(E, 4, 128, 128).transpose(0, 2, 1, 3)),
        "b1": _np.ascontiguousarray(a["L0_ffn_exp_b1"].reshape(E, 4, 128).transpose(0, 2, 1)),
        "b2": _np.ascontiguousarray(a["L0_ffn_exp_b2"].reshape(E, 128, 1)),
        "wdn": _np.ascontiguousarray(a["L1_ffn_w_down"].transpose(0, 2, 1).reshape(E, 2, 128, 128)
                                     .transpose(0, 2, 1, 3)),
    }
    nc = _bacc.Bacc("TRN2", target_bir_lowering=False, num_devices=1)
    t = {n: nc.dram_tensor(f"in_{n}", v.shape, _mybir.dt.from_np(v.dtype), kind="ExternalInput").ap()
         for n, v in arrays.items()}
    out = nc.dram_tensor("out_T", (128, N), F32, kind="ExternalOutput").ap()
    build_program(nc, t, out)
    r = _run(nc, [{f"in_{n}": v for n, v in arrays.items()}], core_ids=[0])
    return _np.ascontiguousarray(r.results[0]["out_T"].T).reshape(NB, T, D)
```
